# Optimizing a Trainium2 kernel written in Bass

```python
import numpy as np
import jax
import jax.numpy as jnp

def _softmax(x, axis=-1):
    return jax.nn.softmax(x, axis=axis)

def _gelu(x):
    return jax.nn.gelu(x, approximate=True)

def _silu(x):
    return jax.nn.silu(x)

def _sigmoid(x):
    return jax.nn.sigmoid(x)

def _layernorm(x, axis=-1, eps=1e-05):
    m = jnp.mean(x, axis=axis, keepdims=True)
    v = jnp.var(x, axis=axis, keepdims=True)
    return (x - m) / jnp.sqrt(v + eps)

def _scatter_add(tgt, idx, src, axis=0):
    return tgt.at[idx].add(src)

def _segment_sum(src, seg, n):
    return jax.ops.segment_sum(src, seg, n)
kernel_name = 'mk_flamingo_gated_d2_seqx_r2_67c710'

def setup_inputs(seed: int=0):
    np.random.seed(seed)
    _w = jnp.asarray

    def _rec_inputs():
        import jax
        import jax.numpy as jnp
        _rk = jax.random.key(seed)
        x = -0.0003929 + 0.9999 * jax.random.normal(jax.random.fold_in(_rk, 1), (8, 224, 512), jnp.float32)
        _lenS = 224 - jax.random.randint(jax.random.fold_in(_rk, 7), (8,), 0, max(1, 224 // 4) + 1, jnp.int32)
        _lenS2 = 750 - jax.random.randint(jax.random.fold_in(_rk, 8), (8,), 0, max(1, 750 // 4) + 1, jnp.int32)
        _ctx_2048P = jax.random.normal(jax.random.fold_in(_rk, 11), (8, 16, 1024), jnp.float32)
        _ctx_2048c = jax.random.dirichlet(jax.random.fold_in(_rk, 511), 0.3 * jnp.ones((16,), jnp.float32), (8, 750))
        _ctx_2048t = jnp.einsum('bsk,bkd->bsd', _ctx_2048c, _ctx_2048P)
        _ctx_2048t = _ctx_2048t * jax.lax.rsqrt(jnp.mean(jnp.square(_ctx_2048t)) + 1e-12) * 0.953939
        ctx_2048 = 4.13588e-05 + 0.999923 * (_ctx_2048t + 0.3 * jax.random.normal(jax.random.fold_in(_rk, 611), (8, 750, 1024), jnp.float32))
        _validS = jnp.arange(224)[None, :] < _lenS[:, None]
        _validS2 = jnp.arange(750)[None, :] < _lenS2[:, None]
        _causal = jnp.tril(jnp.ones((224, 224), dtype=bool))
        mask_BxS2_if0 = jnp.where(jnp.ones((8, 750), dtype=bool), 4, 0).astype(jnp.int32)
        _g = jax.random.normal(jax.random.fold_in(_rk, 9001), (2, 2), jnp.float32)
        _g = jnp.sign(_g) * jnp.maximum(jnp.abs(_g), 1.0) + (_g == 0) * 1.0
        g_xattn = _g[0]
        g_ffn = _g[1]
        return (x, ctx_2048, mask_BxS2_if0, g_xattn, g_ffn)
    x, ctx_2048, mask_BxS2_if0, g_xattn, g_ffn = _rec_inputs()

    def _L0_xattn_setup():
        import jax, jax.numpy as jnp
        import numpy as np
        B, L, P = (4, 2048, 512)
        D_MODEL = 512
        D_GLOBAL = 1024
        HEADDIM = 32
        EPSILON = 0.001
        RMS_EPS = 1e-05

        def rmsnorm(x, g, eps=RMS_EPS):
            var = jnp.mean(jnp.square(x), axis=-1, keepdims=True)
            return x * jax.lax.rsqrt(var + eps) * g

        def _hnet_depool(h, h_patch_full, patch_lens):
            h_patch = h_patch_full[..., :D_MODEL]
            bsz, plen = (h_patch.shape[0], h_patch.shape[1])
            seqlen = h.shape[1]
            logp = jnp.full((bsz, plen), -EPSILON, dtype=jnp.float32)
            bidx = jnp.cumsum(patch_lens, axis=1) - 1
            boundary_mask = jnp.zeros((bsz, seqlen), dtype=jnp.int32)
            boundary_mask = boundary_mask.at[jnp.arange(bsz)[:, None], bidx].set(1)
            dt = (-jnp.log(-jnp.expm1(logp))).astype(h_patch.dtype)
            x = h_patch / dt[..., None]
            n_heads = D_MODEL // HEADDIM
            A = -jnp.ones((n_heads,), dtype=jnp.float32)
            bcoef = jnp.exp(logp).astype(h_patch.dtype)
            x4 = x.reshape(bsz, plen, n_heads, HEADDIM)
            a = jnp.exp(dt[:, :, None] * A[None, None, :])
            u = (dt * bcoef)[:, :, None, None] * x4
            a_b = jnp.broadcast_to(a[..., None], u.shape)

            def comb(lft, rgt):
                aL, uL = lft
                aR, uR = rgt
                return (aL * aR, uL * aR + uR)
            _, s = jax.lax.associative_scan(comb, (a_b, u), axis=1)
            depool = s.reshape(bsz, plen, D_MODEL)
            plug = jnp.clip(jnp.cumsum(boundary_mask, axis=1) - 1, 0, plen - 1)
            depool_out = depool[jnp.arange(bsz)[:, None], plug]
            return depool_out + h
        key = jax.random.key(seed)
        k1, k2, k3, k4 = jax.random.split(key, 4)
        embeds = jax.random.normal(k1, (B, L, D_MODEL), dtype=jnp.float32)
        patch_embeds = jax.random.normal(k2, (B, P, D_GLOBAL), dtype=jnp.float32)
        patch_lens = jnp.full((B, P), L // P, dtype=jnp.int64)
        W_in = jax.random.normal(k3, (D_MODEL, D_MODEL), dtype=jnp.float32) * 0.02
        b_in = jnp.zeros((D_MODEL,), dtype=jnp.float32)
        g_res = jnp.ones((D_MODEL,), dtype=jnp.float32)
        g_init = jnp.ones((D_GLOBAL,), dtype=jnp.float32)
        return {'embeds': embeds, 'patch_embeds': patch_embeds, 'patch_lens': patch_lens, 'W_in': W_in, 'b_in': b_in, 'g_res': g_res, 'g_init': g_init}
    _L0_xattn_all = _L0_xattn_setup()
    _L0_xattn_in = {k: v for k, v in _L0_xattn_all.items() if k in ('W_in', 'b_in', 'g_res', 'g_init')}
    del _L0_xattn_all

    def _L0_ffn_setup():
        import jax, jax.numpy as jnp
        import numpy as np
        HIDDEN = 512
        INTER = 2048
        key = jax.random.key(seed)
        k1, k2, k3, k4, k5 = jax.random.split(key, 5)
        hidden_states = jax.random.normal(k1, (4, 1024, HIDDEN), dtype=jnp.float32)
        W1 = jax.random.normal(k2, (HIDDEN, INTER), dtype=jnp.float32) * (1.0 / np.sqrt(HIDDEN))
        b1 = jax.random.normal(k3, (INTER,), dtype=jnp.float32) * 0.02
        W2 = jax.random.normal(k4, (INTER, HIDDEN), dtype=jnp.float32) * (1.0 / np.sqrt(INTER))
        b2 = jax.random.normal(k5, (HIDDEN,), dtype=jnp.float32) * 0.02
        return {'hidden_states': hidden_states, 'W1': W1, 'b1': b1, 'W2': W2, 'b2': b2}
    _L0_ffn_all = _L0_ffn_setup()
    _L0_ffn_in = {k: v for k, v in _L0_ffn_all.items() if k in ('W1', 'b1', 'W2', 'b2')}
    del _L0_ffn_all

    def _L1_xattn_setup():
        import jax, jax.numpy as jnp
        import numpy as np
        B, N, DIM = (8, 2048, 512)
        M, CTX = (128, 1024)
        HEADS, DH = (16, 64)
        INNER = HEADS * DH
        EPS = 1e-06

        def _split_heads(t):
            b, n, _ = t.shape
            return t.reshape(b, n, HEADS, DH).transpose(0, 2, 1, 3)
        key = jax.random.key(seed)
        ks = jax.random.split(key, 6)
        x = jax.random.normal(ks[0], (B, N, DIM), dtype=jnp.float32)
        context = jax.random.normal(ks[1], (B, M, CTX), dtype=jnp.float32)
        Wq = jax.random.normal(ks[2], (DIM, INNER), dtype=jnp.float32) / np.sqrt(DIM)
        Wkv = jax.random.normal(ks[3], (CTX, 2 * INNER), dtype=jnp.float32) / np.sqrt(CTX)
        null_kv = jax.random.normal(ks[4], (2, DH), dtype=jnp.float32) / np.sqrt(2.0)
        Wout = jax.random.normal(ks[5], (INNER, DIM), dtype=jnp.float32) / np.sqrt(INNER)
        ln_scale = jnp.ones((DIM,), dtype=jnp.float32)
        ln_bias = jnp.zeros((DIM,), dtype=jnp.float32)
        return {'x': x, 'context': context, 'Wq': Wq, 'Wkv': Wkv, 'null_kv': null_kv, 'Wout': Wout, 'ln_scale': ln_scale, 'ln_bias': ln_bias}
    _L1_xattn_all = _L1_xattn_setup()
    _L1_xattn_in = {k: v for k, v in _L1_xattn_all.items() if k in ('Wq', 'Wkv', 'null_kv', 'Wout', 'ln_scale', 'ln_bias')}
    del _L1_xattn_all

    def _L1_ffn_setup():
        import jax, jax.numpy as jnp
        import numpy as np
        BLOCK = 32
        W_BITS = 4
        ACT_BITS = 16

        def act_qdq(x):
            qmax = 2.0 ** (ACT_BITS - 1) - 1.0
            scale = jnp.maximum(jnp.max(jnp.abs(x)) / qmax, 1e-12)
            return jnp.clip(jnp.round(x / scale), -qmax - 1.0, qmax) * scale

        def fixed_qdq_u16(x):
            scale = 1.0 / 65536.0
            return jnp.clip(jnp.round(x / scale), 0.0, 65535.0) * scale

        def lpbq_dequant(w):
            O, I = w.shape
            qmax = 2.0 ** (W_BITS - 1) - 1.0
            wb = w.reshape(O, I // BLOCK, BLOCK)
            s = jnp.maximum(jnp.max(jnp.abs(wb), axis=-1, keepdims=True) / qmax, 1e-12)
            wq = jnp.clip(jnp.round(wb / s), -qmax - 1.0, qmax) * s
            return wq.reshape(O, I)
        key = jax.random.key(seed)
        k1, k2, k3, k4 = jax.random.split(key, 4)
        B, S, H, I = (2, 2048, 512, 1536)
        x = jax.random.normal(k1, (B, S, H), jnp.float32)
        w_gate = jax.random.normal(k2, (I, H), jnp.float32) * 0.02
        w_up = jax.random.normal(k3, (I, H), jnp.float32) * 0.02
        w_down = jax.random.normal(k4, (H, I), jnp.float32) * 0.02
        return {'x': x, 'w_gate': w_gate, 'w_up': w_up, 'w_down': w_down}
    _L1_ffn_all = _L1_ffn_setup()
    _L1_ffn_in = {k: v for k, v in _L1_ffn_all.items() if k in ('w_gate', 'w_up', 'w_down')}
    del _L1_ffn_all
    return {'x': x, 'ctx_2048': ctx_2048, 'mask_BxS2_if0': mask_BxS2_if0, 'g_xattn': g_xattn, 'g_ffn': g_ffn, 'L0_xattn_W_in': _L0_xattn_in['W_in'], 'L0_xattn_b_in': _L0_xattn_in['b_in'], 'L0_xattn_g_res': _L0_xattn_in['g_res'], 'L0_xattn_g_init': _L0_xattn_in['g_init'], 'L0_ffn_W1': _L0_ffn_in['W1'], 'L0_ffn_b1': _L0_ffn_in['b1'], 'L0_ffn_W2': _L0_ffn_in['W2'], 'L0_ffn_b2': _L0_ffn_in['b2'], 'L1_xattn_Wq': _L1_xattn_in['Wq'], 'L1_xattn_Wkv': _L1_xattn_in['Wkv'], 'L1_xattn_null_kv': _L1_xattn_in['null_kv'], 'L1_xattn_Wout': _L1_xattn_in['Wout'], 'L1_xattn_ln_scale': _L1_xattn_in['ln_scale'], 'L1_xattn_ln_bias': _L1_xattn_in['ln_bias'], 'L1_ffn_w_gate': _L1_ffn_in['w_gate'], 'L1_ffn_w_up': _L1_ffn_in['w_up'], 'L1_ffn_w_down': _L1_ffn_in['w_down']}

def reference(x, ctx_2048, mask_BxS2_if0, g_xattn, g_ffn, L0_xattn_W_in, L0_xattn_b_in, L0_xattn_g_res, L0_xattn_g_init, L0_ffn_W1, L0_ffn_b1, L0_ffn_W2, L0_ffn_b2, L1_xattn_Wq, L1_xattn_Wkv, L1_xattn_null_kv, L1_xattn_Wout, L1_xattn_ln_scale, L1_xattn_ln_bias, L1_ffn_w_gate, L1_ffn_w_up, L1_ffn_w_down):
    import jax
    import jax.numpy as jnp

    def _L0_xattn_ref(embeds, patch_embeds, patch_lens, W_in, b_in, g_res, g_init):
        import jax, jax.numpy as jnp
        import numpy as np
        B, L, P = (4, 2048, 512)
        D_MODEL = 512
        D_GLOBAL = 1024
        HEADDIM = 32
        EPSILON = 0.001
        RMS_EPS = 1e-05

        def rmsnorm(x, g, eps=RMS_EPS):
            var = jnp.mean(jnp.square(x), axis=-1, keepdims=True)
            return x * jax.lax.rsqrt(var + eps) * g

        def _hnet_depool(h, h_patch_full, patch_lens):
            h_patch = h_patch_full[..., :D_MODEL]
            bsz, plen = (h_patch.shape[0], h_patch.shape[1])
            seqlen = h.shape[1]
            logp = jnp.full((bsz, plen), -EPSILON, dtype=jnp.float32)
            bidx = jnp.cumsum(patch_lens, axis=1) - 1
            boundary_mask = jnp.zeros((bsz, seqlen), dtype=jnp.int32)
            boundary_mask = boundary_mask.at[jnp.arange(bsz)[:, None], bidx].set(1)
            dt = (-jnp.log(-jnp.expm1(logp))).astype(h_patch.dtype)
            x = h_patch / dt[..., None]
            n_heads = D_MODEL // HEADDIM
            A = -jnp.ones((n_heads,), dtype=jnp.float32)
            bcoef = jnp.exp(logp).astype(h_patch.dtype)
            x4 = x.reshape(bsz, plen, n_heads, HEADDIM)
            a = jnp.exp(dt[:, :, None] * A[None, None, :])
            u = (dt * bcoef)[:, :, None, None] * x4
            a_b = jnp.broadcast_to(a[..., None], u.shape)

            def comb(lft, rgt):
                aL, uL = lft
                aR, uR = rgt
                return (aL * aR, uL * aR + uR)
            _, s = jax.lax.associative_scan(comb, (a_b, u), axis=1)
            depool = s.reshape(bsz, plen, D_MODEL)
            plug = jnp.clip(jnp.cumsum(boundary_mask, axis=1) - 1, 0, plen - 1)
            depool_out = depool[jnp.arange(bsz)[:, None], plug]
            return depool_out + h
        h = rmsnorm(embeds, g_res)
        h = jnp.einsum('bld,ed->ble', h, W_in) + b_in
        h_patch = rmsnorm(patch_embeds, g_init)
        return _hnet_depool(h, h_patch, patch_lens)

    def _L0_ffn_ref(hidden_states, W1, b1, W2, b2):
        import jax, jax.numpy as jnp
        import numpy as np
        HIDDEN = 512
        INTER = 2048
        h = jax.nn.relu(jnp.einsum('bsh,hi->bsi', hidden_states, W1) + b1)
        return jnp.einsum('bsi,ih->bsh', h, W2) + b2

    def _L1_xattn_ref(x, context, Wq, Wkv, null_kv, Wout, ln_scale, ln_bias):
        import jax, jax.numpy as jnp
        import numpy as np
        B, N, DIM = (8, 2048, 512)
        M, CTX = (128, 1024)
        HEADS, DH = (16, 64)
        INNER = HEADS * DH
        EPS = 1e-06

        def _split_heads(t):
            b, n, _ = t.shape
            return t.reshape(b, n, HEADS, DH).transpose(0, 2, 1, 3)
        scale = DH ** (-0.5)
        b = x.shape[0]
        q = _split_heads(jnp.einsum('bnd,df->bnf', x, Wq))
        kv = jnp.einsum('bmc,cf->bmf', context, Wkv)
        k, v = jnp.split(kv, 2, axis=-1)
        k, v = (_split_heads(k), _split_heads(v))
        nk = jnp.broadcast_to(null_kv[0], (b, HEADS, 1, DH))
        nv = jnp.broadcast_to(null_kv[1], (b, HEADS, 1, DH))
        k = jnp.concatenate((nk, k), axis=-2)
        v = jnp.concatenate((nv, v), axis=-2)
        q = q * scale
        sim = jnp.einsum('bhid,bhjd->bhij', q, k)
        attn = jax.nn.softmax(sim, axis=-1)
        out = jnp.einsum('bhij,bhjd->bhid', attn, v)
        out = out.transpose(0, 2, 1, 3).reshape(b, -1, INNER)
        out = jnp.einsum('bnf,fd->bnd', out, Wout)
        mu = jnp.mean(out, axis=-1, keepdims=True)
        var = jnp.var(out, axis=-1, keepdims=True)
        out = (out - mu) * jax.lax.rsqrt(var + EPS) * ln_scale + ln_bias
        return out

    def _L1_ffn_ref(x, w_gate, w_up, w_down):
        import jax, jax.numpy as jnp
        import numpy as np
        BLOCK = 32
        W_BITS = 4
        ACT_BITS = 16

        def act_qdq(x):
            qmax = 2.0 ** (ACT_BITS - 1) - 1.0
            scale = jnp.maximum(jnp.max(jnp.abs(x)) / qmax, 1e-12)
            return jnp.clip(jnp.round(x / scale), -qmax - 1.0, qmax) * scale

        def fixed_qdq_u16(x):
            scale = 1.0 / 65536.0
            return jnp.clip(jnp.round(x / scale), 0.0, 65535.0) * scale

        def lpbq_dequant(w):
            O, I = w.shape
            qmax = 2.0 ** (W_BITS - 1) - 1.0
            wb = w.reshape(O, I // BLOCK, BLOCK)
            s = jnp.maximum(jnp.max(jnp.abs(wb), axis=-1, keepdims=True) / qmax, 1e-12)
            wq = jnp.clip(jnp.round(wb / s), -qmax - 1.0, qmax) * s
            return wq.reshape(O, I)
        x = act_qdq(x)
        up = act_qdq(x @ lpbq_dequant(w_up).T)
        gate = act_qdq(x @ lpbq_dequant(w_gate).T)
        sig = fixed_qdq_u16(jax.nn.sigmoid(gate))
        gate = act_qdq(gate * sig)
        o = act_qdq(gate * up)
        return o @ lpbq_dequant(w_down).T
    x = x + jnp.tanh(g_xattn[0]) * _L0_xattn_ref(_layernorm(x, axis=-1), ctx_2048, mask_BxS2_if0, L0_xattn_W_in, L0_xattn_b_in, L0_xattn_g_res, L0_xattn_g_init)
    x = x + jnp.tanh(g_ffn[0]) * _L0_ffn_ref(_layernorm(x, axis=-1), L0_ffn_W1, L0_ffn_b1, L0_ffn_W2, L0_ffn_b2)
    x = x + jnp.tanh(g_xattn[1]) * _L1_xattn_ref(_layernorm(x, axis=-1), ctx_2048, L1_xattn_Wq, L1_xattn_Wkv, L1_xattn_null_kv, L1_xattn_Wout, L1_xattn_ln_scale, L1_xattn_ln_bias)
    x = x + jnp.tanh(g_ffn[1]) * _L1_ffn_ref(_layernorm(x, axis=-1), L1_ffn_w_gate, L1_ffn_w_up, L1_ffn_w_down)
    return x

_drawn_inputs = setup_inputs


def setup_inputs(seed=0):
    import zlib

    import numpy as np

    out = dict(_drawn_inputs(seed))
    spreads = {'g_ffn': (-1.0, 0.6),
     'L0_xattn_b_in': (0.0, 0.1),
     'L0_xattn_g_res': (1.0, 0.2),
     'L0_xattn_g_init': (1.0, 0.2),
     'L1_xattn_ln_scale': (1.0, 0.2),
     'L1_xattn_ln_bias': (0.0, 0.1)}
    factors = {'L0_ffn_b1': 8.0, 'L0_ffn_b2': 6.338, 'L1_xattn_null_kv': 8.0}
    for name, (base, spread) in spreads.items():
        noise = np.random.default_rng([zlib.crc32(name.encode()), seed]).standard_normal(out[name].shape)
        drawn = base * np.exp(spread * noise) if base else spread * noise
        out[name] = jnp.asarray(drawn.astype(out[name].dtype))
    for name, factor in factors.items():
        out[name] = (out[name] * factor).astype(out[name].dtype)
    return out
```

```python
import numpy as np
import concourse.bass as bass
from concourse import mybir
from contextlib import ExitStack

F32 = mybir.dt.float32
F32R = mybir.dt.float32r
BF16 = mybir.dt.bfloat16
I32 = mybir.dt.int32
ALU = mybir.AluOpType
ACT = mybir.ActivationFunctionType
AX = mybir.AxisListType
RMAX = bass.bass_isa.ReduceOp.max

P = 128
B, S, D = 8, 224, 512
M, DC = 750, 1024
T = B * S
TT = 112
NT = 4
CH = NT * TT
NC = T // CH
KD = D // P
KC = DC // P
FF0 = 2048
NI0 = FF0 // P
FF1 = 1536
NI1 = FF1 // P
H, DH = 16, 64
INNER = H * DH
QB = 32
MAGIC = 1.5 * 2.0 ** 23
LOGP = np.float32(-0.001)
DT = float(np.float32(-np.log(-np.expm1(LOGP))))
BCOEF = float(np.exp(LOGP))
QMAX = 32767.0


class Chain:

    def __init__(self, eng, sem, per=0):
        self.eng, self.sem, self.per, self.base, self.n = eng, sem, per, 0, 0

    def at(self, turn):
        self.base, self.n = turn * self.per, 0

    def step(self, ins):
        self.n += 1
        return ins.then_inc(self.sem, 1)

    def wait(self):
        self.eng.wait_ge(self.sem, self.base + self.n)

    def done(self):
        assert self.n == self.per, (self.n, self.per)


class Mem:

    def __init__(self, nc, name):
        self.nc, self.name, self.stack, self.sems = nc, name, ExitStack(), []

    def __enter__(self):
        self.stack.__enter__()
        return self

    def __exit__(self, *a):
        if self.sems:
            self.nc.clear_and_free_semaphores(self.sems)
            self.nc.all_engine_barrier()
        return self.stack.__exit__(*a)

    def sb(self, name, shape, dtype=F32):
        return self.stack.enter_context(self.nc.sbuf_tensor(f"{self.name}_{name}", shape, dtype))

    def sem(self, name):
        self.sems.append(self.nc.alloc_semaphore(f"{self.name}_{name}"))
        return self.sems[-1]


def f(ap):
    return ap.bitcast(F32)


def three(nc, out, a_hi, a_lo, b_hi, b_lo, first, last):
    nc.tensor.matmul(out, a_hi, b_hi, start=first, stop=False)
    nc.tensor.matmul(out, a_hi, b_lo, start=False, stop=False)
    return nc.tensor.matmul(out, a_lo, b_hi, start=False, stop=last)


def phase_depool(nc, psum, ident, tg, d):
    with Mem(nc, "p1") as m:
        wland = m.sb("wland", [P, KD, D])
        wh, wl = m.sb("wh", [P, KD, D], F32R), m.sb("wl", [P, KD, D], F32R)
        bin_b, gin_b = m.sb("bin_b", [TT, D]), m.sb("gin_b", [TT, D])
        gres = m.sb("gres", [P, KD])
        graw = m.sb("graw", [P, 4])
        lens = m.sb("lens", [B, M], I32)
        lensf, zeros, cum = (m.sb(n, [B, M]) for n in ("lensf", "zeros", "cum"))
        wrap, idx = zeros, lensf
        JP, JC = 125, M // 125
        idxT = m.sb("idxT", [JP, JC, B])
        ti = m.sb("ti", [P, S], I32)
        tf = m.sb("tf", [P, S])
        si = m.sb("si", [P, 2], I32)
        scol = m.sb("scol", [P, 2])
        eq = m.sb("eq", [JP, JC, B, S], BF16)
        ones = m.sb("ones", [JP, P], BF16)
        mark, plug = m.sb("mark", [P, B, S]), m.sb("plug", [P, B, S])
        zrow = m.sb("zrow", [P, S])
        xt = m.sb("xt", [TT, 2, NT, D])
        ctxn = m.sb("ctxn", [TT, NT, DC])
        junk = m.sb("junk", [TT, DC], BF16)
        ssq, rsc = m.sb("ssq", [TT, NT]), m.sb("rsc", [TT, NT])
        uh, ul = m.sb("uh", [TT, 2, NT, D], F32R), m.sb("ul", [TT, 2, NT, D], F32R)
        u32 = m.sb("u32", [TT, D])
        dm, mk = m.sb("dm", [TT, 2, CH]), m.sb("mk", [TT, 2, CH])
        mh, ml = m.sb("mh", [TT, 2, 2, CH], F32R), m.sb("ml", [TT, 2, 2, CH], F32R)
        stats, mv = m.sb("stats", [TT, NT, 6]), m.sb("mv", [TT, NT, 2])
        ve, rs, rr = m.sb("ve", [TT, NT]), m.sb("rs", [TT, NT]), m.sb("rr", [TT, NT])
        nhalf, c_eps, c_dc, c_in = (m.sb(n, [TT, NT]) for n in ("nhalf", "c_eps", "c_dc", "c_in"))
        hold = m.sb("hold", [TT, 1])
        y = m.sb("y", [TT, NT, D])
        yh, yl = m.sb("yh", [P, 2, KD, CH], F32R), m.sb("yl", [P, 2, KD, CH], F32R)
        tmp = m.sb("tmp", [TT, D])

        s = m.sem
        const_in, lens_in, ctx_in, x_out = s("const_in"), s("lens_in"), s("ctx_in"), s("x_out")
        x_in = [s("x_in0"), s("x_in1")]
        pool_c, pool_own = s("pool_c"), s("pool_own")
        idx_ready, idx_t, eq_ready, count_ready = s("idx_ready"), s("idx_t"), s("eq_ready"), s("count_ready")
        dve_own, act_own, w_hi, w_ready = s("dve_own"), s("act_own"), s("w_hi"), s("w_ready")
        var_ready, rstd_ready, y_ready, tr_ready, tr_hi, tr_free = (
            s("var_ready"), s("rstd_ready"), s("y_ready"), s("tr_ready"), s("tr_hi"), s("tr_free"))
        ssq_ready, rsc_ready, u_ready, dm_ready, ex_ready, m_ready = (
            s("ssq_ready"), s("rsc_ready"), s("u_ready"), s("dm_ready"), s("ex_ready"), s("m_ready"))
        out_ready, out_free, x_new = s("out_ready"), s("out_free"), s("x_new")

        with nc.Block() as block:
            @block.sync
            def _(sp):
                sp.dma_start(lens[:, :], d["lens"]).then_inc(lens_in, 16)
                sp.dma_start(graw[:, :], d["gates"].partition_broadcast(P)).then_inc(const_in, 16)
                sp.dma_start(wland[:, :, :], d["w_in_t"].rearrange("(k p) n -> p k n", p=P)).then_inc(const_in, 16)
                sp.dma_start(bin_b[:, :], d["b_in"].partition_broadcast(TT)).then_inc(const_in, 16)
                sp.dma_start(gin_b[:, :], d["g_init"][0:D].partition_broadcast(TT)).then_inc(const_in, 16)
                sp.dma_start(gres[:, :], d["g_res_cols"]).then_inc(const_in, 16)
                for k in range(NC + 1):
                    c = k % NC
                    if k >= 2:
                        sp.wait_ge(x_new, NT * (k - 1))
                        sp.dma_start(d["x1"][CH * (k - 2):CH * (k - 1), :].rearrange("(n p) d -> p n d", p=TT),
                                     xt[:, k % 2]).then_inc(x_out, 16)
                        sp.wait_ge(x_out, 16 * (k - 1))
                    sp.dma_start(xt[:, k % 2], d["x"][CH * c:CH * (c + 1), :].rearrange("(n p) d -> p n d", p=TT)
                                 ).then_inc(x_in[k % 2], 16)
                    if k >= 1:
                        sp.wait_ge(u_ready, NT * k)
                        sp.wait_ge(ssq_ready, NT * k)
                    for b in range(2):
                        src = d["ctx"][2 * c + b, 0:S, :].rearrange("(n p) d -> p n d", p=TT)
                        sp.dma_start(ctxn[:, 2 * b:2 * b + 2, :], src).then_inc(ctx_in, 16)
                sp.wait_ge(x_new, NT * NC)
                sp.dma_start(d["x1"][CH * (NC - 1):T, :].rearrange("(n p) d -> p n d", p=TT), xt[:, (NC - 1) % 2]
                             ).then_inc(x_out, 16)
                sp.wait_ge(x_out, 16 * NC)

            @block.gpsimd
            def _(pool):
                own = Chain(pool, pool_own, 8)
                nc.gpsimd.memset(ident[:, :], 0.0).then_inc(pool_c, 1)
                pool.wait_ge(pool_c, 1)
                nc.gpsimd.affine_select(out=ident[:, :], in_=ident[:, :], compare_op=ALU.not_equal, fill=1.0,
                                        base=0, pattern=[[-1, P]], channel_multiplier=1).then_inc(pool_c, 1)
                for tile, value in ((nhalf, -0.5), (c_eps, 1e-5), (c_dc, 1.0 / DC), (c_in, BCOEF)):
                    nc.gpsimd.memset(tile[:, :], value).then_inc(pool_c, 1)
                nc.gpsimd.iota(ti[:, :], [[1, S]], 0, 0).then_inc(pool_c, 1)
                nc.gpsimd.iota(si[:, :], [[TT, 2]], 0, 1).then_inc(pool_c, 1)

                def prep(k):
                    own.at(k)
                    pool.wait_ge(var_ready, k + 1)
                    own.step(nc.gpsimd.tensor_tensor(rs[:, :], ve[:, :], nhalf[:, :], ALU.pow))
                    own.wait()
                    own.step(nc.gpsimd.tensor_tensor(rr[:, :], rs[:, :], rs[:, :], ALU.mult))
                    own.wait()
                    own.step(nc.gpsimd.tensor_tensor(rr[:, :], rr[:, :], mv[:, :, 1], ALU.mult))
                    own.wait()
                    own.step(nc.gpsimd.tensor_tensor(rr[:, :], rr[:, :], c_eps[:, :], ALU.add))
                    own.wait()
                    own.step(nc.gpsimd.tensor_tensor(rr[:, :], rr[:, :], nhalf[:, :], ALU.pow))
                    own.wait()
                    nc.gpsimd.tensor_tensor(rs[:, :], rs[:, :], rr[:, :], ALU.mult).then_inc(rstd_ready, 1)
                    pool.wait_ge(ssq_ready, NT * k + NT)
                    own.step(nc.gpsimd.tensor_tensor(rsc[:, :], ssq[:, :], c_dc[:, :], ALU.mult))
                    own.wait()
                    own.step(nc.gpsimd.tensor_tensor(rsc[:, :], rsc[:, :], c_eps[:, :], ALU.add))
                    own.wait()
                    own.step(nc.gpsimd.tensor_tensor(rsc[:, :], rsc[:, :], nhalf[:, :], ALU.pow))
                    own.wait()
                    nc.gpsimd.tensor_tensor(rsc[:, :], rsc[:, :], c_in[:, :], ALU.mult).then_inc(rsc_ready, 1)
                    own.done()

                pool.wait_ge(pool_c, 8)
                prep(0)
                with pool.Fori(0, NC // 2) as i:
                    for par in (0, 1):
                        prep(i * 2 + par + 1)

            @block.scalar
            def _(act):
                act.wait_ge(const_in, 80)
                nc.scalar.activation(tg[:, :], graw[:, :], ACT.Tanh).then_inc(act_own, 1)
                act.wait_ge(w_ready, 1)
                nc.scalar.activation(wh[:, :, :], wland[:, :, :], ACT.Copy).then_inc(w_hi, 1)

                def prep(k, par, first=False):
                    act.wait_ge(ctx_in, k * 32 + 32)
                    if not first:
                        act.wait_ge(rsc_ready, k)
                    for n in range(NT):
                        nc.scalar.activation(junk[:, :], ctxn[:, n, :], ACT.Square, accum_out=ssq[:, n:n + 1]
                                             ).then_inc(ssq_ready, 1)
                        act.wait_ge(ssq_ready, k * NT + n + 1)
                    act.wait_ge(dm_ready, k + 1)
                    nc.scalar.activation(dm[:, :, :], dm[:, :, :], ACT.Exp, scale=-DT).then_inc(ex_ready, 1)
                    for n in range(NT):
                        act.wait_ge(tr_ready, k * NT + n + 1)
                        nc.scalar.activation(yh[:, par, :, TT * n:TT * (n + 1)],
                                             psum[:, n % 2, 0:KD * TT].rearrange("p (k t) -> p k t", k=KD), ACT.Copy
                                             ).then_inc(tr_hi, 1)

                prep(0, 0, first=True)
                with act.Fori(0, NC // 2) as i:
                    for par in (0, 1):
                        prep(i * 2 + par + 1, 1 - par)

            @block.vector
            def _(dve):
                v = nc.vector
                pre = Chain(dve, dve_own)
                pre.step(v.memset(zeros[:, :], 0.0))
                pre.step(v.memset(ones[:, :], 1.0))
                pre.step(v.memset(zrow[:, :], 0.0))
                dve.wait_ge(lens_in, 16)
                pre.step(v.tensor_copy(lensf[:, :], lens[:, :]))
                pre.wait()
                pre.step(v.tensor_tensor_scan(cum[:, :], lensf[:, :], zeros[:, :], 0.0, ALU.add, ALU.add))
                pre.wait()
                pre.step(v.tensor_scalar(wrap[:, :], cum[:, :], 0.0, float(S), ALU.is_le, ALU.mult))
                pre.wait()
                v.scalar_tensor_tensor(out=idx[:, :], in0=cum[:, :], scalar=-1.0, in1=wrap[:, :],
                                       op0=ALU.add, op1=ALU.add).then_inc(idx_ready, 1)
                dve.wait_ge(pool_c, 8)
                pre.step(v.tensor_copy(tf[:, :], ti[:, :]))
                pre.step(v.tensor_copy(scol[:, :], si[:, :]))
                dve.wait_ge(const_in, 80)
                for k in range(KD):
                    ins = v.tensor_scalar(wland[:, k, :], wland[:, k, :], gres[:, k:k + 1], None, ALU.mult)
                    if k == KD - 1:
                        ins.then_inc(w_ready, 1)
                    else:
                        pre.step(ins)
                dve.wait_ge(idx_t, 1)
                pre.step(v.tensor_copy(idxT[:, :, :], psum[0:JP, 7, 0:JC * B].rearrange("p (c b) -> p c b", c=JC)))
                pre.wait()
                for c in range(JC):
                    v.tensor_tensor(eq[:, c, :, :], tf[0:JP, :].unsqueeze(1).broadcast_to([JP, B, S]),
                                    idxT[:, c, :].unsqueeze(2).broadcast_to([JP, B, S]), ALU.is_equal
                                    ).then_inc(eq_ready, 1)
                dve.wait_ge(w_hi, 1)
                pre.step(v.tensor_tensor(wl[:, :, :], wland[:, :, :], f(wh[:, :, :]), ALU.subtract))
                for q in range(NC):
                    dve.wait_ge(count_ready, q + 1)
                    pre.step(v.tensor_scalar(mark[:, 2 * q:2 * q + 2, :],
                                             psum[:, 2 + q, 0:CH].rearrange("p (b t) -> p b t", b=2),
                                             1.0, None, ALU.min))
                pre.wait()
                dve.sem_inc(out_free, NT)
                for b in range(B):
                    pre.step(v.tensor_tensor_scan(plug[:, b, :], mark[:, b, :], zrow[:, :], 0.0, ALU.add, ALU.add))
                pre.wait()
                pre.step(v.tensor_scalar(plug[:, :, :], plug[:, :, :], -1.0, 0.0, ALU.add, ALU.max))
                pre.wait()
                pre.step(v.tensor_scalar(plug[:, :, :], plug[:, :, :], float(M - 1), None, ALU.min))
                pre.wait()
                own = Chain(dve, dve_own, 21)
                pre_n = pre.n

                def wait_own():
                    dve.wait_ge(dve_own, own.base + own.n + pre_n)

                def prep(k, par, turn, ci):
                    own.at(k)
                    dve.wait_ge(x_in[par], turn * 16 + 16)
                    for n in range(NT):
                        own.step(v.bn_stats(stats[:, n, :], xt[:, par, n, :]))
                    wait_own()
                    v.memset(hold[:, :], 0.0)
                    for n in range(NT):
                        own.step(v.bn_aggr(mv[:, n, :], stats[:, n, :]))
                    wait_own()
                    v.tensor_scalar(ve[:, :], mv[:, :, 1], 1e-5, None, ALU.add).then_inc(var_ready, 1)
                    pl = plug[0:TT, bass.ds(ci * 2, 2), :]
                    for g in range(2):
                        ins = v.tensor_scalar(dm[:, g, :].rearrange("p (b t) -> p b t", b=2), pl, scol[0:TT, g:g + 1],
                                              0.0, ALU.subtract, ALU.max)
                        if g:
                            ins.then_inc(dm_ready, 1)
                        else:
                            own.step(ins)
                        own.step(v.tensor_scalar(mk[:, g, :].rearrange("p (b t) -> p b t", b=2), pl,
                                                 scol[0:TT, g:g + 1], None, ALU.is_ge))
                    dve.wait_ge(rstd_ready, k + 1)
                    for n in range(NT):
                        v.tensor_scalar(y[:, n, :], xt[:, par, n, :], mv[:, n, 0:1], rs[:, n:n + 1],
                                        ALU.subtract, ALU.mult).then_inc(y_ready, 1)
                    dve.wait_ge(ex_ready, k + 1)
                    wait_own()
                    own.step(v.tensor_tensor(mk[:, :, :], mk[:, :, :], dm[:, :, :], ALU.mult))
                    wait_own()
                    own.step(v.tensor_copy(mh[:, par], mk[:, :, :]))
                    wait_own()
                    v.tensor_tensor(ml[:, par], mk[:, :, :], f(mh[:, par]), ALU.subtract).then_inc(m_ready, 1)
                    for n in range(NT):
                        dve.wait_ge(tr_hi, k * NT + n + 1)
                        v.tensor_tensor(yl[:, par, :, TT * n:TT * (n + 1)],
                                        psum[:, n % 2, 0:KD * TT].rearrange("p (k t) -> p k t", k=KD),
                                        f(yh[:, par, :, TT * n:TT * (n + 1)]), ALU.subtract).then_inc(tr_free, 1)
                    dve.wait_ge(rsc_ready, k + 1)
                    for n in range(NT):
                        own.step(v.scalar_tensor_tensor(out=u32[:, :], in0=ctxn[:, n, 0:D], scalar=rsc[:, n:n + 1],
                                                        in1=gin_b[:, :], op0=ALU.mult, op1=ALU.mult))
                        wait_own()
                        own.step(v.tensor_copy(uh[:, par, n, :], u32[:, :]))
                        wait_own()
                        v.tensor_tensor(ul[:, par, n, :], u32[:, :], f(uh[:, par, n, :]), ALU.subtract
                                        ).then_inc(u_ready, 1)
                        dve.wait_ge(u_ready, k * NT + n + 1)

                def main(c, par):
                    for n in range(NT):
                        dve.wait_ge(out_ready, c * NT + n + 1)
                        v.tensor_tensor(tmp[:, :], psum[0:TT, 2 + n, :], bin_b[:, :], ALU.add).then_inc(out_free, 1)
                        dve.wait_ge(out_free, c * NT + n + 1 + NT)
                        v.scalar_tensor_tensor(out=xt[:, par, n, :], in0=tmp[:, :], scalar=tg[0:TT, 0:1],
                                               in1=xt[:, par, n, :], op0=ALU.mult, op1=ALU.add).then_inc(x_new, 1)
                        dve.wait_ge(x_new, c * NT + n + 1)

                dve.sem_inc(tr_free, 2)
                dve.wait_ge(w_ready, 1)
                dve.wait_ge(eq_ready, JC)
                prep(0, 0, 0, 0)
                own.done()
                dve.wait_ge(act_own, 1)
                with dve.Fori(0, NC // 2) as i:
                    for par in (0, 1):
                        c = i * 2 + par
                        prep(c + 1, 1 - par, i + par, i * -2 + 2 if par else i * 2 + 1)
                        own.done()
                        main(c, par)

            @block.tensor
            def _(pe):
                pe.wait_ge(pool_c, 3)
                pe.wait_ge(idx_ready, 1)
                for c in range(JC):
                    ins = nc.tensor.transpose(psum[0:JP, 7, B * c:B * (c + 1)], idx[:, JP * c:JP * (c + 1)],
                                              ident[0:B, 0:B])
                ins.then_inc(idx_t, 1)
                pe.wait_ge(eq_ready, JC)
                for q in range(NC):
                    for c in range(JC):
                        ins = nc.tensor.matmul(psum[:, 2 + q, 0:CH], ones[:, :],
                                               eq[:, c, 2 * q:2 * q + 2, :].rearrange("p b t -> p (b t)"),
                                               start=(c == 0), stop=(c == JC - 1))
                    ins.then_inc(count_ready, 1)

                def prep(k, par):
                    for n in range(NT):
                        pe.wait_ge(y_ready, k * NT + n + 1)
                        pe.wait_ge(tr_free, k * NT + n + 1)
                        for kt in range(KD):
                            ins = nc.tensor.transpose(psum[:, n % 2, TT * kt:TT * (kt + 1)],
                                                      y[:, n, P * kt:P * (kt + 1)], ident[0:TT, 0:TT])
                        ins.then_inc(tr_ready, 1)

                def main(c, par):
                    pe.wait_ge(tr_free, c * NT + NT + 2)
                    pe.wait_ge(u_ready, c * NT + NT)
                    pe.wait_ge(m_ready, c + 1)
                    for n in range(NT):
                        pe.wait_ge(out_free, c * NT + n + 1)
                        out = psum[0:TT, 2 + n, :]
                        cols = slice(TT * n, TT * (n + 1))
                        for kt in range(KD):
                            three(nc, out, yh[:, par, kt, cols], yl[:, par, kt, cols], wh[:, kt, :], wl[:, kt, :],
                                  kt == 0, False)
                        for g in range(n % 2 + 1):
                            ins = three(nc, out, mh[:, par, g, cols], ml[:, par, g, cols],
                                        uh[:, par, 2 * (n // 2) + g, :], ul[:, par, 2 * (n // 2) + g, :],
                                        False, g == n % 2)
                        ins.then_inc(out_ready, 1)

                pe.wait_ge(w_ready, 1)
                prep(0, 0)
                with pe.Fori(0, NC // 2) as i:
                    for par in (0, 1):
                        prep(i * 2 + par + 1, 1 - par)
                        main(i * 2 + par, par)


class Normed:

    def __init__(self, nc, m, psum, ident, x_dram):
        self.nc, self.psum, self.ident, self.x_dram = nc, psum, ident, x_dram
        self.xt = m.sb("xt", [TT, 2, NT, D])
        self.stats, self.mv = m.sb("stats", [TT, NT, 6]), m.sb("mv", [TT, NT, 2])
        self.ve, self.rs, self.nhalf = m.sb("ve", [TT, NT]), m.sb("rs", [TT, NT]), m.sb("nhalf", [TT, NT])
        self.hold = m.sb("hold", [TT, 1])
        self.y = m.sb("y", [TT, NT, D])
        self.yh, self.yl = m.sb("yh", [P, 2, KD, CH], F32R), m.sb("yl", [P, 2, KD, CH], F32R)
        self.x_in = [m.sem("x_in0"), m.sem("x_in1")]
        self.stats_done, self.var_ready, self.rstd_ready = m.sem("stats_done"), m.sem("var_ready"), m.sem("rstd_ready")
        self.aggr_done, self.nhalf_ready = m.sem("aggr_done"), m.sem("nhalf_ready")
        self.y_ready, self.tr_ready, self.tr_hi, self.tr_free = (
            m.sem("y_ready"), m.sem("tr_ready"), m.sem("tr_hi"), m.sem("tr_free"))

    def load(self, sp, k):
        c = k % NC
        sp.dma_start(self.xt[:, k % 2], self.x_dram[CH * c:CH * (c + 1), :].rearrange("(n p) d -> p n d", p=TT)
                     ).then_inc(self.x_in[k % 2], 16)

    def start_pool(self, pool):
        self.nc.gpsimd.memset(self.nhalf[:, :], -0.5).then_inc(self.nhalf_ready, 1)
        pool.wait_ge(self.nhalf_ready, 1)

    def rstd(self, pool, k):
        pool.wait_ge(self.var_ready, k + 1)
        self.nc.gpsimd.tensor_tensor(self.rs[:, :], self.ve[:, :], self.nhalf[:, :], ALU.pow).then_inc(self.rstd_ready, 1)

    def start_dve(self, dve):
        dve.sem_inc(self.tr_free, 2)

    def row_stats(self, dve, par, turn, n):
        v = self.nc.vector
        if n == 0:
            dve.wait_ge(self.x_in[par], turn * 16 + 16)
        v.bn_stats(self.stats[:, n, :], self.xt[:, par, n, :]).then_inc(self.stats_done, 1)

    def aggregate(self, dve, k):
        v = self.nc.vector
        dve.wait_ge(self.stats_done, k * NT + NT)
        v.memset(self.hold[:, :], 0.0)
        for n in range(NT):
            v.bn_aggr(self.mv[:, n, :], self.stats[:, n, :]).then_inc(self.aggr_done, 1)
        dve.wait_ge(self.aggr_done, k * NT + NT)
        v.tensor_scalar(self.ve[:, :], self.mv[:, :, 1], 1e-5, None, ALU.add).then_inc(self.var_ready, 1)

    def normalise(self, dve, k, par, n):
        if n == 0:
            dve.wait_ge(self.rstd_ready, k + 1)
        self.nc.vector.tensor_scalar(self.y[:, n, :], self.xt[:, par, n, :], self.mv[:, n, 0:1], self.rs[:, n:n + 1],
                                     ALU.subtract, ALU.mult).then_inc(self.y_ready, 1)

    def transpose(self, pe, k, n):
        nc = self.nc
        pe.wait_ge(self.y_ready, k * NT + n + 1)
        pe.wait_ge(self.tr_free, k * NT + n + 1)
        for kt in range(KD):
            ins = nc.tensor.transpose(self.psum[:, n % 2, TT * kt:TT * (kt + 1)], self.y[:, n, P * kt:P * (kt + 1)],
                                      self.ident[0:TT, 0:TT])
        ins.then_inc(self.tr_ready, 1)

    def hi(self, act, k, par, n):
        act.wait_ge(self.tr_ready, k * NT + n + 1)
        self.nc.scalar.activation(self.yh[:, par, :, TT * n:TT * (n + 1)],
                                  self.psum[:, n % 2, 0:KD * TT].rearrange("p (k t) -> p k t", k=KD), ACT.Copy
                                  ).then_inc(self.tr_hi, 1)

    def lo(self, dve, k, par, n):
        dve.wait_ge(self.tr_hi, k * NT + n + 1)
        self.nc.vector.tensor_tensor(self.yl[:, par, :, TT * n:TT * (n + 1)],
                                     self.psum[:, n % 2, 0:KD * TT].rearrange("p (k t) -> p k t", k=KD),
                                     f(self.yh[:, par, :, TT * n:TT * (n + 1)]), ALU.subtract
                                     ).then_inc(self.tr_free, 1)

    def split(self, pe, k):
        pe.wait_ge(self.tr_free, k * NT + NT + 2)


def phase_relu_ffn(nc, psum, ident, tg, d):
    with Mem(nc, "p2") as m:
        nm = Normed(nc, m, psum, ident, d["x1"])
        WL = 1024
        NW = KD * FF0 // WL * 2
        land = m.sb("land", [P, WL])
        w1h, w1l = m.sb("w1h", [P, KD, FF0], F32R), m.sb("w1l", [P, KD, FF0], F32R)
        w2h, w2l = m.sb("w2h", [P, NI0, D], F32R), m.sb("w2l", [P, NI0, D], F32R)
        b1, b2b = m.sb("b1", [P, NI0]), m.sb("b2b", [TT, D])
        hf = m.sb("hf", [P, 2, CH])
        hh, hl = m.sb("hh", [P, 2, CH], F32R), m.sb("hl", [P, 2, CH], F32R)
        tmp = m.sb("tmp", [TT, D])
        NB = 24
        wq = m.sb("wq", [P, NB, QB])
        wt = m.sb("wt", [P, NB, QB])
        bs, br = m.sb("bs", [P, NB]), m.sb("br", [P, NB])
        QS = 3 * KD * FF1 // (NB * QB) // NC
        s = m.sem
        w_in, w_hi, w_lo, b_in, x_out = s("w_in"), s("w_hi"), s("w_lo"), s("b_in"), s("x_out")
        h_ready, h_relu, h_hi, h_split, h_used = s("h_ready"), s("h_relu"), s("h_hi"), s("h_split"), s("h_used")
        out_ready, out_free, x_new = s("out_ready"), s("out_free"), s("x_new")
        q_in, q_own, q_out, q_stored = s("q_in"), s("q_own"), s("q_out"), s("q_stored")

        def slab(name, j):
            return d[name][j // 2, :, NB * QB * (j % 2):NB * QB * (j % 2 + 1)]

        def part(h, j):
            if j < NW // 2:
                return (w1h, w1l)[h][:, j // 2, WL * (j % 2):WL * (j % 2 + 1)]
            i = 2 * (j - NW // 2)
            return (w2h, w2l)[h][:, i:i + 2, :].rearrange("p k n -> p (k n)")

        with nc.Block() as block:
            @block.sync
            def _(sp):
                nm.load(sp, 0)
                sp.dma_start(b1[:, :], d["b1_cols"]).then_inc(b_in, 16)
                sp.dma_start(b2b[:, :], d["b2"].partition_broadcast(TT)).then_inc(b_in, 16)
                for j in range(NW):
                    if j:
                        sp.wait_ge(w_lo, j)
                    if j < NW // 2:
                        src = d["w1"][P * (j // 2):P * (j // 2 + 1), WL * (j % 2):WL * (j % 2 + 1)]
                        sp.dma_start(land[:, :], src).then_inc(w_in, 16)
                    else:
                        i = 2 * P * (j - NW // 2)
                        src = d["w2"][i:i + 2 * P, :].rearrange("(k p) n -> p k n", p=P)
                        sp.dma_start(land[:, :].rearrange("p (k n) -> p k n", k=2), src).then_inc(w_in, 16)
                nm.load(sp, 1)
                for j in range(NC * QS):
                    if j:
                        sp.wait_ge(q_out, j)
                        sp.dma_start(slab("wdq", j - 1), wt[:, :, :].rearrange("p a b -> p (a b)")).then_inc(q_stored, 16)
                    if j % QS == 0 and j:
                        k = j // QS
                        sp.wait_ge(x_new, NT * k)
                        sp.dma_start(d["x2"][CH * (k - 1):CH * k, :].rearrange("(n p) d -> p n d", p=TT),
                                     nm.xt[:, (k - 1) % 2]).then_inc(x_out, 16)
                        sp.wait_ge(x_out, 16 * k)
                        nm.load(sp, k + 1)
                    sp.dma_start(wq[:, :, :].rearrange("p a b -> p (a b)"), slab("w_q", j)).then_inc(q_in, 16)
                sp.wait_ge(q_out, NC * QS)
                sp.dma_start(slab("wdq", NC * QS - 1), wt[:, :, :].rearrange("p a b -> p (a b)")).then_inc(q_stored, 16)
                sp.wait_ge(x_new, NT * NC)
                sp.dma_start(d["x2"][CH * (NC - 1):T, :].rearrange("(n p) d -> p n d", p=TT), nm.xt[:, (NC - 1) % 2]
                             ).then_inc(x_out, 16)
                sp.wait_ge(x_out, 16 * NC)
                sp.wait_ge(q_stored, 16 * NC * QS + 16)

            @block.gpsimd
            def _(pool):
                nm.start_pool(pool)
                nm.rstd(pool, 0)
                with pool.Fori(0, NC // 2) as i:
                    for par in (0, 1):
                        nm.rstd(pool, i * 2 + par + 1)

            @block.scalar
            def _(act):
                for j in range(NW):
                    act.wait_ge(w_in, 16 * (j + 1))
                    nc.scalar.activation(part(0, j), land[:, :], ACT.Copy).then_inc(w_hi, 1)
                    if j == KD - 1:
                        for n in range(NT):
                            nm.hi(act, 0, 0, n)
                act.wait_ge(b_in, 32)
                act.sem_inc(h_relu, 2)
                with act.Fori(0, NC // 2) as i:
                    for par in (0, 1):
                        c = i * 2 + par
                        for it in range(NI0):
                            act.wait_ge(h_ready, c * NI0 + it + 1)
                            act.wait_ge(h_split, c * NI0 + it + 1)
                            nc.scalar.activation(hf[:, it % 2, :], psum[:, 2 + it % 2, 0:CH], ACT.Relu,
                                                 bias=b1[:, it:it + 1]).then_inc(h_relu, 1)
                            if 11 <= it < 15:
                                nm.hi(act, c + 1, 1 - par, it - 11)

            @block.vector
            def _(dve):
                v = nc.vector
                own = Chain(dve, q_own, 7 * QS)

                def dequantise(j):
                    dve.wait_ge(q_in, j * 16 + 16)
                    own.step(v.tensor_reduce(bs[:, :], wq[:, :, :], AX.X, ALU.max, apply_absolute_value=True))
                    own.wait()
                    own.step(v.tensor_scalar(bs[:, :], bs[:, :], float(np.float32(1.0) / np.float32(7.0)), 1e-12, ALU.mult, ALU.max))
                    own.wait()
                    own.step(v.reciprocal(br[:, :], bs[:, :]))
                    own.wait()
                    own.step(v.tensor_tensor(wq[:, :, :], wq[:, :, :], br[:, :].unsqueeze(2).broadcast_to([P, NB, QB]),
                                             ALU.mult))
                    yield
                    own.wait()
                    own.step(v.tensor_scalar(wq[:, :, :], wq[:, :, :], MAGIC, -MAGIC, ALU.add, ALU.add))
                    own.wait()
                    own.step(v.tensor_scalar(wq[:, :, :], wq[:, :, :], 7.0, -8.0, ALU.min, ALU.max))
                    own.wait()
                    own.step(v.tensor_tensor(wq[:, :, :], wq[:, :, :], bs[:, :].unsqueeze(2).broadcast_to([P, NB, QB]),
                                             ALU.mult))
                    dve.wait_ge(q_stored, j * 16 + 16)
                    own.wait()
                    v.transpose(wt[:, :, :].rearrange("p a b -> p (a b)"), wq[:, :, :].rearrange("p a b -> p (a b)")
                                ).then_inc(q_out, 1)
                    yield

                nm.start_dve(dve)
                dve.sem_inc(h_split, 2)
                dve.sem_inc(out_free, NT)
                dve.sem_inc(q_stored, 16)
                for n in range(NT):
                    nm.row_stats(dve, 0, 0, n)
                nm.aggregate(dve, 0)
                for n in range(NT):
                    nm.normalise(dve, 0, 0, n)
                for j in range(NW):
                    dve.wait_ge(w_hi, j + 1)
                    v.tensor_tensor(part(1, j), land[:, :], f(part(0, j)), ALU.subtract).then_inc(w_lo, 1)
                    if j == KD - 1:
                        for n in range(NT):
                            nm.lo(dve, 0, 0, n)
                with dve.Fori(0, NC // 2) as i:
                    for par in (0, 1):
                        c = i * 2 + par
                        own.at(c)
                        slabs = [dequantise(c * QS + r) for r in range(QS)]
                        for it in range(NI0):
                            dve.wait_ge(h_relu, c * NI0 + it + 1 + 2)
                            if it >= 2:
                                dve.wait_ge(h_used, c * (NI0 - 1) + it - 1)
                            v.tensor_copy(hh[:, it % 2, :], hf[:, it % 2, :]).then_inc(h_hi, 1)
                            dve.wait_ge(h_hi, c * NI0 + it + 1)
                            v.tensor_tensor(hl[:, it % 2, :], hf[:, it % 2, :],
                                            f(hh[:, it % 2, :]), ALU.subtract).then_inc(h_split, 1)
                            if it < 2 * QS:
                                next(slabs[it // 2])
                            if 3 <= it < 7:
                                nm.row_stats(dve, 1 - par, i + par, it - 3)
                            elif it == 7:
                                nm.aggregate(dve, c + 1)
                            elif 8 <= it < 12:
                                nm.normalise(dve, c + 1, 1 - par, it - 8)
                            elif it >= 12:
                                nm.lo(dve, c + 1, 1 - par, it - 12)
                        own.done()
                        for n in range(NT):
                            dve.wait_ge(out_ready, c * NT + n + 1)
                            v.tensor_tensor(tmp[:, :], psum[0:TT, 4 + n, :], b2b[:, :], ALU.add).then_inc(out_free, 1)
                            dve.wait_ge(out_free, c * NT + n + 1 + NT)
                            v.scalar_tensor_tensor(out=nm.xt[:, par, n, :], in0=tmp[:, :], scalar=tg[0:TT, 2:3],
                                                   in1=nm.xt[:, par, n, :], op0=ALU.mult, op1=ALU.add).then_inc(x_new, 1)
                            dve.wait_ge(x_new, c * NT + n + 1)

            @block.tensor
            def _(pe):
                for n in range(NT):
                    nm.transpose(pe, 0, n)
                pe.wait_ge(w_lo, NW // 2)

                def up(c, par, it):
                    pe.wait_ge(h_relu, c * NI0 + it + 1)
                    for kt in range(KD):
                        cols = slice(P * it, P * (it + 1))
                        ins = three(nc, psum[:, 2 + it % 2, 0:CH], w1h[:, kt, cols], w1l[:, kt, cols],
                                    nm.yh[:, par, kt, :], nm.yl[:, par, kt, :], kt == 0, kt == KD - 1)
                    ins.then_inc(h_ready, 1)

                def down(c, par, it):
                    pe.wait_ge(h_split, c * NI0 + it + 1 + 2)
                    for n in range(NT):
                        if it == 0:
                            pe.wait_ge(out_free, c * NT + n + 1)
                        cols = slice(TT * n, TT * (n + 1))
                        ins = three(nc, psum[0:TT, 4 + n, :], hh[:, it % 2, cols], hl[:, it % 2, cols],
                                    w2h[:, it, :], w2l[:, it, :], it == 0, it == NI0 - 1)
                        if it == NI0 - 1:
                            ins.then_inc(out_ready, 1)
                        elif n == NT - 1:
                            ins.then_inc(h_used, 1)

                with pe.Fori(0, NC // 2) as i:
                    for par in (0, 1):
                        c = i * 2 + par
                        nm.split(pe, c)
                        up(c, par, 0)
                        for it in range(NI0):
                            if it + 1 < NI0:
                                up(c, par, it + 1)
                            if it == 0:
                                pe.wait_ge(w_lo, NW)
                            down(c, par, it)
                            if 9 <= it < 13:
                                nm.transpose(pe, c + 1, it - 9)


def phase_queries(nc, psum, ident, tg, d):
    with Mem(nc, "p3") as m:
        nm = Normed(nc, m, psum, ident, d["x2"])
        NG = INNER // P
        RG = 4
        land = m.sb("land", [P, KD, INNER])
        wh, wl = m.sb("wh", [P, KD, INNER], F32R), m.sb("wl", [P, KD, INNER], F32R)
        stage = m.sb("stage", [P, RG, CH])
        s = m.sem
        w_in, w_hi, w_lo = s("w_in"), s("w_hi"), s("w_lo")
        q_ready, q_done = s("q_ready"), s("q_done")
        q_out = [s(f"q_out{i}") for i in range(RG)]

        with nc.Block() as block:
            @block.sync
            def _(sp):
                nm.load(sp, 0)
                sp.dma_start(land[:, :, :], d["wq"].rearrange("(k p) n -> p k n", p=P)).then_inc(w_in, 16)
                nm.load(sp, 1)
                for k in range(NC):
                    for g in range(NG):
                        e = k * NG + g
                        sp.wait_ge(q_done, e + 1 + RG)
                        sp.dma_start(d["qT"][P * g:P * (g + 1), CH * k:CH * (k + 1)], stage[:, g % RG, :]
                                     ).then_inc(q_out[g % RG], 16)
                        if g == 0 and k + 2 <= NC:
                            sp.wait_ge(nm.y_ready, NT * (k + 1))
                            nm.load(sp, k + 2)
                for i in range(RG):
                    sp.wait_ge(q_out[i], 16 + 16 * NC * NG // RG)

            @block.gpsimd
            def _(pool):
                nm.start_pool(pool)
                nm.rstd(pool, 0)
                with pool.Fori(0, NC // 2) as i:
                    for par in (0, 1):
                        nm.rstd(pool, i * 2 + par + 1)

            @block.scalar
            def _(act):
                act.wait_ge(w_in, 16)
                nc.scalar.activation(wh[:, :, :], land[:, :, :], ACT.Copy).then_inc(w_hi, 1)
                for n in range(NT):
                    nm.hi(act, 0, 0, n)
                act.sem_inc(q_done, RG)
                for i in range(RG):
                    act.sem_inc(q_out[i], 16)
                with act.Fori(0, NC // 2) as i:
                    for par in (0, 1):
                        c = i * 2 + par
                        for g in range(NG):
                            act.wait_ge(q_ready, c * NG + g + 1)
                            act.wait_ge(q_out[g % RG], (c * (NG // RG) + g // RG) * 16 + 16)
                            nc.scalar.activation(stage[:, g % RG, :], psum[:, 2 + g % RG, 0:CH], ACT.Copy,
                                                 scale=DH ** -0.5).then_inc(q_done, 1)
                            if g >= NG - NT:
                                nm.hi(act, c + 1, 1 - par, g - (NG - NT))

            @block.vector
            def _(dve):
                v = nc.vector
                nm.start_dve(dve)
                for n in range(NT):
                    nm.row_stats(dve, 0, 0, n)
                nm.aggregate(dve, 0)
                for n in range(NT):
                    nm.normalise(dve, 0, 0, n)
                dve.wait_ge(w_hi, 1)
                v.tensor_tensor(wl[:, :, :], land[:, :, :], f(wh[:, :, :]), ALU.subtract).then_inc(w_lo, 1)
                for n in range(NT):
                    nm.lo(dve, 0, 0, n)
                with dve.Fori(0, NC // 2) as i:
                    for par in (0, 1):
                        for n in range(NT):
                            nm.row_stats(dve, 1 - par, i + par, n)
                        nm.aggregate(dve, i * 2 + par + 1)
                        for n in range(NT):
                            nm.normalise(dve, i * 2 + par + 1, 1 - par, n)
                        for n in range(NT):
                            nm.lo(dve, i * 2 + par + 1, 1 - par, n)

            @block.tensor
            def _(pe):
                for n in range(NT):
                    nm.transpose(pe, 0, n)
                pe.wait_ge(w_lo, 1)
                with pe.Fori(0, NC // 2) as i:
                    for par in (0, 1):
                        c = i * 2 + par
                        nm.split(pe, c)
                        for g in range(NG):
                            pe.wait_ge(q_done, c * NG + g + 1)
                            for kt in range(KD):
                                cols = slice(P * g, P * (g + 1))
                                ins = three(nc, psum[:, 2 + g % RG, 0:CH], wh[:, kt, cols], wl[:, kt, cols],
                                            nm.yh[:, par, kt, :], nm.yl[:, par, kt, :], kt == 0, kt == KD - 1)
                            ins.then_inc(q_ready, 1)
                            if NG - NT - 1 <= g < NG - 1:
                                nm.transpose(pe, c + 1, g - (NG - NT - 1))


TURN = ("S0 G0 R0 C4 G1 C5 T00 T01 S1 G2 R1 C6 T02 G3 C7 A0 T10 S2 G4 R2 Q T11 T12 G5 c0 A1 T20 "
        "S3 G6 R3 c1 T21 T22 G7 c2 A2 T30 G8 c3 T31 T32 G9 A3").split()


def turn_steps(project=True, read_on=True, keys=False, values=False):
    steps = [x for x in TURN if (project or x[0] not in "GCQ") and (read_on or x[0] != "c")]
    if keys:
        steps.insert(steps.index("G8"), "K")
    if values:
        steps.insert(steps.index("G1"), "V")
    return steps


def phase_attention(nc, psum, ident, d):
    HG = 4
    GW = HG * DH
    NG = H // HG
    ROWS = M // 6
    MK = M + 1
    MP = M + 2
    HW = 376
    LO = M - HW
    BK = 512
    NP = 10
    NU = NG * B
    with Mem(nc, "p4") as m:
        wland = m.sb("wland", [P, 2, KC, GW])
        wh, wl = m.sb("wh", [P, 2, KC, GW], F32R), m.sb("wl", [P, 2, KC, GW], F32R)
        land = m.sb("land", [P, 4, 2, HW])
        ch, cl = m.sb("ch", [P, 2, KC, HW], F32R), m.sb("cl", [P, 2, KC, HW], F32R)
        kt_ = m.sb("kt", [P, 2, HG, MP], F32R)
        v_ = m.sb("v", [P, 2, 6, HG, 2 * DH], F32R)
        q32 = m.sb("q32", [P, HG, S])
        qh, ql = m.sb("qh", [P, 2, HG, S], F32R), m.sb("ql", [P, 2, HG, S], F32R)
        p = m.sb("p", [TT, 4, MP])
        ph, pl = m.sb("ph", [P, 4, 2 * S], F32R), m.sb("pl", [P, 4, 2 * S], F32R)
        tmp = m.sb("tmp", [DH, 2, S])
        ao = m.sb("ao", [P, 2, 2, S])
        negm, rsum, rinv = m.sb("negm", [TT, 4]), m.sb("rsum", [TT, 4]), m.sb("rinv", [TT, 4])
        hold = m.sb("hold", [TT, 4])
        nk, nkh = m.sb("nk", [P, 2]), m.sb("nkh", [P, 2], F32R)
        nv, nvr = m.sb("nv", [1, DH]), m.sb("nvr", [1, HG, 2 * DH], F32R)

        s = m.sem
        w_in, w_hi, w_lo = [s("wk_in"), s("wv_in")], s("w_hi"), s("w_lo")
        c_in, c_hi, c_lo = [s(f"c_in{i}") for i in range(4)], s("c_hi"), s("c_lo")
        q_in, q_hi, q_lo = s("q_in"), s("q_hi"), s("q_lo")
        null_in, null_own, null_row = s("null_in"), s("null_own"), s("null_row")
        sc_ready, mx_done, exp_done = s("sc_ready"), s("mx_done"), s("exp_done")
        rinv_done, norm_done = s("rinv_done"), s("norm_done")
        at_ready, at_hi, at_done = s("at_ready"), s("at_hi"), s("at_done")
        pj_ready, pj_hi, pj_lo = s("pj_ready"), s("pj_hi"), s("pj_lo")
        ao_out = [s(f"ao_out{i}") for i in range(4)]

        def wait(e, sem, value):
            if not isinstance(value, int) or value > 0:
                e.wait_ge(sem, value)

        def group(i):
            half, j = divmod(i, 5)
            return ("k", half, j) if j < 2 else ("v", half, 3 * half + j - 2)

        def run(e, unit, group_start=None):
            def pair(g, k, u0, turn, change=False, last=False):
                if change:
                    later = [(g, B - 1), (g + 1, 0), (g + 1, 1)]
                else:
                    later = [(g, k * 2 + 1), (g, k * 2 + 2), (g, k * 2 + 3)]
                here = [(g, k * 2), (g, k * 2 + 1)]
                for par in (0, 1):
                    unit(u0 + par, par, turn, here[par], later[par], later[par + 1],
                         dict(project=not (last and par), read_on=not last,
                              keys=change and par == 0, values=change and par == 1))

            with e.Fori(0, NG - 1) as g:
                if group_start:
                    group_start(g)
                with e.Fori(0, B // 2 - 1) as k:
                    pair(g, k, g * B + k * 2, g * (B // 2) + k)
                pair(g, B // 2 - 1, g * B + (B - 2), g * (B // 2) + (B // 2 - 1), change=True)
            g = NG - 1
            with e.Fori(0, B // 2 - 1) as k:
                pair(g, k, k * 2 + g * B, k + g * (B // 2))
            pair(g, B // 2 - 1, NU - 2, NU // 2 - 1, last=True)

        with nc.Block() as block:
            @block.sync
            def _(sp):
                def weights(g):
                    for i in range(2):
                        src = d["wkv"][:, bass.ds(g * GW + i * INNER, GW)].rearrange("(k p) n -> p k n", p=P)
                        sp.dma_start(wland[:, i], src).then_inc(w_in[i], 16)

                def piece(w, b, j):
                    half, jj = divmod(j, 4)
                    sp.wait_ge(c_lo, w * 8 + j + 1)
                    src = d["ctx_t"][bass.ds(b, 1), 2 * P * jj:2 * P * (jj + 1), half * LO:half * LO + HW]
                    sp.dma_start(land[:, jj], src.rearrange("o (k p) t -> p (o k) t", p=P)).then_inc(c_in[jj], 16)

                def queries(u, g, b):
                    wait(sp, q_lo, u)
                    src = d["qT"][bass.ds(g * GW, GW), bass.ds(b * S, S)].rearrange("(h e) t -> e h t", e=DH)
                    for half in range(2):
                        sp.dma_start(q32[DH * half:DH * (half + 1)], src).then_inc(q_in, 16)

                def store(u, par, g, b, pr):
                    sp.wait_ge(at_done, u * 16 + (8 * pr + 8 + 2))
                    dst = d["aT"][bass.ds(g * GW + pr * P, P), bass.ds(b * S, S)]
                    sp.dma_start(dst, ao[:, par, pr, :]).then_inc(ao_out[2 * par + pr], 16)

                def unit(u, par, turn, here, next1, next2, kind):
                    if kind["project"]:
                        queries(u + 1, *next1)
                    for j in range(8):
                        if j == 4:
                            store(u, par, *here, 0)
                        if kind["read_on"]:
                            piece(u + 2, next2[1], j)
                    store(u, par, *here, 1)

                weights(0)
                for j in range(8):
                    piece(0, 0, j)
                sp.wait_ge(null_own, 1)
                for half in range(2):
                    sp.dma_start(nk[DH * half:DH * (half + 1), 0:1], d["null_kv"][0].unsqueeze(1)).then_inc(null_in, 16)
                sp.dma_start(nv[:, :], d["null_kv"][1:2, :]).then_inc(null_in, 16)
                queries(0, 0, 0)
                sp.wait_ge(null_own, 8)
                for par in range(2):
                    sp.dma_start(f(v_[ROWS:ROWS + 1, par, 5, :, :]), f(nvr[:, :, :])).then_inc(null_row, 16)
                for j in range(8):
                    piece(1, 1, j)
                def group_start(g):
                    sp.wait_ge(w_lo, g * 2 + 2)
                    weights(g + 1)
                run(sp, unit, group_start)
                for i in range(4):
                    sp.wait_ge(ao_out[i], 16 * (NU // 2) + 16)

            @block.gpsimd
            def _(pool):
                nc.gpsimd.memset(nk[:, :], 0.0).then_inc(null_own, 1)

                def unit(u, par, turn, here, next1, next2, kind):
                    for n in range(2 * HG):
                        pool.wait_ge(rinv_done, u * 8 + n + 1)
                        nc.gpsimd.tensor_tensor(hold[:, n % 4:n % 4 + 1], rinv[:, n % 4:n % 4 + 1], rinv[:, n % 4:n % 4 + 1], ALU.mult)
                        nc.gpsimd.tensor_scalar(p[:, n % 4, 0:MK], p[:, n % 4, 0:MK], rinv[:, n % 4:n % 4 + 1], 1.0,
                                                ALU.mult, ALU.mult).then_inc(norm_done, 1)
                run(pool, unit)

            def weights_free(e, step, u):
                wait(e, pj_ready, u * NP + (NP + 7 if step == "K" else NP))

            def rows_free(e, u, j):
                wait(e, pj_ready, u * NP + (NP + 5 if j < 4 else NP))

            @block.scalar
            def _(act):
                def split(step, u, par, wgroup):
                    if step in "KV":
                        i = "KV".index(step)
                        act.wait_ge(w_in[i], wgroup * 16 + 16)
                        weights_free(act, step, u)
                        nc.scalar.activation(wh[:, i], wland[:, i], ACT.Copy).then_inc(w_hi, 1)
                    elif step == "Q":
                        act.wait_ge(q_in, u * 32 + 64)
                        nc.scalar.activation(qh[:, 1 - par], q32[:, :, :], ACT.Copy).then_inc(q_hi, 1)
                    else:
                        w, j = u + (1 if step[0] == "C" else 2), int(step[1])
                        act.wait_ge(c_in[j % 4], w * 32 + (j // 4) * 16 + 16)
                        rows_free(act, u, j)
                        nc.scalar.activation(ch[:, j // 4, 2 * (j % 4):2 * (j % 4) + 2, :], land[:, j % 4], ACT.Copy
                                             ).then_inc(c_hi, 1)

                def project(u, par, i):
                    kind, half, j = group(i)
                    act.wait_ge(pj_ready, u * NP + (NP + i + 1))
                    bank = psum[:, 6 + i % 2, :]
                    if kind == "k":
                        t0, t1 = (0, HW) if half == 0 else (HW, M)
                        for e in range(2):
                            ins = nc.scalar.activation(kt_[0:DH, 1 - par, 2 * j + e, t0:t1],
                                                       bank[DH * e:DH * (e + 1), 0:t1 - t0], ACT.Copy)
                    else:
                        ins = nc.scalar.activation(v_[0:ROWS, 1 - par, j, :, 0:DH],
                                                   bank[0:ROWS, 0:GW].rearrange("p (h e) -> p h e", h=HG), ACT.Copy)
                    ins.then_inc(pj_hi, 1)

                def unit(u, par, turn, here, next1, next2, kind):
                    for step in turn_steps(**kind):
                        if step[0] in "CcQKV":
                            split(step, u, par, next1[0] if step == "V" else next2[0])
                        elif step[0] == "G":
                            project(u, par, int(step[1]))
                        elif step[0] == "S":
                            for i in range(2):
                                n = 2 * int(step[1]) + i
                                act.wait_ge(mx_done, u * 8 + n + 1)
                                nc.scalar.activation(p[:, n % 4, 0:MK],
                                                     psum[0:TT, 2 * i:2 * i + 2, :].rearrange("p a n -> p (a n)")[:, 0:MK],
                                                     ACT.Exp, bias=negm[:, n % 4:n % 4 + 1],
                                                     accum_out=rsum[:, n % 4:n % 4 + 1]).then_inc(exp_done, 1)
                        elif step[0] == "T":
                            h, c = int(step[1]), int(step[2])
                            rows = ROWS + (c == 2)
                            act.wait_ge(at_ready, u * 16 + (4 * h + c + 1))
                            nc.scalar.activation(ph[0:rows, (3 * h + c) % 4, :], psum[0:rows, 4 + c % 2, 0:2 * S],
                                                 ACT.Copy).then_inc(at_hi, 1)
                        elif step[0] == "A":
                            h = int(step[1])
                            act.wait_ge(at_ready, u * 16 + (4 * h + 4))
                            nc.scalar.activation(tmp[:, h % 2, :], psum[DH:P, 5, 0:S], ACT.Copy).then_inc(at_hi, 1)

                act.sem_inc(exp_done, 2)
                for step in ("K", "c0", "c1", "c2", "c3"):
                    split(step, -2, 1, 0)
                for step in ("V", "C4", "C5", "C6", "C7"):
                    split(step, -1, 1, 0)
                for i in range(NP):
                    project(-1, 1, i)
                    if i == 5:
                        for step in ("Q", "c0", "c1", "c2", "c3"):
                            split(step, -1, 1, 0)
                run(act, unit)

            @block.vector
            def _(dve):
                v = nc.vector

                def split(step, u, par, wgroup):
                    if step in "KV":
                        i = "KV".index(step)
                        dve.wait_ge(w_hi, wgroup * 2 + i + 1)
                        v.tensor_tensor(wl[:, i], wland[:, i], f(wh[:, i]), ALU.subtract).then_inc(w_lo, 1)
                    elif step == "Q":
                        dve.wait_ge(q_hi, u + 2)
                        v.tensor_tensor(ql[:, 1 - par], q32[:, :, :], f(qh[:, 1 - par]), ALU.subtract).then_inc(q_lo, 1)
                    else:
                        w, j = u + (1 if step[0] == "C" else 2), int(step[1])
                        dve.wait_ge(c_hi, w * 8 + j + 1)
                        at = (slice(None), j // 4, slice(2 * (j % 4), 2 * (j % 4) + 2))
                        v.tensor_tensor(cl[at], land[:, j % 4], f(ch[at]), ALU.subtract).then_inc(c_lo, 1)

                def project(u, par, i):
                    kind, half, j = group(i)
                    dve.wait_ge(pj_hi, u * NP + (NP + i + 1))
                    bank = psum[:, 6 + i % 2, :]
                    if kind == "k":
                        t0, t1 = (0, HW) if half == 0 else (HW, M)
                        for e in range(2):
                            ins = v.tensor_tensor(kt_[DH:P, 1 - par, 2 * j + e, t0:t1],
                                                  bank[DH * e:DH * (e + 1), 0:t1 - t0],
                                                  f(kt_[0:DH, 1 - par, 2 * j + e, t0:t1]), ALU.subtract)
                    else:
                        ins = v.tensor_tensor(v_[0:ROWS, 1 - par, j, :, DH:2 * DH],
                                              bank[0:ROWS, 0:GW].rearrange("p (h e) -> p h e", h=HG),
                                              f(v_[0:ROWS, 1 - par, j, :, 0:DH]), ALU.subtract)
                    ins.then_inc(pj_lo, 1)

                def unit(u, par, turn, here, next1, next2, kind):
                    for step in turn_steps(**kind):
                        if step[0] in "CcQKV":
                            split(step, u, par, next1[0] if step == "V" else next2[0])
                        elif step[0] == "G":
                            project(u, par, int(step[1]))
                        elif step[0] == "S":
                            for i in range(2):
                                n = 2 * int(step[1]) + i
                                dve.wait_ge(sc_ready, u * 8 + n + 1)
                                v.tensor_reduce(negm[:, n % 4:n % 4 + 1],
                                                psum[0:TT, 2 * i:2 * i + 2, :].rearrange("p a n -> p (a n)")[:, 0:MK],
                                                AX.X, ALU.max, negate=True).then_inc(mx_done, 1)
                        elif step[0] == "R":
                            for i in range(2):
                                n = 2 * int(step[1]) + i
                                dve.wait_ge(exp_done, u * 8 + (n + 1 + 2))
                                v.reciprocal(rinv[:, n % 4:n % 4 + 1], rsum[:, n % 4:n % 4 + 1]).then_inc(rinv_done, 1)
                        elif step[0] == "T":
                            h, c = int(step[1]), int(step[2])
                            rows = ROWS + (c == 2)
                            dve.wait_ge(at_hi, u * 16 + (4 * h + c + 1))
                            v.tensor_tensor(pl[0:rows, (3 * h + c) % 4, :], psum[0:rows, 4 + c % 2, 0:2 * S],
                                            f(ph[0:rows, (3 * h + c) % 4, :]), ALU.subtract).then_inc(at_done, 1)
                        elif step[0] == "A":
                            h = int(step[1])
                            dve.wait_ge(at_hi, u * 16 + (4 * h + 4))
                            if h % 2 == 0:
                                dve.wait_ge(ao_out[2 * par + h // 2], turn * 16 + 16)
                            v.tensor_tensor(ao[DH * (h % 2):DH * (h % 2 + 1), par, h // 2, :], psum[0:DH, 5, 0:S],
                                            tmp[:, h % 2, :], ALU.add).then_inc(at_done, 1)

                dve.sem_inc(c_lo, 4)
                dve.sem_inc(at_done, 2)
                dve.sem_inc(pj_lo, 2)
                for i in range(4):
                    dve.sem_inc(ao_out[i], 16)
                for step in ("K", "c0", "c1", "c2", "c3"):
                    split(step, -2, 1, 0)
                null = Chain(dve, null_own)
                null.n = 1
                dve.wait_ge(null_in, 48)
                null.wait()
                null.step(v.tensor_copy(nkh[:, :], nk[:, :]))
                for par in range(2):
                    null.step(v.tensor_copy(kt_[0:DH, par, :, M:MP], nk[0:DH, :].unsqueeze(1).broadcast_to([DH, HG, 2])))
                null.step(v.tensor_copy(nvr[:, :, 0:DH], nv[:, :].unsqueeze(1).broadcast_to([1, HG, DH])))
                null.wait()
                for par in range(2):
                    null.step(v.tensor_tensor(kt_[DH:P, par, :, M:MP],
                                              nk[DH:P, :].unsqueeze(1).broadcast_to([DH, HG, 2]),
                                              f(nkh[DH:P, :]).unsqueeze(1).broadcast_to([DH, HG, 2]), ALU.subtract))
                null.step(v.tensor_tensor(nvr[:, :, DH:2 * DH], nv[:, :].unsqueeze(1).broadcast_to([1, HG, DH]),
                                          f(nvr[:, :, 0:DH]), ALU.subtract))
                assert null.n == 8
                for step in ("V", "C4", "C5", "C6", "C7"):
                    split(step, -1, 1, 0)
                for i in range(NP):
                    project(-1, 1, i)
                    if i == 5:
                        for step in ("Q", "c0", "c1", "c2", "c3"):
                            split(step, -1, 1, 0)
                run(dve, unit)

            @block.tensor
            def _(pe):
                def project(u, i, wgroup):
                    kind, half, j = group(i)
                    pe.wait_ge(pj_lo, u * NP + (NP + i + 1))
                    if i % 5 == 0:
                        pe.wait_ge(c_lo, u * 8 + (8 + 4 * half + 4 + 4))
                    if i == 0 or i == 2:
                        pe.wait_ge(w_lo, wgroup * 2 + (1 if i == 0 else 2))
                    for kt in range(KC):
                        first, last = kt == 0, kt == KC - 1
                        if kind == "k":
                            c0, c1 = (0, HW) if half == 0 else (HW - LO, HW)
                            cols = slice(P * j, P * (j + 1))
                            ins = three(nc, psum[:, 6 + i % 2, 0:c1 - c0], wh[:, 0, kt, cols], wl[:, 0, kt, cols],
                                        ch[:, half, kt, c0:c1], cl[:, half, kt, c0:c1], first, last)
                        else:
                            c0 = ROWS * j - half * LO
                            ins = three(nc, psum[0:ROWS, 6 + i % 2, 0:GW],
                                        ch[:, half, kt, c0:c0 + ROWS], cl[:, half, kt, c0:c0 + ROWS],
                                        wh[:, 1, kt, :], wl[:, 1, kt, :], first, last)
                    ins.then_inc(pj_ready, 1)

                def unit(u, par, turn, here, next1, next2, kind):
                    for step in turn_steps(**kind):
                        if step[0] == "G":
                            project(u, int(step[1]), next1[0])
                        elif step[0] == "S":
                            h = int(step[1])
                            if h == 0:
                                pe.wait_ge(q_lo, u + 1)
                                pe.wait_ge(pj_lo, u * NP + (7 + 2))
                            for i in range(2):
                                pe.wait_ge(exp_done, u * 8 + (2 * h + i + 1))
                                cols = slice(TT * i, TT * (i + 1))
                                for b, c1 in ((0, BK), (1, MP)):
                                    out = psum[0:TT, 2 * i + b, 0:c1 - BK * b]
                                    nc.tensor.matmul(out, qh[:, par, h, cols], kt_[:, par, h, BK * b:c1],
                                                     start=True, stop=False)
                                    ins = nc.tensor.matmul(out, ql[:, par, h, cols], kt_[:, par, h, BK * b:c1],
                                                           start=False, stop=True)
                                ins.then_inc(sc_ready, 1)
                        elif step[0] == "T":
                            h, c = int(step[1]), int(step[2])
                            rows = ROWS + (c == 2)
                            if c == 0:
                                pe.wait_ge(norm_done, u * 8 + (2 * h + 2))
                            pe.wait_ge(at_done, u * 16 + (4 * h + c + 1))
                            for t in (0, 1):
                                for i in range(2):
                                    at = S * t + TT * i
                                    r0 = ROWS * (2 * c + t)
                                    ins = nc.tensor.transpose(psum[0:rows, 4 + c % 2, at:at + TT],
                                                              p[:, (2 * h + i) % 4, r0:r0 + rows], ident[0:TT, 0:TT])
                            ins.then_inc(at_ready, 1)
                        elif step[0] == "A":
                            h = int(step[1])
                            if h == 0:
                                pe.wait_ge(pj_lo, u * NP + (NP + 2))
                            pe.wait_ge(at_done, u * 16 + (4 * h + 3 + 2))
                            for t in range(6):
                                rows = ROWS + (t == 5)
                                slot = (3 * h + t // 2) % 4
                                cols = slice(S * (t % 2), S * (t % 2 + 1))
                                nc.tensor.matmul(psum[:, 5, 0:S], v_[0:rows, par, t, h, :], ph[0:rows, slot, cols],
                                                 start=t == 0, stop=False)
                                ins = nc.tensor.matmul(psum[:, 5, 0:S], v_[0:rows, par, t, h, :], pl[0:rows, slot, cols],
                                                       start=False, stop=t == 5)
                            ins.then_inc(at_ready, 1)

                pe.wait_ge(null_own, 8)
                pe.wait_ge(null_row, 32)
                for i in range(NP):
                    project(-1, i, 0)
                run(pe, unit)


def phase_attention_out(nc, psum, ident, tg, ymax, d):
    KI = INNER // P
    NE = NC * NT
    with Mem(nc, "p5") as m:
        wland = m.sb("wland", [P, KI, D])
        wh, wl = m.sb("wh", [P, KI, D], F32R), m.sb("wl", [P, KI, D], F32R)
        aland = m.sb("aland", [P, KI, CH])
        ah, al = m.sb("ah", [P, 2, KI, CH], F32R), m.sb("al", [P, 2, KI, CH], F32R)
        scale_b, bias_b = m.sb("scale_b", [TT, D]), m.sb("bias_b", [TT, D])
        xt = m.sb("xt", [TT, 2, NT, D])
        z, y = m.sb("z", [TT, 2, D]), m.sb("y", [TT, 2, D])
        st1, st2 = m.sb("st1", [TT, 2, 6]), m.sb("st2", [TT, 2, 6])
        mv1, mv2 = m.sb("mv1", [TT, 2, 2]), m.sb("mv2", [TT, 2, 2])
        rs1, rs2 = m.sb("rs1", [TT, 2, 2]), m.sb("rs2", [TT, 2, 2])
        nhalf = m.sb("nhalf", [TT, 1])
        stage = m.sb("stage", [P, 2, KD, CH])
        s = m.sem
        const_in, w_in, w_hi, w_lo, ln_ready = s("const_in"), s("w_in"), s("w_hi"), s("w_lo"), s("ln_ready")
        a_in, a_hi, a_lo, x_in, x_out, y_out = s("a_in"), s("a_hi"), s("a_lo"), [s("x_in0"), s("x_in1")], s("x_out"), s("y_out")
        dve_own, pool_own, nhalf_ready, x_biased = s("dve_own"), s("pool_own"), s("nhalf_ready"), s("x_biased")
        out_ready, mv1_ready, rs1_ready, z_ready = s("out_ready"), s("mv1_ready"), s("rs1_ready"), s("z_ready")
        x_new, mv2_ready, rs2_ready, y_ready, max_done = (
            s("x_new"), s("mv2_ready"), s("rs2_ready"), s("y_ready"), s("max_done"))
        tr_ready, tr_read = s("tr_ready"), s("tr_read")

        def piece(c, j):
            return c * NT + j

        with nc.Block() as block:
            @block.sync
            def _(sp):
                def load(c):
                    sp.dma_start(xt[:, c % 2], d["x2"][CH * c:CH * (c + 1), :].rearrange("(n p) d -> p n d", p=TT)
                                 ).then_inc(x_in[c % 2], 16)
                sp.dma_start(wland[:, :, :], d["wout"].rearrange("(k p) n -> p k n", p=P)).then_inc(w_in, 16)
                sp.dma_start(scale_b[:, :], d["ln_scale"].partition_broadcast(TT)).then_inc(const_in, 16)
                sp.dma_start(bias_b[:, :], d["ln_bias"].partition_broadcast(TT)).then_inc(const_in, 16)
                load(0)
                load(1)
                for c in range(-1, NC + 1):
                    if c + 1 < NC:
                        if c >= 0:
                            sp.wait_ge(a_lo, piece(c + 1, 0))
                        sp.dma_start(aland[:, :, :],
                                     d["aT"][:, CH * (c + 1):CH * (c + 2)].rearrange("(k p) t -> p k t", p=P)
                                     ).then_inc(a_in, 16)
                    if c >= 1:
                        k = c - 1
                        sp.wait_ge(x_new, NT * (k + 1))
                        sp.dma_start(d["x3"][CH * k:CH * (k + 1), :].rearrange("(n p) d -> p n d", p=TT), xt[:, k % 2]
                                     ).then_inc(x_out, 16)
                        sp.wait_ge(tr_read, NT * (k + 1))
                        sp.dma_start(d["yT"][:, CH * k:CH * (k + 1)].rearrange("(k p) t -> p k t", p=P), stage[:, k % 2]
                                     ).then_inc(y_out, 16)
                        if k + 2 < NC:
                            sp.wait_ge(x_out, 16 * (k + 1))
                            sp.wait_ge(y_ready, NT * (k + 1))
                            load(k + 2)
                sp.wait_ge(x_out, 16 * NC)
                sp.wait_ge(y_out, 16 * NC)

            @block.gpsimd
            def _(pool):
                own = Chain(pool, pool_own)
                nc.gpsimd.memset(nhalf[:, :], -0.5).then_inc(nhalf_ready, 1)
                pool.wait_ge(nhalf_ready, 1)

                def moments(mv, rs, e, eps, done):
                    i = e % 2
                    own.step(nc.gpsimd.tensor_scalar(rs[:, i, 0:1], mv[:, i, 1:2], eps, 1.0, ALU.add, ALU.mult))
                    own.wait()
                    own.step(nc.gpsimd.tensor_tensor(rs[:, i, 0:1], rs[:, i, 0:1], nhalf[:, :], ALU.pow))
                    own.wait()
                    own.step(nc.gpsimd.tensor_tensor(rs[:, i, 1:2], mv[:, i, 0:1], rs[:, i, 0:1], ALU.mult))
                    own.wait()
                    nc.gpsimd.tensor_scalar(rs[:, i, 1:2], rs[:, i, 1:2], -1.0, 1.0, ALU.mult, ALU.mult).then_inc(done, 1)

                def bias(c):
                    pool.wait_ge(x_in[c % 2], 16 * (c // 2 + 1))
                    for n in range(NT):
                        nc.gpsimd.tensor_tensor(xt[:, c % 2, n, :], xt[:, c % 2, n, :], bias_b[:, :], ALU.add
                                                ).then_inc(x_biased, 1)

                pool.wait_ge(ln_ready, 2)
                bias(0)
                for e in range(NE + 1):
                    if e < NE:
                        pool.wait_ge(mv1_ready, e + 1)
                        moments(mv1, rs1, e, 1e-6, rs1_ready)
                    if e >= 1:
                        pool.wait_ge(mv2_ready, e)
                        moments(mv2, rs2, e - 1, 1e-5, rs2_ready)
                    if e % NT == 2 and e // NT + 1 < NC:
                        bias(e // NT + 1)

            @block.scalar
            def _(act):
                def split(c, j):
                    cols = slice(2 * j, 2 * j + 2)
                    act.wait_ge(a_in, 16 * (c + 1))
                    if c >= 2:
                        act.wait_ge(out_ready, NT * (c - 1))
                    nc.scalar.activation(ah[:, c % 2, cols, :], aland[:, cols, :], ACT.Copy).then_inc(a_hi, 1)

                act.wait_ge(w_in, 16)
                nc.scalar.activation(wh[:, :, :], wland[:, :, :], ACT.Copy).then_inc(w_hi, 1)
                for j in range(NT):
                    split(0, j)
                for e in range(NE + 2):
                    c, n = divmod(e, NT)
                    if e < NE:
                        act.wait_ge(rs1_ready, e + 1)
                        if e >= 2:
                            act.wait_ge(x_new, e - 1)
                        nc.scalar.activation(z[:, e % 2, :], psum[0:TT, e % 4, :], ACT.Identity,
                                             bias=rs1[:, e % 2, 1:2], scale=rs1[:, e % 2, 0:1]).then_inc(z_ready, 1)
                        if c + 1 < NC:
                            split(c + 1, n)
                    if 1 <= e <= NE:
                        k = e - 1
                        act.wait_ge(rs2_ready, k + 1)
                        if k >= 2:
                            act.wait_ge(max_done, k - 1)
                            act.wait_ge(tr_ready, k - 1)
                        nc.scalar.activation(y[:, k % 2, :], xt[:, (k // NT) % 2, k % NT, :], ACT.Identity,
                                             bias=rs2[:, k % 2, 1:2], scale=rs2[:, k % 2, 0:1]).then_inc(y_ready, 1)
                    if e >= 2:
                        k = e - 2
                        act.wait_ge(tr_ready, k + 1)
                        if k % NT == 0 and k // NT >= 2:
                            act.wait_ge(y_out, 16 * (k // NT - 1))
                        nc.scalar.activation(stage[:, (k // NT) % 2, :, TT * (k % NT):TT * (k % NT + 1)],
                                             psum[:, 4 + k % 2, 0:KD * TT].rearrange("p (k t) -> p k t", k=KD),
                                             ACT.Copy).then_inc(tr_read, 1)

            @block.vector
            def _(dve):
                v = nc.vector
                own = Chain(dve, dve_own)

                def split(c, j):
                    cols = slice(2 * j, 2 * j + 2)
                    dve.wait_ge(a_hi, piece(c, j) + 1)
                    v.tensor_tensor(al[:, c % 2, cols, :], aland[:, cols, :], f(ah[:, c % 2, cols, :]), ALU.subtract
                                    ).then_inc(a_lo, 1)

                own.step(v.memset(ymax[:, :], 0.0))
                own.wait()
                dve.wait_ge(const_in, 32)
                for tile in (scale_b, bias_b):
                    v.tensor_scalar(tile[:, :], tile[:, :], tg[0:TT, 1:2], None, ALU.mult).then_inc(ln_ready, 1)
                dve.wait_ge(ln_ready, 2)
                dve.wait_ge(w_hi, 1)
                v.tensor_tensor(wl[:, :, :], wland[:, :, :], f(wh[:, :, :]), ALU.subtract).then_inc(w_lo, 1)
                for j in range(NT):
                    split(0, j)
                for e in range(NE + 2):
                    c, n = divmod(e, NT)
                    if e < NE:
                        dve.wait_ge(out_ready, e + 1)
                        own.step(v.bn_stats(st1[:, e % 2, :], psum[0:TT, e % 4, :]))
                        own.wait()
                        if e >= 2:
                            dve.wait_ge(rs1_ready, e - 1)
                        v.bn_aggr(mv1[:, e % 2, :], st1[:, e % 2, :]).then_inc(mv1_ready, 1)
                        if c + 1 < NC:
                            split(c + 1, n)
                    if 1 <= e <= NE:
                        k = e - 1
                        rows = xt[:, (k // NT) % 2, k % NT, :]
                        dve.wait_ge(z_ready, k + 1)
                        dve.wait_ge(x_biased, k + 1)
                        own.step(v.tensor_tensor(z[:, k % 2, :], z[:, k % 2, :], scale_b[:, :], ALU.mult))
                        own.wait()
                        v.tensor_tensor(rows, rows, z[:, k % 2, :], ALU.add).then_inc(x_new, 1)
                        dve.wait_ge(x_new, k + 1)
                        own.step(v.bn_stats(st2[:, k % 2, :], rows))
                        own.wait()
                        v.bn_aggr(mv2[:, k % 2, :], st2[:, k % 2, :]).then_inc(mv2_ready, 1)
                    if e >= 2:
                        k = e - 2
                        dve.wait_ge(y_ready, k + 1)
                        v.tensor_reduce(ymax[0:TT, k:k + 1], y[:, k % 2, :], AX.X, ALU.max, apply_absolute_value=True
                                        ).then_inc(max_done, 1)

            @block.tensor
            def _(pe):
                pe.wait_ge(w_lo, 1)
                for e in range(NE + 2):
                    c, n = divmod(e, NT)
                    if e < NE:
                        pe.wait_ge(a_lo, piece(c, NT))
                        if e >= 4:
                            pe.wait_ge(z_ready, e - 3)
                        for kt in range(KI):
                            cols = slice(TT * n, TT * (n + 1))
                            ins = three(nc, psum[0:TT, e % 4, :], ah[:, c % 2, kt, cols], al[:, c % 2, kt, cols],
                                        wh[:, kt, :], wl[:, kt, :], kt == 0, kt == KI - 1)
                        ins.then_inc(out_ready, 1)
                    if e >= 2:
                        k = e - 2
                        pe.wait_ge(y_ready, k + 1)
                        if k >= 2:
                            pe.wait_ge(tr_read, k - 1)
                        for kt in range(KD):
                            ins = nc.tensor.transpose(psum[:, 4 + k % 2, TT * kt:TT * (kt + 1)],
                                                      y[:, k % 2, P * kt:P * (kt + 1)], ident[0:TT, 0:TT])
                        ins.then_inc(tr_ready, 1)


def overall_scale(nc, m, name, maxima, scale, inverse):
    top, all_top, steps, reduced = m.sb(f"{name}_top", [P, 1]), m.sb(f"{name}_all", [P, 1]), m.sem(f"{name}_steps"), m.sem(f"{name}_red")

    def on_pool(pool):
        pool.wait_ge(steps, 1)
        nc.gpsimd.partition_all_reduce(all_top[:, :], top[:, :], P, RMAX).then_inc(reduced, 1)

    def on_vector(dve):
        v = nc.vector
        v.tensor_reduce(top[:, :], maxima, AX.X, ALU.max).then_inc(steps, 1)
        dve.wait_ge(reduced, 1)
        v.tensor_scalar(scale, all_top[:, :], float(np.float32(1.0) / np.float32(QMAX)), 1e-12, ALU.mult, ALU.max
                        ).then_inc(steps, 1)
        dve.wait_ge(steps, 2)
        v.reciprocal(inverse, scale).then_inc(steps, 1)

    return on_pool, on_vector, steps


def phase_project_quantised(nc, psum, g_, d, up, ymax, gmax, umax, g2max, gscale):
    with Mem(nc, "p6b" if up else "p6a") as m:
        land = m.sb("land", [P, 2, FF1])
        wh, wl = m.sb("wh", [P, KD, FF1], F32R), m.sb("wl", [P, KD, FF1], F32R)
        yland = m.sb("yland", [P, 2, KD, CH])
        yh, yl = m.sb("yh", [P, 2, KD, CH], F32R), m.sb("yl", [P, 2, KD, CH], F32R)
        sy, iy = m.sb("sy", [P, 1]), m.sb("iy", [P, 1])
        s = m.sem
        w_in, w_hi, w_lo = [s("w_in0"), s("w_in1")], s("w_hi"), s("w_lo")
        y_in, y_own, y_whole, y_hi, y_lo = [s("y_in0"), s("y_in1")], s("y_own"), s("y_whole"), s("y_hi"), s("y_lo")
        o_ready, o_read, o_max = s("o_ready"), s("o_read"), s("o_max")
        y_pool, y_vector, y_steps = overall_scale(nc, m, "y", ymax[:, :], sy[:, :], iy[:, :])
        RB = 8
        if up:
            RS = 4
            GT = 3
            stage = m.sb("stage", [P, RS, CH])
            sig = m.sb("sig", [P, T])
            hold = m.sb("hold", [P, 1])
            s_out = [s(f"s_out{i}") for i in range(RS)]
            g_own, g_whole, sig_ready, sig_own, sig_whole, sig_used = (
                s("g_own"), s("g_whole"), s("sig_ready"), s("sig_own"), s("sig_whole"), s("sig_used"))
            sg, ig = gscale
            g_pool, g_vector, g_steps = overall_scale(nc, m, "g", gmax[:, :], sg, ig)
        w0 = KD if up else 0

        with nc.Block() as block:
            @block.sync
            def _(sp):
                def load(k):
                    c = k % NC
                    sp.dma_start(yland[:, k % 2], d["yT"][:, CH * c:CH * (c + 1)].rearrange("(k p) t -> p k t", p=P)
                                 ).then_inc(y_in[k % 2], 16)
                load(0)
                for j in range(KD):
                    if j >= 2:
                        sp.wait_ge(w_lo, j - 1)
                    sp.dma_start(land[:, j % 2], d["wdq"][w0 + j]).then_inc(w_in[j % 2], 16)
                load(1)
                for k in range(NC):
                    if up:
                        for it in range(NI1):
                            e = k * NI1 + it
                            sp.wait_ge(o_read, e + 1 + RB)
                            sp.dma_start(d["upT"][P * it:P * (it + 1), CH * k:CH * (k + 1)], stage[:, e % RS, :]
                                         ).then_inc(s_out[e % RS], 16)
                            if it == 0 and k + 2 <= NC:
                                sp.wait_ge(y_lo, k + 1)
                                load(k + 2)
                    elif k + 2 <= NC:
                        sp.wait_ge(y_lo, k + 1)
                        load(k + 2)
                if up:
                    for i in range(RS):
                        sp.wait_ge(s_out[i], 16 + 16 * NC * NI1 // RS)

            @block.gpsimd
            def _(pool):
                y_pool(pool)
                if up:
                    g_pool(pool)
                    own = Chain(pool, sig_own)
                    for t in range(NI1):
                        pool.wait_ge(sig_ready, t + 1)
                        own.step(nc.gpsimd.tensor_scalar(sig[:, :], sig[:, :], 65536.0, MAGIC, ALU.mult, ALU.add))
                        own.wait()
                        own.step(nc.gpsimd.tensor_scalar(sig[:, :], sig[:, :], -MAGIC, 1.0, ALU.add, ALU.mult))
                        own.wait()
                        nc.gpsimd.tensor_scalar(sig[:, :], sig[:, :], 65535.0, 0.0, ALU.min, ALU.max
                                                ).then_inc(sig_whole, 1)

            @block.scalar
            def _(act):
                def hi(k, par):
                    act.wait_ge(y_whole, k + 1)
                    nc.scalar.activation(yh[:, par], yland[:, par], ACT.Copy).then_inc(y_hi, 1)

                for j in range(KD):
                    act.wait_ge(w_in[j % 2], 16 * (j // 2 + 1))
                    nc.scalar.activation(wh[:, j, :], land[:, j % 2, :], ACT.Copy).then_inc(w_hi, 1)
                hi(0, 0)
                act.sem_inc(o_read, RB)
                if up:
                    for i in range(RS):
                        act.sem_inc(s_out[i], 16)
                with act.Fori(0, NC // 2) as i:
                    for par in (0, 1):
                        c = i * 2 + par
                        for it in range(NI1):
                            act.wait_ge(o_ready, c * NI1 + it + 1)
                            if up:
                                act.wait_ge(s_out[it % RS], c * (16 * NI1 // RS) + (16 * (it // RS) + 16))
                                act.wait_ge(o_max, c * NI1 + it + 1)
                                out = stage[:, it % RS, :]
                            else:
                                out = g_[:, it, bass.ds(c * CH, CH)]
                            nc.scalar.activation(out, psum[:, (it + 4 * par) % RB, 0:CH], ACT.Identity, scale=sy[:, :]
                                                 ).then_inc(o_read, 1)
                            if it == 6:
                                hi(c + 1, 1 - par)
                            if up and it % 4 == 2:
                                r = it // 4
                                act.wait_ge(g_whole, c * GT + r + 1)
                                act.wait_ge(sig_used, c * GT + r + 1)
                                nc.scalar.activation(sig[:, :], g_[:, bass.ds(c * GT + r, 1), :].rearrange("p a t -> p (a t)"),
                                                     ACT.Sigmoid).then_inc(sig_ready, 1)

            @block.vector
            def _(dve):
                v = nc.vector
                own = Chain(dve, y_own, 8 if up else 2)

                def whole(k, par, turn):
                    dve.wait_ge(y_in[par], turn * 16 + 16)
                    own.step(v.tensor_scalar(yland[:, par], yland[:, par], iy[:, :], QMAX, ALU.mult, ALU.min))
                    own.wait()
                    own.step(v.tensor_scalar(yland[:, par], yland[:, par], -QMAX - 1, MAGIC, ALU.max, ALU.add))
                    own.wait()
                    v.tensor_scalar(yland[:, par], yland[:, par], -MAGIC, None, ALU.add).then_inc(y_whole, 1)

                def lo(k, par):
                    dve.wait_ge(y_hi, k + 1)
                    v.tensor_tensor(yl[:, par], yland[:, par], f(yh[:, par]), ALU.subtract).then_inc(y_lo, 1)

                def gate_tile(c, r):
                    return g_[:, bass.ds(c * GT + r, 1), :].rearrange("p a t -> p (a t)")

                def gate_whole(c, r):
                    g = gate_tile(c, r)
                    own.step(v.tensor_scalar(g, g, ig, QMAX, ALU.mult, ALU.min))
                    own.wait()
                    own.step(v.tensor_scalar(g, g, -QMAX - 1, MAGIC, ALU.max, ALU.add))
                    own.wait()
                    v.tensor_scalar(g, g, -MAGIC, sg, ALU.add, ALU.mult).then_inc(g_whole, 1)

                def gate_silu(c, r):
                    g = gate_tile(c, r)
                    dve.wait_ge(g_whole, c * GT + r + 1)
                    dve.wait_ge(sig_whole, c * GT + r + 1)
                    v.scalar_tensor_tensor(out=g, in0=sig[:, :], scalar=2.0 ** -16, in1=g, op0=ALU.mult, op1=ALU.mult
                                           ).then_inc(sig_used, 1)
                    dve.wait_ge(sig_used, c * GT + (r + 1 + 1))
                    v.tensor_reduce(g2max[:, bass.ds(c * GT + r, 1)], g, AX.X, ALU.max, apply_absolute_value=True)

                y_vector(dve)
                dve.wait_ge(y_steps, 3)
                if up:
                    g_vector(dve)
                    dve.wait_ge(g_steps, 3)
                    dve.sem_inc(o_max, RS)
                    dve.sem_inc(sig_used, 1)
                own.per, first = 0, own.per
                whole(0, 0, 0)
                skew = own.n
                for j in range(KD):
                    dve.wait_ge(w_hi, j + 1)
                    v.tensor_tensor(wl[:, j, :], land[:, j % 2, :], f(wh[:, j, :]), ALU.subtract).then_inc(w_lo, 1)
                lo(0, 0)
                own.per = first
                with dve.Fori(0, NC // 2) as i:
                    for par in (0, 1):
                        c = i * 2 + par
                        own.at(c)
                        own.base = own.base + skew
                        whole(c + 1, 1 - par, i + par)
                        for it in range(NI1):
                            dve.wait_ge(o_read, c * NI1 + (it + 1 + RB))
                            src = stage[:, it % RS, :] if up else g_[:, it, bass.ds(c * CH, CH)]
                            top = umax if up else gmax
                            v.tensor_reduce(top[:, bass.ds(c * NI1 + it, 1)], src, AX.X, ALU.max,
                                            apply_absolute_value=True).then_inc(o_max, 1)
                            if it == 8:
                                lo(c + 1, 1 - par)
                            if up and it % 4 == 0 and it:
                                gate_silu(c, it // 4 - 1)
                            if up and it % 4 == 0:
                                gate_whole(c, it // 4)
                        if up:
                            gate_silu(c, GT - 1)
                        own.done()

            @block.tensor
            def _(pe):
                pe.wait_ge(w_lo, KD)
                with pe.Fori(0, NC // 2) as i:
                    for par in (0, 1):
                        c = i * 2 + par
                        pe.wait_ge(y_lo, c + 1)
                        for it in range(NI1):
                            pe.wait_ge(o_read, c * NI1 + it + 1)
                            cols = slice(P * it, P * (it + 1))
                            for kt in range(KD):
                                ins = three(nc, psum[:, (it + 4 * par) % RB, 0:CH], wh[:, kt, cols], wl[:, kt, cols],
                                            yh[:, par, kt, :], yl[:, par, kt, :], kt == 0, kt == KD - 1)
                            ins.then_inc(o_ready, 1)


def phase_mix_down(nc, psum, g_, tg, d, umax, g2max):
    with Mem(nc, "p6c") as m:
        land = m.sb("land", [P, FF1])
        wh, wl = m.sb("wh", [P, NI1, D], F32R), m.sb("wl", [P, NI1, D], F32R)
        u = m.sb("u", [P, 2, T])
        ohi, olo = m.sb("ohi", [P, 2, NI1, TT], F32R), m.sb("olo", [P, 2, NI1, TT], F32R)
        ow = m.sb("ow", [P, NI1, TT])
        xt = m.sb("xt", [TT, 2, NT, D])
        fin = m.sb("fin", [TT, 2, D])
        omax = m.sb("omax", [P, NI1])
        su, iu, s2, i2, so, io, su2, tgo = (m.sb(n, [P, 1]) for n in ("su", "iu", "s2", "i2", "so", "io", "su2", "tgo"))
        s = m.sem
        w_in, w_hi, w_lo, u_in = s("w_in"), s("w_hi"), s("w_lo"), [s("u_in0"), s("u_in1")]
        scales, g_scaled, u_scaled, g_own, u_whole, g_whole = (
            s("scales"), s("g_scaled"), s("u_scaled"), s("g_own"), s("u_whole"), s("g_whole"))
        u_clip, mixed, measured, tgo_ready = s("u_clip"), s("mixed"), s("measured"), s("tgo_ready")
        x_in, x_out = [s("x_in0"), s("x_in1")], s("x_out")
        o_own, o_split = s("o_own"), s("o_split")
        out_ready, fin_done, x_new = s("out_ready"), s("fin_done"), s("x_new")
        u_pool, u_vector, u_steps = overall_scale(nc, m, "um", umax[:, :], su[:, :], iu[:, :])
        g_pool, g_vector, g_steps = overall_scale(nc, m, "gm", g2max[:, :], s2[:, :], i2[:, :])
        o_pool, o_vector, o_steps = overall_scale(nc, m, "om", omax[:, :], so[:, :], io[:, :])
        WS = NI1 // 3

        with nc.Block() as block:
            @block.sync
            def _(sp):
                def load_x(c):
                    sp.dma_start(xt[:, c % 2], d["x3"][CH * c:CH * (c + 1), :].rearrange("(n p) d -> p n d", p=TT)
                                 ).then_inc(x_in[c % 2], 16)
                for t in range(NI1):
                    if t >= 2:
                        sp.wait_ge(mixed, t - 1)
                    sp.dma_start(u[:, t % 2, :], d["upT"][P * t:P * (t + 1), :]).then_inc(u_in[t % 2], 16)
                    if t < WS:
                        if t:
                            sp.wait_ge(w_lo, t)
                        sp.dma_start(land[:, :], d["wdq"][2 * KD + t]).then_inc(w_in, 16)
                load_x(0)
                load_x(1)
                for c in range(NC):
                    sp.wait_ge(x_new, NT * (c + 1) + 2)
                    sp.dma_start(d["out"][CH * c:CH * (c + 1), :].rearrange("(n p) d -> p n d", p=TT), xt[:, c % 2]
                                 ).then_inc(x_out, 16)
                    if c + 2 < NC:
                        sp.wait_ge(x_out, 16 * (c + 1))
                        load_x(c + 2)
                sp.wait_ge(x_out, 16 * NC)

            @block.gpsimd
            def _(pool):
                u_pool(pool)
                g_pool(pool)
                own = Chain(pool, g_own)
                for t in range(NI1):
                    g = g_[:, t, :]
                    pool.wait_ge(g_scaled, t + 1)
                    own.step(nc.gpsimd.tensor_scalar(g, g, -MAGIC, 1.0, ALU.add, ALU.mult))
                    pool.wait_ge(u_scaled, t + 1)
                    nc.gpsimd.tensor_scalar(u[:, t % 2, :], u[:, t % 2, :], -MAGIC, 1.0, ALU.add, ALU.mult
                                            ).then_inc(u_whole, 1)
                    own.wait()
                    nc.gpsimd.tensor_scalar(g, g, QMAX, -QMAX - 1, ALU.min, ALU.max).then_inc(g_whole, 1)
                o_pool(pool)
                pool.sem_inc(x_new, 2)
                with pool.Fori(0, NC // 2) as i:
                    for par in (0, 1):
                        c = i * 2 + par
                        pool.wait_ge(x_in[par], i * 16 + 16)
                        for n in range(NT):
                            pool.wait_ge(fin_done, c * NT + (n + 1 + 4))
                            nc.gpsimd.tensor_tensor(xt[:, par, n, :], xt[:, par, n, :], fin[:, n % 2, :], ALU.add
                                                    ).then_inc(x_new, 1)

            @block.scalar
            def _(act):
                act.wait_ge(scales, 1)
                for t in range(NI1):
                    nc.scalar.activation(g_[:, t, :], g_[:, t, :], ACT.Copy, bias=MAGIC, scale=i2[:, :]).then_inc(g_scaled, 1)
                    act.wait_ge(u_in[t % 2], 16 * (t // 2 + 1))
                    nc.scalar.activation(u[:, t % 2, :], u[:, t % 2, :], ACT.Copy, bias=MAGIC, scale=iu[:, :]
                                         ).then_inc(u_scaled, 1)
                    if t < WS:
                        act.wait_ge(w_in, 16 * (t + 1))
                        nc.scalar.activation(wh[:, 3 * t:3 * t + 3, :].rearrange("p k n -> p (k n)"), land[:, :], ACT.Copy
                                             ).then_inc(w_hi, 1)
                act.sem_inc(fin_done, 4)
                act.wait_ge(tgo_ready, 1)
                with act.Fori(0, NC // 2) as i:
                    for par in (0, 1):
                        c = i * 2 + par
                        for n in range(NT):
                            act.wait_ge(out_ready, c * NT + (n + 1 + 2))
                            act.wait_ge(x_new, c * NT + n + 1)
                            nc.scalar.activation(fin[:, n % 2, :], psum[0:TT, n, :], ACT.Identity, scale=tgo[0:TT, :]
                                                 ).then_inc(fin_done, 1)

            @block.vector
            def _(dve):
                v = nc.vector
                u_vector(dve)
                g_vector(dve)
                dve.wait_ge(u_steps, 3)
                dve.wait_ge(g_steps, 3)
                v.tensor_tensor(su2[:, :], su[:, :], s2[:, :], ALU.mult).then_inc(scales, 1)
                dve.wait_ge(scales, 1)
                for t in range(NI1):
                    if t < WS:
                        dve.wait_ge(w_hi, t + 1)
                        v.tensor_tensor(wl[:, 3 * t:3 * t + 3, :].rearrange("p k n -> p (k n)"), land[:, :],
                                        f(wh[:, 3 * t:3 * t + 3, :]).rearrange("p k n -> p (k n)"), ALU.subtract
                                        ).then_inc(w_lo, 1)
                    ut = u[:, t % 2, :]
                    dve.wait_ge(u_whole, t + 1)
                    v.tensor_scalar(ut, ut, QMAX, -QMAX - 1, ALU.min, ALU.max).then_inc(u_clip, 1)
                    dve.wait_ge(u_clip, t + 1)
                    dve.wait_ge(g_whole, t + 1)
                    v.scalar_tensor_tensor(out=g_[:, t, :], in0=ut, scalar=su2[:, :], in1=g_[:, t, :],
                                           op0=ALU.mult, op1=ALU.mult).then_inc(mixed, 1)
                    dve.wait_ge(mixed, t + 1)
                    v.tensor_reduce(omax[:, t:t + 1], g_[:, t, :], AX.X, ALU.max, apply_absolute_value=True
                                    ).then_inc(measured, 1)
                dve.wait_ge(measured, NI1)
                o_vector(dve)
                dve.wait_ge(o_steps, 3)
                v.tensor_tensor(tgo[:, :], tg[:, 3:4], so[:, :], ALU.mult).then_inc(tgo_ready, 1)
                own = Chain(dve, o_own, 4 * NT)
                dve.sem_inc(out_ready, 2)
                with dve.Fori(0, NC // 2) as i:
                    for par in (0, 1):
                        c = i * 2 + par
                        own.at(c)
                        for n in range(NT):
                            own.step(v.tensor_scalar(ow[:, :, :], g_[:, :, bass.ds(c * CH + n * TT, TT)], io[:, :], QMAX,
                                                     ALU.mult, ALU.min))
                            own.wait()
                            own.step(v.tensor_scalar(ow[:, :, :], ow[:, :, :], -QMAX - 1, MAGIC, ALU.max, ALU.add))
                            own.wait()
                            own.step(v.tensor_scalar(ow[:, :, :], ow[:, :, :], -MAGIC, None, ALU.add))
                            own.wait()
                            dve.wait_ge(out_ready, c * NT + n + 1)
                            own.step(v.tensor_copy(ohi[:, n % 2], ow[:, :, :]))
                            own.wait()
                            v.tensor_tensor(olo[:, n % 2], ow[:, :, :], f(ohi[:, n % 2]), ALU.subtract
                                            ).then_inc(o_split, 1)
                            dve.wait_ge(o_split, c * NT + n + 1)
                        own.done()

            @block.tensor
            def _(pe):
                pe.wait_ge(w_lo, WS)
                with pe.Fori(0, NC // 2) as i:
                    for par in (0, 1):
                        c = i * 2 + par
                        for n in range(NT):
                            pe.wait_ge(o_split, c * NT + n + 1)
                            pe.wait_ge(fin_done, c * NT + n + 1)
                            for kt in range(NI1):
                                ins = three(nc, psum[0:TT, n, :], ohi[:, n % 2, kt, :], olo[:, n % 2, kt, :],
                                            wh[:, kt, :], wl[:, kt, :], kt == 0, kt == NI1 - 1)
                            ins.then_inc(out_ready, 1)


def phase_quantised_ffn(nc, psum, tg, ymax, d):
    with Mem(nc, "p6") as m:
        g_ = m.sb("gate", [P, NI1, T])
        gmax, umax, g2max = m.sb("gmax", [P, NC * NI1]), m.sb("umax", [P, NC * NI1]), m.sb("g2max", [P, NI1])
        sg, ig = m.sb("sg", [P, 1]), m.sb("ig", [P, 1])
        for up in (False, True):
            phase_project_quantised(nc, psum, g_, d, up, ymax, gmax, umax, g2max, (sg[:, :], ig[:, :]))
        phase_mix_down(nc, psum, g_, tg, d, umax, g2max)


def build(nc, d):
    with Mem(nc, "all") as m:
        psum = m.stack.enter_context(nc.psum_tensor("psum", [P, 8, 512], F32))
        ident = m.sb("ident", [P, P])
        tg = m.sb("tg", [P, 4])
        phase_depool(nc, psum, ident, tg, d)
        phase_relu_ffn(nc, psum, ident, tg, d)
        phase_queries(nc, psum, ident, tg, d)
        phase_attention(nc, psum, ident, d)
        ymax = m.sb("ymax", [P, NC * NT])
        phase_attention_out(nc, psum, ident, tg, ymax, d)
        phase_quantised_ffn(nc, psum, tg, ymax, d)


SCRATCH = {"x1": [T, D], "x2": [T, D], "qT": [INNER, T], "wdq": [3 * KD, P, FF1], "aT": [INNER, T],
           "x3": [T, D], "yT": [D, T], "upT": [FF1, T]}


def kernel(**a):
    import numpy as np
    import concourse.bacc as bacc
    from concourse import mybir as mb
    from concourse.bass_utils import run_bass_kernel_spmd as run

    def cols(v, n):
        return v.reshape(n, 128).T

    def blocks(w):
        o, i = w.shape
        return w.reshape(o // QB, QB, i // P, 4, QB).transpose(2, 3, 1, 0, 4).reshape(i // P, P, o)

    down = blocks(a["L1_ffn_w_down"])
    down = down.reshape(KD, 3, P, D).transpose(0, 2, 1, 3).reshape(KD, P, 3 * D)
    arrays = {
        "x": a["x"].reshape(T, D), "ctx": a["ctx_2048"], "ctx_t": a["ctx_2048"].transpose(0, 2, 1),
        "lens": a["mask_BxS2_if0"], "gates": np.concatenate([a["g_xattn"], a["g_ffn"]]),
        "w_in_t": a["L0_xattn_W_in"].T, "b_in": a["L0_xattn_b_in"],
        "g_res_cols": cols(a["L0_xattn_g_res"], KD), "g_init": a["L0_xattn_g_init"],
        "w1": a["L0_ffn_W1"], "b1_cols": cols(a["L0_ffn_b1"], NI0), "w2": a["L0_ffn_W2"], "b2": a["L0_ffn_b2"],
        "w_q": np.concatenate([blocks(a["L1_ffn_w_gate"]), blocks(a["L1_ffn_w_up"]), down]),
        "wq": a["L1_xattn_Wq"], "wkv": a["L1_xattn_Wkv"], "null_kv": a["L1_xattn_null_kv"], "wout": a["L1_xattn_Wout"],
        "ln_scale": a["L1_xattn_ln_scale"], "ln_bias": a["L1_xattn_ln_bias"],
    }
    nc = bacc.Bacc("TRN2", target_bir_lowering=False, num_devices=1)
    arrays = {k: np.ascontiguousarray(v) for k, v in arrays.items()}
    d = {k: nc.dram_tensor(f"in_{k}", v.shape, mb.dt.from_np(v.dtype), kind="ExternalInput").ap() for k, v in arrays.items()}
    for k, shape in SCRATCH.items():
        d[k] = nc.dram_tensor(f"scratch_{k}", shape, mb.dt.float32, kind="Internal").ap()
    d["out"] = nc.dram_tensor("out", [T, D], mb.dt.float32, kind="ExternalOutput").ap()
    build(nc, d)
    r = run(nc, [{f"in_{k}": v for k, v in arrays.items()}], core_ids=[0])
    return r.results[0]["out"].reshape(B, S, D)
```

```python
import numpy as np
import concourse.bass as bass
from concourse import mybir
from contextlib import ExitStack

F32 = mybir.dt.float32
F32R = mybir.dt.float32r
BF16 = mybir.dt.bfloat16
I32 = mybir.dt.int32
ALU = mybir.AluOpType
ACT = mybir.ActivationFunctionType
AX = mybir.AxisListType
RMAX = bass.bass_isa.ReduceOp.max

P = 128
B, S, D = 8, 224, 512
M, DC = 750, 1024
T = B * S
TT = 112
NT = 4
CH = NT * TT
NC = T // CH
KD = D // P
KC = DC // P
FF0 = 2048
NI0 = FF0 // P
FF1 = 1536
NI1 = FF1 // P
H, DH = 16, 64
INNER = H * DH
RU = KD
QB = 32
MAGIC = 1.5 * 2.0 ** 23
LOGP = np.float32(-0.001)
DT = float(np.float32(-np.log(-np.expm1(LOGP))))
BCOEF = float(np.exp(LOGP))
QMAX = 32767.0


class Chain:

    def __init__(self, eng, sem, per=0):
        self.eng, self.sem, self.per, self.base, self.n = eng, sem, per, 0, 0

    def at(self, turn):
        self.base, self.n = turn * self.per, 0

    def step(self, ins):
        self.n += 1
        return ins.then_inc(self.sem, 1)

    def wait(self):
        self.eng.wait_ge(self.sem, self.base + self.n)

    def done(self):
        assert self.n == self.per, (self.n, self.per)


class Mem:

    def __init__(self, nc, name):
        self.nc, self.name, self.stack, self.sems = nc, name, ExitStack(), []

    def __enter__(self):
        self.stack.__enter__()
        return self

    def __exit__(self, *a):
        if self.sems:
            self.nc.clear_and_free_semaphores(self.sems)
            self.nc.all_engine_barrier()
        return self.stack.__exit__(*a)

    def sb(self, name, shape, dtype=F32):
        return self.stack.enter_context(self.nc.sbuf_tensor(f"{self.name}_{name}", shape, dtype))

    def sem(self, name):
        self.sems.append(self.nc.alloc_semaphore(f"{self.name}_{name}"))
        return self.sems[-1]


def f(ap):
    return ap.bitcast(F32)


def hold(eng, held):
    eng.sem_inc(held, 1)


def three(nc, out, a_hi, a_lo, b_hi, b_lo, first, last):
    nc.tensor.matmul(out, a_hi, b_hi, start=first, stop=False)
    nc.tensor.matmul(out, a_hi, b_lo, start=False, stop=False)
    return nc.tensor.matmul(out, a_lo, b_hi, start=False, stop=last)


def phase_depool(nc, psum, ident, tg, d):
    with Mem(nc, "p1") as m:
        wland = m.sb("wland", [P, KD, D])
        wh, wl = m.sb("wh", [P, KD, D], F32R), m.sb("wl", [P, KD, D], F32R)
        bin_b, gin_b = m.sb("bin_b", [TT, D]), m.sb("gin_b", [TT, D])
        gres = m.sb("gres", [P, KD])
        graw = m.sb("graw", [P, 4])
        lens = m.sb("lens", [B, M], I32)
        lensf, zeros, cum = (m.sb(n, [B, M]) for n in ("lensf", "zeros", "cum"))
        wrap, idx = zeros, lensf
        JP, JC = 125, M // 125
        idxT = m.sb("idxT", [JP, JC, B])
        ti = m.sb("ti", [P, S], I32)
        tf = m.sb("tf", [P, S])
        si = m.sb("si", [P, 2], I32)
        scol = m.sb("scol", [P, 2])
        eq = m.sb("eq", [JP, JC, B, S], BF16)
        ones = m.sb("ones", [JP, P], BF16)
        mark, plug = m.sb("mark", [P, B, S]), m.sb("plug", [P, B, S])
        zrow = m.sb("zrow", [P, S])
        xt = m.sb("xt", [TT, 2, NT, D])
        ctxn = m.sb("ctxn", [TT, NT, DC])
        junk = m.sb("junk", [TT, DC], BF16)
        ssq, rsc = m.sb("ssq", [TT, NT]), m.sb("rsc", [TT, NT])
        uh, ul = m.sb("uh", [TT, 2, NT, D], F32R), m.sb("ul", [TT, 2, NT, D], F32R)
        u32 = m.sb("u32", [TT, D])
        dm, mk = m.sb("dm", [TT, 2, CH]), m.sb("mk", [TT, 2, CH])
        mh, ml = m.sb("mh", [TT, 2, 2, CH], F32R), m.sb("ml", [TT, 2, 2, CH], F32R)
        stats, mv = m.sb("stats", [TT, NT, 6]), m.sb("mv", [TT, NT, 2])
        ve, rs, rr = m.sb("ve", [TT, NT]), m.sb("rs", [TT, NT]), m.sb("rr", [TT, NT])
        nhalf, c_eps, c_dc, c_in = (m.sb(n, [TT, NT]) for n in ("nhalf", "c_eps", "c_dc", "c_in"))
        hold = m.sb("hold", [TT, 1])
        y = m.sb("y", [TT, NT, D])
        yh, yl = m.sb("yh", [P, 2, KD, CH], F32R), m.sb("yl", [P, 2, KD, CH], F32R)
        tmp = m.sb("tmp", [TT, D])

        s = m.sem
        const_in, lens_in, ctx_in, x_out = s("const_in"), s("lens_in"), s("ctx_in"), s("x_out")
        x_in = [s("x_in0"), s("x_in1")]
        pool_c, pool_own = s("pool_c"), s("pool_own")
        idx_ready, idx_t, eq_ready, count_ready = s("idx_ready"), s("idx_t"), s("eq_ready"), s("count_ready")
        dve_own, act_own, w_hi, w_ready = s("dve_own"), s("act_own"), s("w_hi"), s("w_ready")
        var_ready, rstd_ready, y_ready, tr_ready, tr_hi, tr_free = (
            s("var_ready"), s("rstd_ready"), s("y_ready"), s("tr_ready"), s("tr_hi"), s("tr_free"))
        ssq_ready, rsc_ready, u_ready, dm_ready, ex_ready, m_ready = (
            s("ssq_ready"), s("rsc_ready"), s("u_ready"), s("dm_ready"), s("ex_ready"), s("m_ready"))
        out_ready, out_free, x_new = s("out_ready"), s("out_free"), s("x_new")

        with nc.Block() as block:
            @block.sync
            def _(sp):
                sp.dma_start(lens[:, :], d["lens"]).then_inc(lens_in, 16)
                sp.dma_start(graw[:, :], d["gates"].partition_broadcast(P)).then_inc(const_in, 16)
                sp.dma_start(wland[:, :, :], d["w_in_t"].rearrange("(k p) n -> p k n", p=P)).then_inc(const_in, 16)
                sp.dma_start(bin_b[:, :], d["b_in"].partition_broadcast(TT)).then_inc(const_in, 16)
                sp.dma_start(gin_b[:, :], d["g_init"][0:D].partition_broadcast(TT)).then_inc(const_in, 16)
                sp.dma_start(gres[:, :], d["g_res_cols"]).then_inc(const_in, 16)
                for k in range(NC + 1):
                    c = k % NC
                    if k >= 2:
                        sp.wait_ge(x_new, NT * (k - 1))
                        sp.dma_start(d["x1"][CH * (k - 2):CH * (k - 1), :].rearrange("(n p) d -> p n d", p=TT),
                                     xt[:, k % 2]).then_inc(x_out, 16)
                        sp.wait_ge(x_out, 16 * (k - 1))
                    sp.dma_start(xt[:, k % 2], d["x"][CH * c:CH * (c + 1), :].rearrange("(n p) d -> p n d", p=TT)
                                 ).then_inc(x_in[k % 2], 16)
                    if k >= 1:
                        sp.wait_ge(u_ready, NT * k)
                        sp.wait_ge(ssq_ready, NT * k)
                    for b in range(2):
                        src = d["ctx"][2 * c + b, 0:S, :].rearrange("(n p) d -> p n d", p=TT)
                        sp.dma_start(ctxn[:, 2 * b:2 * b + 2, :], src).then_inc(ctx_in, 16)
                sp.wait_ge(x_new, NT * NC)
                sp.dma_start(d["x1"][CH * (NC - 1):T, :].rearrange("(n p) d -> p n d", p=TT), xt[:, (NC - 1) % 2]
                             ).then_inc(x_out, 16)
                sp.wait_ge(x_out, 16 * NC)

            @block.gpsimd
            def _(pool):
                own = Chain(pool, pool_own, 8)
                nc.gpsimd.memset(ident[:, :], 0.0).then_inc(pool_c, 1)
                pool.wait_ge(pool_c, 1)
                nc.gpsimd.affine_select(out=ident[:, :], in_=ident[:, :], compare_op=ALU.not_equal, fill=1.0,
                                        base=0, pattern=[[-1, P]], channel_multiplier=1).then_inc(pool_c, 1)
                for tile, value in ((nhalf, -0.5), (c_eps, 1e-5), (c_dc, 1.0 / DC), (c_in, BCOEF)):
                    nc.gpsimd.memset(tile[:, :], value).then_inc(pool_c, 1)
                nc.gpsimd.iota(ti[:, :], [[1, S]], 0, 0).then_inc(pool_c, 1)
                nc.gpsimd.iota(si[:, :], [[TT, 2]], 0, 1).then_inc(pool_c, 1)

                def prep(k):
                    own.at(k)
                    pool.wait_ge(var_ready, k + 1)
                    own.step(nc.gpsimd.tensor_tensor(rs[:, :], ve[:, :], nhalf[:, :], ALU.pow))
                    own.wait()
                    own.step(nc.gpsimd.tensor_tensor(rr[:, :], rs[:, :], rs[:, :], ALU.mult))
                    own.wait()
                    own.step(nc.gpsimd.tensor_tensor(rr[:, :], rr[:, :], mv[:, :, 1], ALU.mult))
                    own.wait()
                    own.step(nc.gpsimd.tensor_tensor(rr[:, :], rr[:, :], c_eps[:, :], ALU.add))
                    own.wait()
                    own.step(nc.gpsimd.tensor_tensor(rr[:, :], rr[:, :], nhalf[:, :], ALU.pow))
                    own.wait()
                    nc.gpsimd.tensor_tensor(rs[:, :], rs[:, :], rr[:, :], ALU.mult).then_inc(rstd_ready, 1)
                    pool.wait_ge(ssq_ready, NT * k + NT)
                    own.step(nc.gpsimd.tensor_tensor(rsc[:, :], ssq[:, :], c_dc[:, :], ALU.mult))
                    own.wait()
                    own.step(nc.gpsimd.tensor_tensor(rsc[:, :], rsc[:, :], c_eps[:, :], ALU.add))
                    own.wait()
                    own.step(nc.gpsimd.tensor_tensor(rsc[:, :], rsc[:, :], nhalf[:, :], ALU.pow))
                    own.wait()
                    nc.gpsimd.tensor_tensor(rsc[:, :], rsc[:, :], c_in[:, :], ALU.mult).then_inc(rsc_ready, 1)
                    own.done()

                pool.wait_ge(pool_c, 8)
                prep(0)
                with pool.Fori(0, NC // 2) as i:
                    for par in (0, 1):
                        prep(i * 2 + par + 1)

            @block.scalar
            def _(act):
                act.wait_ge(const_in, 80)
                nc.scalar.activation(tg[:, :], graw[:, :], ACT.Tanh).then_inc(act_own, 1)
                act.wait_ge(w_ready, 1)
                nc.scalar.activation(wh[:, :, :], wland[:, :, :], ACT.Copy).then_inc(w_hi, 1)

                def prep(k, par, first=False):
                    act.wait_ge(ctx_in, k * 32 + 32)
                    if not first:
                        act.wait_ge(rsc_ready, k)
                    for n in range(NT):
                        nc.scalar.activation(junk[:, :], ctxn[:, n, :], ACT.Square, accum_out=ssq[:, n:n + 1]
                                             ).then_inc(ssq_ready, 1)
                        act.wait_ge(ssq_ready, k * NT + n + 1)
                    act.wait_ge(dm_ready, k + 1)
                    nc.scalar.activation(dm[:, :, :], dm[:, :, :], ACT.Exp, scale=-DT).then_inc(ex_ready, 1)
                    for n in range(NT):
                        act.wait_ge(tr_ready, k * NT + n + 1)
                        nc.scalar.activation(yh[:, par, :, TT * n:TT * (n + 1)],
                                             psum[:, n % 2, 0:KD * TT].rearrange("p (k t) -> p k t", k=KD), ACT.Copy
                                             ).then_inc(tr_hi, 1)

                prep(0, 0, first=True)
                with act.Fori(0, NC // 2) as i:
                    for par in (0, 1):
                        prep(i * 2 + par + 1, 1 - par)

            @block.vector
            def _(dve):
                v = nc.vector
                pre = Chain(dve, dve_own)
                pre.step(v.memset(zeros[:, :], 0.0))
                pre.step(v.memset(ones[:, :], 1.0))
                pre.step(v.memset(zrow[:, :], 0.0))
                dve.wait_ge(lens_in, 16)
                pre.step(v.tensor_copy(lensf[:, :], lens[:, :]))
                pre.wait()
                pre.step(v.tensor_tensor_scan(cum[:, :], lensf[:, :], zeros[:, :], 0.0, ALU.add, ALU.add))
                pre.wait()
                pre.step(v.tensor_scalar(wrap[:, :], cum[:, :], 0.0, float(S), ALU.is_le, ALU.mult))
                pre.wait()
                v.scalar_tensor_tensor(out=idx[:, :], in0=cum[:, :], scalar=-1.0, in1=wrap[:, :],
                                       op0=ALU.add, op1=ALU.add).then_inc(idx_ready, 1)
                dve.wait_ge(pool_c, 8)
                pre.step(v.tensor_copy(tf[:, :], ti[:, :]))
                pre.step(v.tensor_copy(scol[:, :], si[:, :]))
                dve.wait_ge(const_in, 80)
                for k in range(KD):
                    ins = v.tensor_scalar(wland[:, k, :], wland[:, k, :], gres[:, k:k + 1], None, ALU.mult)
                    if k == KD - 1:
                        ins.then_inc(w_ready, 1)
                    else:
                        pre.step(ins)
                dve.wait_ge(idx_t, 1)
                pre.step(v.tensor_copy(idxT[:, :, :], psum[0:JP, 7, 0:JC * B].rearrange("p (c b) -> p c b", c=JC)))
                pre.wait()
                for c in range(JC):
                    v.tensor_tensor(eq[:, c, :, :], tf[0:JP, :].unsqueeze(1).broadcast_to([JP, B, S]),
                                    idxT[:, c, :].unsqueeze(2).broadcast_to([JP, B, S]), ALU.is_equal
                                    ).then_inc(eq_ready, 1)
                dve.wait_ge(w_hi, 1)
                pre.step(v.tensor_tensor(wl[:, :, :], wland[:, :, :], f(wh[:, :, :]), ALU.subtract))
                for q in range(NC):
                    dve.wait_ge(count_ready, q + 1)
                    pre.step(v.tensor_scalar(mark[:, 2 * q:2 * q + 2, :],
                                             psum[:, 2 + q, 0:CH].rearrange("p (b t) -> p b t", b=2),
                                             1.0, None, ALU.min))
                pre.wait()
                dve.sem_inc(out_free, NT)
                for b in range(B):
                    pre.step(v.tensor_tensor_scan(plug[:, b, :], mark[:, b, :], zrow[:, :], 0.0, ALU.add, ALU.add))
                pre.wait()
                pre.step(v.tensor_scalar(plug[:, :, :], plug[:, :, :], -1.0, 0.0, ALU.add, ALU.max))
                pre.wait()
                pre.step(v.tensor_scalar(plug[:, :, :], plug[:, :, :], float(M - 1), None, ALU.min))
                pre.wait()
                own = Chain(dve, dve_own, 21)
                pre_n = pre.n

                def wait_own():
                    dve.wait_ge(dve_own, own.base + own.n + pre_n)

                def prep(k, par, turn, ci):
                    own.at(k)
                    dve.wait_ge(x_in[par], turn * 16 + 16)
                    for n in range(NT):
                        own.step(v.bn_stats(stats[:, n, :], xt[:, par, n, :]))
                    wait_own()
                    v.memset(hold[:, :], 0.0)
                    for n in range(NT):
                        own.step(v.bn_aggr(mv[:, n, :], stats[:, n, :]))
                    wait_own()
                    v.tensor_scalar(ve[:, :], mv[:, :, 1], 1e-5, None, ALU.add).then_inc(var_ready, 1)
                    pl = plug[0:TT, bass.ds(ci * 2, 2), :]
                    for g in range(2):
                        ins = v.tensor_scalar(dm[:, g, :].rearrange("p (b t) -> p b t", b=2), pl, scol[0:TT, g:g + 1],
                                              0.0, ALU.subtract, ALU.max)
                        if g:
                            ins.then_inc(dm_ready, 1)
                        else:
                            own.step(ins)
                        own.step(v.tensor_scalar(mk[:, g, :].rearrange("p (b t) -> p b t", b=2), pl,
                                                 scol[0:TT, g:g + 1], None, ALU.is_ge))
                    dve.wait_ge(rstd_ready, k + 1)
                    for n in range(NT):
                        v.tensor_scalar(y[:, n, :], xt[:, par, n, :], mv[:, n, 0:1], rs[:, n:n + 1],
                                        ALU.subtract, ALU.mult).then_inc(y_ready, 1)
                    dve.wait_ge(ex_ready, k + 1)
                    wait_own()
                    own.step(v.tensor_tensor(mk[:, :, :], mk[:, :, :], dm[:, :, :], ALU.mult))
                    wait_own()
                    own.step(v.tensor_copy(mh[:, par], mk[:, :, :]))
                    wait_own()
                    v.tensor_tensor(ml[:, par], mk[:, :, :], f(mh[:, par]), ALU.subtract).then_inc(m_ready, 1)
                    for n in range(NT):
                        dve.wait_ge(tr_hi, k * NT + n + 1)
                        v.tensor_tensor(yl[:, par, :, TT * n:TT * (n + 1)],
                                        psum[:, n % 2, 0:KD * TT].rearrange("p (k t) -> p k t", k=KD),
                                        f(yh[:, par, :, TT * n:TT * (n + 1)]), ALU.subtract).then_inc(tr_free, 1)
                    dve.wait_ge(rsc_ready, k + 1)
                    for n in range(NT):
                        own.step(v.scalar_tensor_tensor(out=u32[:, :], in0=ctxn[:, n, 0:D], scalar=rsc[:, n:n + 1],
                                                        in1=gin_b[:, :], op0=ALU.mult, op1=ALU.mult))
                        wait_own()
                        own.step(v.tensor_copy(uh[:, par, n, :], u32[:, :]))
                        wait_own()
                        v.tensor_tensor(ul[:, par, n, :], u32[:, :], f(uh[:, par, n, :]), ALU.subtract
                                        ).then_inc(u_ready, 1)
                        dve.wait_ge(u_ready, k * NT + n + 1)

                def main(c, par):
                    for n in range(NT):
                        dve.wait_ge(out_ready, c * NT + n + 1)
                        v.tensor_tensor(tmp[:, :], psum[0:TT, 2 + n, :], bin_b[:, :], ALU.add).then_inc(out_free, 1)
                        dve.wait_ge(out_free, c * NT + n + 1 + NT)
                        v.scalar_tensor_tensor(out=xt[:, par, n, :], in0=tmp[:, :], scalar=tg[0:TT, 0:1],
                                               in1=xt[:, par, n, :], op0=ALU.mult, op1=ALU.add).then_inc(x_new, 1)
                        dve.wait_ge(x_new, c * NT + n + 1)

                dve.sem_inc(tr_free, 2)
                dve.wait_ge(w_ready, 1)
                dve.wait_ge(eq_ready, JC)
                prep(0, 0, 0, 0)
                own.done()
                dve.wait_ge(act_own, 1)
                with dve.Fori(0, NC // 2) as i:
                    for par in (0, 1):
                        c = i * 2 + par
                        prep(c + 1, 1 - par, i + par, i * -2 + 2 if par else i * 2 + 1)
                        own.done()
                        main(c, par)

            @block.tensor
            def _(pe):
                pe.wait_ge(pool_c, 3)
                pe.wait_ge(idx_ready, 1)
                for c in range(JC):
                    ins = nc.tensor.transpose(psum[0:JP, 7, B * c:B * (c + 1)], idx[:, JP * c:JP * (c + 1)],
                                              ident[0:B, 0:B])
                ins.then_inc(idx_t, 1)
                pe.wait_ge(eq_ready, JC)
                for q in range(NC):
                    for c in range(JC):
                        ins = nc.tensor.matmul(psum[:, 2 + q, 0:CH], ones[:, :],
                                               eq[:, c, 2 * q:2 * q + 2, :].rearrange("p b t -> p (b t)"),
                                               start=(c == 0), stop=(c == JC - 1))
                    ins.then_inc(count_ready, 1)

                def prep(k, par):
                    for n in range(NT):
                        pe.wait_ge(y_ready, k * NT + n + 1)
                        pe.wait_ge(tr_free, k * NT + n + 1)
                        for kt in range(KD):
                            ins = nc.tensor.transpose(psum[:, n % 2, TT * kt:TT * (kt + 1)],
                                                      y[:, n, P * kt:P * (kt + 1)], ident[0:TT, 0:TT])
                        ins.then_inc(tr_ready, 1)

                def main(c, par):
                    pe.wait_ge(tr_free, c * NT + NT + 2)
                    pe.wait_ge(u_ready, c * NT + NT)
                    pe.wait_ge(m_ready, c + 1)
                    for n in range(NT):
                        pe.wait_ge(out_free, c * NT + n + 1)
                        out = psum[0:TT, 2 + n, :]
                        cols = slice(TT * n, TT * (n + 1))
                        for kt in range(KD):
                            three(nc, out, yh[:, par, kt, cols], yl[:, par, kt, cols], wh[:, kt, :], wl[:, kt, :],
                                  kt == 0, False)
                        for g in range(n % 2 + 1):
                            ins = three(nc, out, mh[:, par, g, cols], ml[:, par, g, cols],
                                        uh[:, par, 2 * (n // 2) + g, :], ul[:, par, 2 * (n // 2) + g, :],
                                        False, g == n % 2)
                        ins.then_inc(out_ready, 1)

                pe.wait_ge(w_ready, 1)
                prep(0, 0)
                with pe.Fori(0, NC // 2) as i:
                    for par in (0, 1):
                        prep(i * 2 + par + 1, 1 - par)
                        main(i * 2 + par, par)


class Normed:

    def __init__(self, nc, m, psum, ident, x_dram):
        self.nc, self.psum, self.ident, self.x_dram = nc, psum, ident, x_dram
        self.xt = m.sb("xt", [TT, 2, NT, D])
        self.stats, self.mv = m.sb("stats", [TT, NT, 6]), m.sb("mv", [TT, NT, 2])
        self.ve, self.rs, self.nhalf = m.sb("ve", [TT, NT]), m.sb("rs", [TT, NT]), m.sb("nhalf", [TT, NT])
        self.hold = m.sb("hold", [TT, 1])
        self.y = m.sb("y", [TT, NT, D])
        self.yh, self.yl = m.sb("yh", [P, 2, KD, CH], F32R), m.sb("yl", [P, 2, KD, CH], F32R)
        self.x_in = [m.sem("x_in0"), m.sem("x_in1")]
        self.stats_done, self.var_ready, self.rstd_ready = m.sem("stats_done"), m.sem("var_ready"), m.sem("rstd_ready")
        self.aggr_done, self.nhalf_ready = m.sem("aggr_done"), m.sem("nhalf_ready")
        self.y_ready, self.tr_ready, self.tr_hi, self.tr_free = (
            m.sem("y_ready"), m.sem("tr_ready"), m.sem("tr_hi"), m.sem("tr_free"))

    def load(self, sp, k):
        c = k % NC
        sp.dma_start(self.xt[:, k % 2], self.x_dram[CH * c:CH * (c + 1), :].rearrange("(n p) d -> p n d", p=TT)
                     ).then_inc(self.x_in[k % 2], 16)

    def start_pool(self, pool):
        self.nc.gpsimd.memset(self.nhalf[:, :], -0.5).then_inc(self.nhalf_ready, 1)
        pool.wait_ge(self.nhalf_ready, 1)

    def rstd(self, pool, k):
        pool.wait_ge(self.var_ready, k + 1)
        self.nc.gpsimd.tensor_tensor(self.rs[:, :], self.ve[:, :], self.nhalf[:, :], ALU.pow).then_inc(self.rstd_ready, 1)

    def start_dve(self, dve):
        dve.sem_inc(self.tr_free, 2)

    def row_stats(self, dve, par, turn, n):
        v = self.nc.vector
        if n == 0:
            dve.wait_ge(self.x_in[par], turn * 16 + 16)
        v.bn_stats(self.stats[:, n, :], self.xt[:, par, n, :]).then_inc(self.stats_done, 1)

    def aggregate(self, dve, k):
        v = self.nc.vector
        dve.wait_ge(self.stats_done, k * NT + NT)
        v.memset(self.hold[:, :], 0.0)
        for n in range(NT):
            v.bn_aggr(self.mv[:, n, :], self.stats[:, n, :]).then_inc(self.aggr_done, 1)
        dve.wait_ge(self.aggr_done, k * NT + NT)
        v.tensor_scalar(self.ve[:, :], self.mv[:, :, 1], 1e-5, None, ALU.add).then_inc(self.var_ready, 1)

    def normalise(self, dve, k, par, n):
        if n == 0:
            dve.wait_ge(self.rstd_ready, k + 1)
        self.nc.vector.tensor_scalar(self.y[:, n, :], self.xt[:, par, n, :], self.mv[:, n, 0:1], self.rs[:, n:n + 1],
                                     ALU.subtract, ALU.mult).then_inc(self.y_ready, 1)

    def transpose(self, pe, k, n):
        nc = self.nc
        pe.wait_ge(self.y_ready, k * NT + n + 1)
        pe.wait_ge(self.tr_free, k * NT + n + 1)
        for kt in range(KD):
            ins = nc.tensor.transpose(self.psum[:, n % 2, TT * kt:TT * (kt + 1)], self.y[:, n, P * kt:P * (kt + 1)],
                                      self.ident[0:TT, 0:TT])
        ins.then_inc(self.tr_ready, 1)

    def hi(self, act, k, par, n):
        act.wait_ge(self.tr_ready, k * NT + n + 1)
        self.nc.scalar.activation(self.yh[:, par, :, TT * n:TT * (n + 1)],
                                  self.psum[:, n % 2, 0:KD * TT].rearrange("p (k t) -> p k t", k=KD), ACT.Copy
                                  ).then_inc(self.tr_hi, 1)

    def lo(self, dve, k, par, n):
        dve.wait_ge(self.tr_hi, k * NT + n + 1)
        self.nc.vector.tensor_tensor(self.yl[:, par, :, TT * n:TT * (n + 1)],
                                     self.psum[:, n % 2, 0:KD * TT].rearrange("p (k t) -> p k t", k=KD),
                                     f(self.yh[:, par, :, TT * n:TT * (n + 1)]), ALU.subtract
                                     ).then_inc(self.tr_free, 1)

    def split(self, pe, k):
        pe.wait_ge(self.tr_free, k * NT + NT + 2)


def phase_relu_ffn(nc, psum, ident, tg, d):
    with Mem(nc, "p2") as m:
        nm = Normed(nc, m, psum, ident, d["x1"])
        WL = 1024
        NW = KD * FF0 // WL * 2
        land = m.sb("land", [P, WL])
        w1h, w1l = m.sb("w1h", [P, KD, FF0], F32R), m.sb("w1l", [P, KD, FF0], F32R)
        w2h, w2l = m.sb("w2h", [P, NI0, D], F32R), m.sb("w2l", [P, NI0, D], F32R)
        b1, b2b = m.sb("b1", [P, NI0]), m.sb("b2b", [TT, D])
        hf = m.sb("hf", [P, 2, CH])
        hh, hl = m.sb("hh", [P, 2, CH], F32R), m.sb("hl", [P, 2, CH], F32R)
        tmp = m.sb("tmp", [TT, D])
        NB = 24
        wq = m.sb("wq", [P, NB, QB])
        wt = m.sb("wt", [P, NB, QB])
        bs, br = m.sb("bs", [P, NB]), m.sb("br", [P, NB])
        QS = 3 * KD * FF1 // (NB * QB) // NC
        s = m.sem
        w_in, w_hi, w_lo, b_in, x_out = s("w_in"), s("w_hi"), s("w_lo"), s("b_in"), s("x_out")
        h_ready, h_relu, h_hi, h_split, h_used = s("h_ready"), s("h_relu"), s("h_hi"), s("h_split"), s("h_used")
        out_ready, out_free, x_new = s("out_ready"), s("out_free"), s("x_new")
        q_in, q_own, q_out, q_stored = s("q_in"), s("q_own"), s("q_out"), s("q_stored")

        def slab(name, j):
            return d[name][j // 2, :, NB * QB * (j % 2):NB * QB * (j % 2 + 1)]

        def part(h, j):
            if j < NW // 2:
                return (w1h, w1l)[h][:, j // 2, WL * (j % 2):WL * (j % 2 + 1)]
            i = 2 * (j - NW // 2)
            return (w2h, w2l)[h][:, i:i + 2, :].rearrange("p k n -> p (k n)")

        with nc.Block() as block:
            @block.sync
            def _(sp):
                nm.load(sp, 0)
                sp.dma_start(b1[:, :], d["b1_cols"]).then_inc(b_in, 16)
                sp.dma_start(b2b[:, :], d["b2"].partition_broadcast(TT)).then_inc(b_in, 16)
                for j in range(NW):
                    if j:
                        sp.wait_ge(w_lo, j)
                    if j < NW // 2:
                        src = d["w1"][P * (j // 2):P * (j // 2 + 1), WL * (j % 2):WL * (j % 2 + 1)]
                        sp.dma_start(land[:, :], src).then_inc(w_in, 16)
                    else:
                        i = 2 * P * (j - NW // 2)
                        src = d["w2"][i:i + 2 * P, :].rearrange("(k p) n -> p k n", p=P)
                        sp.dma_start(land[:, :].rearrange("p (k n) -> p k n", k=2), src).then_inc(w_in, 16)
                nm.load(sp, 1)
                for j in range(NC * QS):
                    if j:
                        sp.wait_ge(q_out, j)
                        sp.dma_start(slab("wdq", j - 1), wt[:, :, :].rearrange("p a b -> p (a b)")).then_inc(q_stored, 16)
                    if j % QS == 0 and j:
                        k = j // QS
                        sp.wait_ge(x_new, NT * k)
                        sp.dma_start(d["x2"][CH * (k - 1):CH * k, :].rearrange("(n p) d -> p n d", p=TT),
                                     nm.xt[:, (k - 1) % 2]).then_inc(x_out, 16)
                        sp.wait_ge(x_out, 16 * k)
                        nm.load(sp, k + 1)
                    sp.dma_start(wq[:, :, :].rearrange("p a b -> p (a b)"), slab("w_q", j)).then_inc(q_in, 16)
                sp.wait_ge(q_out, NC * QS)
                sp.dma_start(slab("wdq", NC * QS - 1), wt[:, :, :].rearrange("p a b -> p (a b)")).then_inc(q_stored, 16)
                sp.wait_ge(x_new, NT * NC)
                sp.dma_start(d["x2"][CH * (NC - 1):T, :].rearrange("(n p) d -> p n d", p=TT), nm.xt[:, (NC - 1) % 2]
                             ).then_inc(x_out, 16)
                sp.wait_ge(x_out, 16 * NC)
                sp.wait_ge(q_stored, 16 * NC * QS + 16)

            @block.gpsimd
            def _(pool):
                nm.start_pool(pool)
                nm.rstd(pool, 0)
                with pool.Fori(0, NC // 2) as i:
                    for par in (0, 1):
                        nm.rstd(pool, i * 2 + par + 1)

            @block.scalar
            def _(act):
                for j in range(NW):
                    act.wait_ge(w_in, 16 * (j + 1))
                    nc.scalar.activation(part(0, j), land[:, :], ACT.Copy).then_inc(w_hi, 1)
                    if j == KD - 1:
                        for n in range(NT):
                            nm.hi(act, 0, 0, n)
                act.wait_ge(b_in, 32)
                act.sem_inc(h_relu, 2)
                with act.Fori(0, NC // 2) as i:
                    for par in (0, 1):
                        c = i * 2 + par
                        for it in range(NI0):
                            act.wait_ge(h_ready, c * NI0 + it + 1)
                            act.wait_ge(h_split, c * NI0 + it + 1)
                            nc.scalar.activation(hf[:, it % 2, :], psum[:, 2 + it % 2, 0:CH], ACT.Relu,
                                                 bias=b1[:, it:it + 1]).then_inc(h_relu, 1)
                            if 11 <= it < 15:
                                nm.hi(act, c + 1, 1 - par, it - 11)

            @block.vector
            def _(dve):
                v = nc.vector
                own = Chain(dve, q_own, 7 * QS)

                def dequantise(j):
                    dve.wait_ge(q_in, j * 16 + 16)
                    own.step(v.tensor_reduce(bs[:, :], wq[:, :, :], AX.X, ALU.max, apply_absolute_value=True))
                    own.wait()
                    own.step(v.tensor_scalar(bs[:, :], bs[:, :], float(np.float32(1.0) / np.float32(7.0)), 1e-12, ALU.mult, ALU.max))
                    own.wait()
                    own.step(v.reciprocal(br[:, :], bs[:, :]))
                    own.wait()
                    own.step(v.tensor_tensor(wq[:, :, :], wq[:, :, :], br[:, :].unsqueeze(2).broadcast_to([P, NB, QB]),
                                             ALU.mult))
                    yield
                    own.wait()
                    own.step(v.tensor_scalar(wq[:, :, :], wq[:, :, :], MAGIC, -MAGIC, ALU.add, ALU.add))
                    own.wait()
                    own.step(v.tensor_scalar(wq[:, :, :], wq[:, :, :], 7.0, -8.0, ALU.min, ALU.max))
                    own.wait()
                    own.step(v.tensor_tensor(wq[:, :, :], wq[:, :, :], bs[:, :].unsqueeze(2).broadcast_to([P, NB, QB]),
                                             ALU.mult))
                    dve.wait_ge(q_stored, j * 16 + 16)
                    own.wait()
                    v.transpose(wt[:, :, :].rearrange("p a b -> p (a b)"), wq[:, :, :].rearrange("p a b -> p (a b)")
                                ).then_inc(q_out, 1)
                    yield

                nm.start_dve(dve)
                dve.sem_inc(h_split, 2)
                dve.sem_inc(out_free, NT)
                dve.sem_inc(q_stored, 16)
                for n in range(NT):
                    nm.row_stats(dve, 0, 0, n)
                nm.aggregate(dve, 0)
                for n in range(NT):
                    nm.normalise(dve, 0, 0, n)
                for j in range(NW):
                    dve.wait_ge(w_hi, j + 1)
                    v.tensor_tensor(part(1, j), land[:, :], f(part(0, j)), ALU.subtract).then_inc(w_lo, 1)
                    if j == KD - 1:
                        for n in range(NT):
                            nm.lo(dve, 0, 0, n)
                with dve.Fori(0, NC // 2) as i:
                    for par in (0, 1):
                        c = i * 2 + par
                        own.at(c)
                        slabs = [dequantise(c * QS + r) for r in range(QS)]
                        for it in range(NI0):
                            dve.wait_ge(h_relu, c * NI0 + it + 1 + 2)
                            if it >= 2:
                                dve.wait_ge(h_used, c * (NI0 - 1) + it - 1)
                            v.tensor_copy(hh[:, it % 2, :], hf[:, it % 2, :]).then_inc(h_hi, 1)
                            dve.wait_ge(h_hi, c * NI0 + it + 1)
                            v.tensor_tensor(hl[:, it % 2, :], hf[:, it % 2, :],
                                            f(hh[:, it % 2, :]), ALU.subtract).then_inc(h_split, 1)
                            if it < 2 * QS:
                                next(slabs[it // 2])
                            if 3 <= it < 7:
                                nm.row_stats(dve, 1 - par, i + par, it - 3)
                            elif it == 7:
                                nm.aggregate(dve, c + 1)
                            elif 8 <= it < 12:
                                nm.normalise(dve, c + 1, 1 - par, it - 8)
                            elif it >= 12:
                                nm.lo(dve, c + 1, 1 - par, it - 12)
                        own.done()
                        for n in range(NT):
                            dve.wait_ge(out_ready, c * NT + n + 1)
                            v.tensor_tensor(tmp[:, :], psum[0:TT, 4 + n, :], b2b[:, :], ALU.add).then_inc(out_free, 1)
                            dve.wait_ge(out_free, c * NT + n + 1 + NT)
                            v.scalar_tensor_tensor(out=nm.xt[:, par, n, :], in0=tmp[:, :], scalar=tg[0:TT, 2:3],
                                                   in1=nm.xt[:, par, n, :], op0=ALU.mult, op1=ALU.add).then_inc(x_new, 1)
                            dve.wait_ge(x_new, c * NT + n + 1)

            @block.tensor
            def _(pe):
                for n in range(NT):
                    nm.transpose(pe, 0, n)
                pe.wait_ge(w_lo, NW // 2)

                def up(c, par, it):
                    pe.wait_ge(h_relu, c * NI0 + it + 1)
                    for kt in range(KD):
                        cols = slice(P * it, P * (it + 1))
                        ins = three(nc, psum[:, 2 + it % 2, 0:CH], w1h[:, kt, cols], w1l[:, kt, cols],
                                    nm.yh[:, par, kt, :], nm.yl[:, par, kt, :], kt == 0, kt == KD - 1)
                    ins.then_inc(h_ready, 1)

                def down(c, par, it):
                    pe.wait_ge(h_split, c * NI0 + it + 1 + 2)
                    for n in range(NT):
                        if it == 0:
                            pe.wait_ge(out_free, c * NT + n + 1)
                        cols = slice(TT * n, TT * (n + 1))
                        ins = three(nc, psum[0:TT, 4 + n, :], hh[:, it % 2, cols], hl[:, it % 2, cols],
                                    w2h[:, it, :], w2l[:, it, :], it == 0, it == NI0 - 1)
                        if it == NI0 - 1:
                            ins.then_inc(out_ready, 1)
                        elif n == NT - 1:
                            ins.then_inc(h_used, 1)

                with pe.Fori(0, NC // 2) as i:
                    for par in (0, 1):
                        c = i * 2 + par
                        nm.split(pe, c)
                        up(c, par, 0)
                        for it in range(NI0):
                            if it + 1 < NI0:
                                up(c, par, it + 1)
                            if it == 0:
                                pe.wait_ge(w_lo, NW)
                            down(c, par, it)
                            if 9 <= it < 13:
                                nm.transpose(pe, c + 1, it - 9)


def phase_queries(nc, psum, ident, tg, d):
    with Mem(nc, "p3") as m:
        nm = Normed(nc, m, psum, ident, d["x2"])
        NG = INNER // P
        RG = 4
        land = m.sb("land", [P, KD, INNER])
        wh, wl = m.sb("wh", [P, KD, INNER], F32R), m.sb("wl", [P, KD, INNER], F32R)
        stage = m.sb("stage", [P, RG, CH])
        s = m.sem
        w_in, w_hi, w_lo = s("w_in"), s("w_hi"), s("w_lo")
        q_ready, q_done = s("q_ready"), s("q_done")
        q_out = [s(f"q_out{i}") for i in range(RG)]

        with nc.Block() as block:
            @block.sync
            def _(sp):
                nm.load(sp, 0)
                sp.dma_start(land[:, :, :], d["wq"].rearrange("(k p) n -> p k n", p=P)).then_inc(w_in, 16)
                nm.load(sp, 1)
                for k in range(NC):
                    for g in range(NG):
                        e = k * NG + g
                        sp.wait_ge(q_done, e + 1 + RG)
                        sp.dma_start(d["qT"][P * g:P * (g + 1), CH * k:CH * (k + 1)], stage[:, g % RG, :]
                                     ).then_inc(q_out[g % RG], 16)
                        if g == 0 and k + 2 <= NC:
                            sp.wait_ge(nm.y_ready, NT * (k + 1))
                            nm.load(sp, k + 2)
                for i in range(RG):
                    sp.wait_ge(q_out[i], 16 + 16 * NC * NG // RG)

            @block.gpsimd
            def _(pool):
                nm.start_pool(pool)
                nm.rstd(pool, 0)
                with pool.Fori(0, NC // 2) as i:
                    for par in (0, 1):
                        nm.rstd(pool, i * 2 + par + 1)

            @block.scalar
            def _(act):
                act.wait_ge(w_in, 16)
                nc.scalar.activation(wh[:, :, :], land[:, :, :], ACT.Copy).then_inc(w_hi, 1)
                for n in range(NT):
                    nm.hi(act, 0, 0, n)
                act.sem_inc(q_done, RG)
                for i in range(RG):
                    act.sem_inc(q_out[i], 16)
                with act.Fori(0, NC // 2) as i:
                    for par in (0, 1):
                        c = i * 2 + par
                        for g in range(NG):
                            act.wait_ge(q_ready, c * NG + g + 1)
                            act.wait_ge(q_out[g % RG], (c * (NG // RG) + g // RG) * 16 + 16)
                            nc.scalar.activation(stage[:, g % RG, :], psum[:, 2 + g % RG, 0:CH], ACT.Copy,
                                                 scale=DH ** -0.5).then_inc(q_done, 1)
                            if g >= NG - NT:
                                nm.hi(act, c + 1, 1 - par, g - (NG - NT))

            @block.vector
            def _(dve):
                v = nc.vector
                nm.start_dve(dve)
                for n in range(NT):
                    nm.row_stats(dve, 0, 0, n)
                nm.aggregate(dve, 0)
                for n in range(NT):
                    nm.normalise(dve, 0, 0, n)
                dve.wait_ge(w_hi, 1)
                v.tensor_tensor(wl[:, :, :], land[:, :, :], f(wh[:, :, :]), ALU.subtract).then_inc(w_lo, 1)
                for n in range(NT):
                    nm.lo(dve, 0, 0, n)
                with dve.Fori(0, NC // 2) as i:
                    for par in (0, 1):
                        for n in range(NT):
                            nm.row_stats(dve, 1 - par, i + par, n)
                        nm.aggregate(dve, i * 2 + par + 1)
                        for n in range(NT):
                            nm.normalise(dve, i * 2 + par + 1, 1 - par, n)
                        for n in range(NT):
                            nm.lo(dve, i * 2 + par + 1, 1 - par, n)

            @block.tensor
            def _(pe):
                for n in range(NT):
                    nm.transpose(pe, 0, n)
                pe.wait_ge(w_lo, 1)
                with pe.Fori(0, NC // 2) as i:
                    for par in (0, 1):
                        c = i * 2 + par
                        nm.split(pe, c)
                        for g in range(NG):
                            pe.wait_ge(q_done, c * NG + g + 1)
                            for kt in range(KD):
                                cols = slice(P * g, P * (g + 1))
                                ins = three(nc, psum[:, 2 + g % RG, 0:CH], wh[:, kt, cols], wl[:, kt, cols],
                                            nm.yh[:, par, kt, :], nm.yl[:, par, kt, :], kt == 0, kt == KD - 1)
                            ins.then_inc(q_ready, 1)
                            if NG - NT - 1 <= g < NG - 1:
                                nm.transpose(pe, c + 1, g - (NG - NT - 1))


TURN = ("S0 G0 R0 C4 G1 C5 T00 T01 S1 G2 R1 C6 T02 G3 C7 A0 T10 S2 G4 R2 Q T11 T12 G5 c0 A1 T20 "
        "S3 G6 R3 c1 T21 T22 G7 c2 A2 T30 G8 c3 T31 T32 G9 A3").split()


def turn_steps(project=True, read_on=True, keys=False, values=False):
    steps = [x for x in TURN if (project or x[0] not in "GCQ") and (read_on or x[0] != "c")]
    if keys:
        steps.insert(steps.index("G8"), "K")
    if values:
        steps.insert(steps.index("G1"), "V")
    return steps


def phase_attention(nc, psum, ident, d):
    HG = 4
    GW = HG * DH
    NG = H // HG
    ROWS = M // 6
    MK = M + 1
    MP = M + 2
    HW = 376
    LO = M - HW
    BK = 512
    NP = 10
    NU = NG * B
    with Mem(nc, "p4") as m:
        wland = m.sb("wland", [P, 2, KC, GW])
        wh, wl = m.sb("wh", [P, 2, KC, GW], F32R), m.sb("wl", [P, 2, KC, GW], F32R)
        land = m.sb("land", [P, 4, 2, HW])
        ch, cl = m.sb("ch", [P, 2, KC, HW], F32R), m.sb("cl", [P, 2, KC, HW], F32R)
        kt_ = m.sb("kt", [P, 2, HG, MP], F32R)
        v_ = m.sb("v", [P, 2, 6, HG, 2 * DH], F32R)
        q32 = m.sb("q32", [P, HG, S])
        qh, ql = m.sb("qh", [P, 2, HG, S], F32R), m.sb("ql", [P, 2, HG, S], F32R)
        p = m.sb("p", [TT, 4, MP])
        ph, pl = m.sb("ph", [P, 4, 2 * S], F32R), m.sb("pl", [P, 4, 2 * S], F32R)
        tmp = m.sb("tmp", [DH, 2, S])
        ao = m.sb("ao", [P, 2, 2, S])
        negm, rsum, rinv = m.sb("negm", [TT, 4]), m.sb("rsum", [TT, 4]), m.sb("rinv", [TT, 4])
        hold = m.sb("hold", [TT, 4])
        nk, nkh = m.sb("nk", [P, 2]), m.sb("nkh", [P, 2], F32R)
        nv, nvr = m.sb("nv", [1, DH]), m.sb("nvr", [1, HG, 2 * DH], F32R)

        s = m.sem
        w_in, w_hi, w_lo = [s("wk_in"), s("wv_in")], s("w_hi"), s("w_lo")
        c_in, c_hi, c_lo = [s(f"c_in{i}") for i in range(4)], s("c_hi"), s("c_lo")
        q_in, q_hi, q_lo = s("q_in"), s("q_hi"), s("q_lo")
        null_in, null_own, null_row = s("null_in"), s("null_own"), s("null_row")
        sc_ready, mx_done, exp_done = s("sc_ready"), s("mx_done"), s("exp_done")
        rinv_done, norm_done = s("rinv_done"), s("norm_done")
        at_ready, at_hi, at_done = s("at_ready"), s("at_hi"), s("at_done")
        pj_ready, pj_hi, pj_lo = s("pj_ready"), s("pj_hi"), s("pj_lo")
        ao_out = [s(f"ao_out{i}") for i in range(4)]

        def wait(e, sem, value):
            if not isinstance(value, int) or value > 0:
                e.wait_ge(sem, value)

        def group(i):
            half, j = divmod(i, 5)
            return ("k", half, j) if j < 2 else ("v", half, 3 * half + j - 2)

        def run(e, unit, group_start=None):
            def pair(g, k, u0, turn, change=False, last=False):
                if change:
                    later = [(g, B - 1), (g + 1, 0), (g + 1, 1)]
                else:
                    later = [(g, k * 2 + 1), (g, k * 2 + 2), (g, k * 2 + 3)]
                here = [(g, k * 2), (g, k * 2 + 1)]
                for par in (0, 1):
                    unit(u0 + par, par, turn, here[par], later[par], later[par + 1],
                         dict(project=not (last and par), read_on=not last,
                              keys=change and par == 0, values=change and par == 1))

            with e.Fori(0, NG - 1) as g:
                if group_start:
                    group_start(g)
                with e.Fori(0, B // 2 - 1) as k:
                    pair(g, k, g * B + k * 2, g * (B // 2) + k)
                pair(g, B // 2 - 1, g * B + (B - 2), g * (B // 2) + (B // 2 - 1), change=True)
            g = NG - 1
            with e.Fori(0, B // 2 - 1) as k:
                pair(g, k, k * 2 + g * B, k + g * (B // 2))
            pair(g, B // 2 - 1, NU - 2, NU // 2 - 1, last=True)

        with nc.Block() as block:
            @block.sync
            def _(sp):
                def weights(g):
                    for i in range(2):
                        src = d["wkv"][:, bass.ds(g * GW + i * INNER, GW)].rearrange("(k p) n -> p k n", p=P)
                        sp.dma_start(wland[:, i], src).then_inc(w_in[i], 16)

                def piece(w, b, j):
                    half, jj = divmod(j, 4)
                    sp.wait_ge(c_lo, w * 8 + j + 1)
                    src = d["ctx_t"][bass.ds(b, 1), 2 * P * jj:2 * P * (jj + 1), half * LO:half * LO + HW]
                    sp.dma_start(land[:, jj], src.rearrange("o (k p) t -> p (o k) t", p=P)).then_inc(c_in[jj], 16)

                def queries(u, g, b):
                    wait(sp, q_lo, u)
                    src = d["qT"][bass.ds(g * GW, GW), bass.ds(b * S, S)].rearrange("(h e) t -> e h t", e=DH)
                    for half in range(2):
                        sp.dma_start(q32[DH * half:DH * (half + 1)], src).then_inc(q_in, 16)

                def store(u, par, g, b, pr):
                    sp.wait_ge(at_done, u * 16 + (8 * pr + 8 + 2))
                    dst = d["aT"][bass.ds(g * GW + pr * P, P), bass.ds(b * S, S)]
                    sp.dma_start(dst, ao[:, par, pr, :]).then_inc(ao_out[2 * par + pr], 16)

                def unit(u, par, turn, here, next1, next2, kind):
                    if kind["project"]:
                        queries(u + 1, *next1)
                    for j in range(8):
                        if j == 4:
                            store(u, par, *here, 0)
                        if kind["read_on"]:
                            piece(u + 2, next2[1], j)
                    store(u, par, *here, 1)

                weights(0)
                for j in range(8):
                    piece(0, 0, j)
                sp.wait_ge(null_own, 1)
                for half in range(2):
                    sp.dma_start(nk[DH * half:DH * (half + 1), 0:1], d["null_kv"][0].unsqueeze(1)).then_inc(null_in, 16)
                sp.dma_start(nv[:, :], d["null_kv"][1:2, :]).then_inc(null_in, 16)
                queries(0, 0, 0)
                sp.wait_ge(null_own, 8)
                for par in range(2):
                    sp.dma_start(f(v_[ROWS:ROWS + 1, par, 5, :, :]), f(nvr[:, :, :])).then_inc(null_row, 16)
                for j in range(8):
                    piece(1, 1, j)
                def group_start(g):
                    sp.wait_ge(w_lo, g * 2 + 2)
                    weights(g + 1)
                run(sp, unit, group_start)
                for i in range(4):
                    sp.wait_ge(ao_out[i], 16 * (NU // 2) + 16)

            @block.gpsimd
            def _(pool):
                nc.gpsimd.memset(nk[:, :], 0.0).then_inc(null_own, 1)

                def unit(u, par, turn, here, next1, next2, kind):
                    for n in range(2 * HG):
                        pool.wait_ge(rinv_done, u * 8 + n + 1)
                        nc.gpsimd.tensor_tensor(hold[:, n % 4:n % 4 + 1], rinv[:, n % 4:n % 4 + 1], rinv[:, n % 4:n % 4 + 1], ALU.mult)
                        nc.gpsimd.tensor_scalar(p[:, n % 4, 0:MK], p[:, n % 4, 0:MK], rinv[:, n % 4:n % 4 + 1], 1.0,
                                                ALU.mult, ALU.mult).then_inc(norm_done, 1)
                run(pool, unit)

            def weights_free(e, step, u):
                wait(e, pj_ready, u * NP + (NP + 7 if step == "K" else NP))

            def rows_free(e, u, j):
                wait(e, pj_ready, u * NP + (NP + 5 if j < 4 else NP))

            @block.scalar
            def _(act):
                def split(step, u, par, wgroup):
                    if step in "KV":
                        i = "KV".index(step)
                        act.wait_ge(w_in[i], wgroup * 16 + 16)
                        weights_free(act, step, u)
                        nc.scalar.activation(wh[:, i], wland[:, i], ACT.Copy).then_inc(w_hi, 1)
                    elif step == "Q":
                        act.wait_ge(q_in, u * 32 + 64)
                        nc.scalar.activation(qh[:, 1 - par], q32[:, :, :], ACT.Copy).then_inc(q_hi, 1)
                    else:
                        w, j = u + (1 if step[0] == "C" else 2), int(step[1])
                        act.wait_ge(c_in[j % 4], w * 32 + (j // 4) * 16 + 16)
                        rows_free(act, u, j)
                        nc.scalar.activation(ch[:, j // 4, 2 * (j % 4):2 * (j % 4) + 2, :], land[:, j % 4], ACT.Copy
                                             ).then_inc(c_hi, 1)

                def project(u, par, i):
                    kind, half, j = group(i)
                    act.wait_ge(pj_ready, u * NP + (NP + i + 1))
                    bank = psum[:, 6 + i % 2, :]
                    if kind == "k":
                        t0, t1 = (0, HW) if half == 0 else (HW, M)
                        for e in range(2):
                            ins = nc.scalar.activation(kt_[0:DH, 1 - par, 2 * j + e, t0:t1],
                                                       bank[DH * e:DH * (e + 1), 0:t1 - t0], ACT.Copy)
                    else:
                        ins = nc.scalar.activation(v_[0:ROWS, 1 - par, j, :, 0:DH],
                                                   bank[0:ROWS, 0:GW].rearrange("p (h e) -> p h e", h=HG), ACT.Copy)
                    ins.then_inc(pj_hi, 1)

                def unit(u, par, turn, here, next1, next2, kind):
                    for step in turn_steps(**kind):
                        if step[0] in "CcQKV":
                            split(step, u, par, next1[0] if step == "V" else next2[0])
                        elif step[0] == "G":
                            project(u, par, int(step[1]))
                        elif step[0] == "S":
                            for i in range(2):
                                n = 2 * int(step[1]) + i
                                act.wait_ge(mx_done, u * 8 + n + 1)
                                nc.scalar.activation(p[:, n % 4, 0:MK],
                                                     psum[0:TT, 2 * i:2 * i + 2, :].rearrange("p a n -> p (a n)")[:, 0:MK],
                                                     ACT.Exp, bias=negm[:, n % 4:n % 4 + 1],
                                                     accum_out=rsum[:, n % 4:n % 4 + 1]).then_inc(exp_done, 1)
                        elif step[0] == "T":
                            h, c = int(step[1]), int(step[2])
                            rows = ROWS + (c == 2)
                            act.wait_ge(at_ready, u * 16 + (4 * h + c + 1))
                            nc.scalar.activation(ph[0:rows, (3 * h + c) % 4, :], psum[0:rows, 4 + c % 2, 0:2 * S],
                                                 ACT.Copy).then_inc(at_hi, 1)
                        elif step[0] == "A":
                            h = int(step[1])
                            act.wait_ge(at_ready, u * 16 + (4 * h + 4))
                            nc.scalar.activation(tmp[:, h % 2, :], psum[DH:P, 5, 0:S], ACT.Copy).then_inc(at_hi, 1)

                act.sem_inc(exp_done, 2)
                for step in ("K", "c0", "c1", "c2", "c3"):
                    split(step, -2, 1, 0)
                for step in ("V", "C4", "C5", "C6", "C7"):
                    split(step, -1, 1, 0)
                for i in range(NP):
                    project(-1, 1, i)
                    if i == 5:
                        for step in ("Q", "c0", "c1", "c2", "c3"):
                            split(step, -1, 1, 0)
                run(act, unit)

            @block.vector
            def _(dve):
                v = nc.vector

                def split(step, u, par, wgroup):
                    if step in "KV":
                        i = "KV".index(step)
                        dve.wait_ge(w_hi, wgroup * 2 + i + 1)
                        v.tensor_tensor(wl[:, i], wland[:, i], f(wh[:, i]), ALU.subtract).then_inc(w_lo, 1)
                    elif step == "Q":
                        dve.wait_ge(q_hi, u + 2)
                        v.tensor_tensor(ql[:, 1 - par], q32[:, :, :], f(qh[:, 1 - par]), ALU.subtract).then_inc(q_lo, 1)
                    else:
                        w, j = u + (1 if step[0] == "C" else 2), int(step[1])
                        dve.wait_ge(c_hi, w * 8 + j + 1)
                        at = (slice(None), j // 4, slice(2 * (j % 4), 2 * (j % 4) + 2))
                        v.tensor_tensor(cl[at], land[:, j % 4], f(ch[at]), ALU.subtract).then_inc(c_lo, 1)

                def project(u, par, i):
                    kind, half, j = group(i)
                    dve.wait_ge(pj_hi, u * NP + (NP + i + 1))
                    bank = psum[:, 6 + i % 2, :]
                    if kind == "k":
                        t0, t1 = (0, HW) if half == 0 else (HW, M)
                        for e in range(2):
                            ins = v.tensor_tensor(kt_[DH:P, 1 - par, 2 * j + e, t0:t1],
                                                  bank[DH * e:DH * (e + 1), 0:t1 - t0],
                                                  f(kt_[0:DH, 1 - par, 2 * j + e, t0:t1]), ALU.subtract)
                    else:
                        ins = v.tensor_tensor(v_[0:ROWS, 1 - par, j, :, DH:2 * DH],
                                              bank[0:ROWS, 0:GW].rearrange("p (h e) -> p h e", h=HG),
                                              f(v_[0:ROWS, 1 - par, j, :, 0:DH]), ALU.subtract)
                    ins.then_inc(pj_lo, 1)

                def unit(u, par, turn, here, next1, next2, kind):
                    for step in turn_steps(**kind):
                        if step[0] in "CcQKV":
                            split(step, u, par, next1[0] if step == "V" else next2[0])
                        elif step[0] == "G":
                            project(u, par, int(step[1]))
                        elif step[0] == "S":
                            for i in range(2):
                                n = 2 * int(step[1]) + i
                                dve.wait_ge(sc_ready, u * 8 + n + 1)
                                v.tensor_reduce(negm[:, n % 4:n % 4 + 1],
                                                psum[0:TT, 2 * i:2 * i + 2, :].rearrange("p a n -> p (a n)")[:, 0:MK],
                                                AX.X, ALU.max, negate=True).then_inc(mx_done, 1)
                        elif step[0] == "R":
                            for i in range(2):
                                n = 2 * int(step[1]) + i
                                dve.wait_ge(exp_done, u * 8 + (n + 1 + 2))
                                v.reciprocal(rinv[:, n % 4:n % 4 + 1], rsum[:, n % 4:n % 4 + 1]).then_inc(rinv_done, 1)
                        elif step[0] == "T":
                            h, c = int(step[1]), int(step[2])
                            rows = ROWS + (c == 2)
                            dve.wait_ge(at_hi, u * 16 + (4 * h + c + 1))
                            v.tensor_tensor(pl[0:rows, (3 * h + c) % 4, :], psum[0:rows, 4 + c % 2, 0:2 * S],
                                            f(ph[0:rows, (3 * h + c) % 4, :]), ALU.subtract).then_inc(at_done, 1)
                        elif step[0] == "A":
                            h = int(step[1])
                            dve.wait_ge(at_hi, u * 16 + (4 * h + 4))
                            if h % 2 == 0:
                                dve.wait_ge(ao_out[2 * par + h // 2], turn * 16 + 16)
                            v.tensor_tensor(ao[DH * (h % 2):DH * (h % 2 + 1), par, h // 2, :], psum[0:DH, 5, 0:S],
                                            tmp[:, h % 2, :], ALU.add).then_inc(at_done, 1)

                dve.sem_inc(c_lo, 4)
                dve.sem_inc(at_done, 2)
                dve.sem_inc(pj_lo, 2)
                for i in range(4):
                    dve.sem_inc(ao_out[i], 16)
                for step in ("K", "c0", "c1", "c2", "c3"):
                    split(step, -2, 1, 0)
                null = Chain(dve, null_own)
                null.n = 1
                dve.wait_ge(null_in, 48)
                null.wait()
                null.step(v.tensor_copy(nkh[:, :], nk[:, :]))
                for par in range(2):
                    null.step(v.tensor_copy(kt_[0:DH, par, :, M:MP], nk[0:DH, :].unsqueeze(1).broadcast_to([DH, HG, 2])))
                null.step(v.tensor_copy(nvr[:, :, 0:DH], nv[:, :].unsqueeze(1).broadcast_to([1, HG, DH])))
                null.wait()
                for par in range(2):
                    null.step(v.tensor_tensor(kt_[DH:P, par, :, M:MP],
                                              nk[DH:P, :].unsqueeze(1).broadcast_to([DH, HG, 2]),
                                              f(nkh[DH:P, :]).unsqueeze(1).broadcast_to([DH, HG, 2]), ALU.subtract))
                null.step(v.tensor_tensor(nvr[:, :, DH:2 * DH], nv[:, :].unsqueeze(1).broadcast_to([1, HG, DH]),
                                          f(nvr[:, :, 0:DH]), ALU.subtract))
                assert null.n == 8
                for step in ("V", "C4", "C5", "C6", "C7"):
                    split(step, -1, 1, 0)
                for i in range(NP):
                    project(-1, 1, i)
                    if i == 5:
                        for step in ("Q", "c0", "c1", "c2", "c3"):
                            split(step, -1, 1, 0)
                run(dve, unit)

            @block.tensor
            def _(pe):
                def project(u, i, wgroup):
                    kind, half, j = group(i)
                    pe.wait_ge(pj_lo, u * NP + (NP + i + 1))
                    if i % 5 == 0:
                        pe.wait_ge(c_lo, u * 8 + (8 + 4 * half + 4 + 4))
                    if i == 0 or i == 2:
                        pe.wait_ge(w_lo, wgroup * 2 + (1 if i == 0 else 2))
                    for kt in range(KC):
                        first, last = kt == 0, kt == KC - 1
                        if kind == "k":
                            c0, c1 = (0, HW) if half == 0 else (HW - LO, HW)
                            cols = slice(P * j, P * (j + 1))
                            ins = three(nc, psum[:, 6 + i % 2, 0:c1 - c0], wh[:, 0, kt, cols], wl[:, 0, kt, cols],
                                        ch[:, half, kt, c0:c1], cl[:, half, kt, c0:c1], first, last)
                        else:
                            c0 = ROWS * j - half * LO
                            ins = three(nc, psum[0:ROWS, 6 + i % 2, 0:GW],
                                        ch[:, half, kt, c0:c0 + ROWS], cl[:, half, kt, c0:c0 + ROWS],
                                        wh[:, 1, kt, :], wl[:, 1, kt, :], first, last)
                    ins.then_inc(pj_ready, 1)

                def unit(u, par, turn, here, next1, next2, kind):
                    for step in turn_steps(**kind):
                        if step[0] == "G":
                            project(u, int(step[1]), next1[0])
                        elif step[0] == "S":
                            h = int(step[1])
                            if h == 0:
                                pe.wait_ge(q_lo, u + 1)
                                pe.wait_ge(pj_lo, u * NP + (7 + 2))
                            for i in range(2):
                                pe.wait_ge(exp_done, u * 8 + (2 * h + i + 1))
                                cols = slice(TT * i, TT * (i + 1))
                                for b, c1 in ((0, BK), (1, MP)):
                                    out = psum[0:TT, 2 * i + b, 0:c1 - BK * b]
                                    nc.tensor.matmul(out, qh[:, par, h, cols], kt_[:, par, h, BK * b:c1],
                                                     start=True, stop=False)
                                    ins = nc.tensor.matmul(out, ql[:, par, h, cols], kt_[:, par, h, BK * b:c1],
                                                           start=False, stop=True)
                                ins.then_inc(sc_ready, 1)
                        elif step[0] == "T":
                            h, c = int(step[1]), int(step[2])
                            rows = ROWS + (c == 2)
                            if c == 0:
                                pe.wait_ge(norm_done, u * 8 + (2 * h + 2))
                            pe.wait_ge(at_done, u * 16 + (4 * h + c + 1))
                            for t in (0, 1):
                                for i in range(2):
                                    at = S * t + TT * i
                                    r0 = ROWS * (2 * c + t)
                                    ins = nc.tensor.transpose(psum[0:rows, 4 + c % 2, at:at + TT],
                                                              p[:, (2 * h + i) % 4, r0:r0 + rows], ident[0:TT, 0:TT])
                            ins.then_inc(at_ready, 1)
                        elif step[0] == "A":
                            h = int(step[1])
                            if h == 0:
                                pe.wait_ge(pj_lo, u * NP + (NP + 2))
                            pe.wait_ge(at_done, u * 16 + (4 * h + 3 + 2))
                            for t in range(6):
                                rows = ROWS + (t == 5)
                                slot = (3 * h + t // 2) % 4
                                cols = slice(S * (t % 2), S * (t % 2 + 1))
                                nc.tensor.matmul(psum[:, 5, 0:S], v_[0:rows, par, t, h, :], ph[0:rows, slot, cols],
                                                 start=t == 0, stop=False)
                                ins = nc.tensor.matmul(psum[:, 5, 0:S], v_[0:rows, par, t, h, :], pl[0:rows, slot, cols],
                                                       start=False, stop=t == 5)
                            ins.then_inc(at_ready, 1)

                pe.wait_ge(null_own, 8)
                pe.wait_ge(null_row, 32)
                for i in range(NP):
                    project(-1, i, 0)
                run(pe, unit)


def phase_attention_out(nc, psum, ident, tg, ymax, y_all, d):
    KI = INNER // P
    NE = NC * NT
    RA, RX = 3, 6
    with Mem(nc, "p5") as m:
        wland = m.sb("wland", [P, KI, D])
        wh, wl = m.sb("wh", [P, KI, D], F32R), m.sb("wl", [P, KI, D], F32R)
        aland = m.sb("aland", [P, RA, KI, TT])
        ah, al = m.sb("ah", [P, RA, KI, TT], F32R), m.sb("al", [P, RA, KI, TT], F32R)
        scale_b, bias_b = m.sb("scale_b", [TT, D]), m.sb("bias_b", [TT, D])
        xt = m.sb("xt", [TT, RX, D])
        z, y = m.sb("z", [TT, 2, D]), m.sb("y", [TT, 2, D])
        st1, st2 = m.sb("st1", [TT, 2, 6]), m.sb("st2", [TT, 2, 6])
        mv1, mv2 = m.sb("mv1", [TT, 2, 2]), m.sb("mv2", [TT, 2, 2])
        rs1, rs2 = m.sb("rs1", [TT, 2, 2]), m.sb("rs2", [TT, 2, 2])
        nhalf = m.sb("nhalf", [TT, 1])
        s = m.sem
        const_in, w_in, w_hi, w_lo, ln_ready = s("const_in"), [s("w_in0"), s("w_in1")], s("w_hi"), s("w_lo"), s("ln_ready")
        a_in, a_hi, a_lo = [s(f"a_in{i}") for i in range(RA)], s("a_hi"), s("a_lo")
        x_in, x_out = [s(f"x_in{i}") for i in range(RX)], [s(f"x_out{i}") for i in range(RX)]
        dve_own, pool_own, nhalf_ready, x_biased = s("dve_own"), s("pool_own"), s("nhalf_ready"), s("x_biased")
        out_ready, mv1_ready, rs1_ready, z_ready, z_scaled = (
            s("out_ready"), s("mv1_ready"), s("rs1_ready"), s("z_ready"), s("z_scaled"))
        x_new, mv2_ready, rs2_ready, y_ready, max_done = (
            s("x_new"), s("mv2_ready"), s("rs2_ready"), s("y_ready"), s("max_done"))
        tr_ready, tr_read = s("tr_ready"), s("tr_read")

        def rows(name, e):
            return d[name][TT * e:TT * (e + 1), :]

        with nc.Block() as block:
            @block.sync
            def _(sp):
                def load_a(e):
                    sp.dma_start(aland[:, e % RA], d["aT"][:, TT * e:TT * (e + 1)].rearrange("(k p) t -> p k t", p=P)
                                 ).then_inc(a_in[e % RA], 16)

                def load_x(e):
                    sp.dma_start(xt[:, e % RX, :], rows("x2", e)).then_inc(x_in[e % RX], 16)

                for h in (0, 1):
                    half = slice(KI // 2 * h, KI // 2 * (h + 1))
                    sp.dma_start(wland[:, half, :], d["wout"].rearrange("(k p) n -> p k n", p=P)[:, half, :]
                                 ).then_inc(w_in[h], 16)
                    load_a(h)
                sp.dma_start(scale_b[:, :], d["ln_scale"].partition_broadcast(TT)).then_inc(const_in, 16)
                sp.dma_start(bias_b[:, :], d["ln_bias"].partition_broadcast(TT)).then_inc(const_in, 16)
                for e in range(RX):
                    load_x(e)
                for e in range(2, NE + RX):
                    if e < NE:
                        if e >= RA:
                            sp.wait_ge(a_lo, e - RA + 1)
                        load_a(e)
                    if e >= RX:
                        k = e - RX
                        sp.wait_ge(x_new, k + 1)
                        sp.dma_start(rows("x3", k), xt[:, k % RX, :]).then_inc(x_out[k % RX], 16)
                        sp.wait_ge(x_out[k % RX], 16 * (k // RX + 1))
                        if e < NE:
                            sp.wait_ge(y_ready, k + 1)
                            load_x(e)

            @block.gpsimd
            def _(pool):
                own = Chain(pool, pool_own)
                nc.gpsimd.memset(nhalf[:, :], -0.5).then_inc(nhalf_ready, 1)
                pool.wait_ge(nhalf_ready, 1)

                def moments(mv, rs, e, eps, done):
                    i = e % 2
                    own.step(nc.gpsimd.tensor_scalar(rs[:, i, 0:1], mv[:, i, 1:2], eps, 1.0, ALU.add, ALU.mult))
                    own.wait()
                    own.step(nc.gpsimd.tensor_tensor(rs[:, i, 0:1], rs[:, i, 0:1], nhalf[:, :], ALU.pow))
                    own.wait()
                    nc.gpsimd.tensor_scalar(rs[:, i, 1:2], mv[:, i, 0:1], rs[:, i, 0:1], -1.0, ALU.mult, ALU.mult
                                            ).then_inc(done, 1)

                def bias(e):
                    pool.wait_ge(x_in[e % RX], 16 * (e // RX + 1))
                    nc.gpsimd.tensor_tensor(xt[:, e % RX, :], xt[:, e % RX, :], bias_b[:, :], ALU.add).then_inc(x_biased, 1)

                pool.wait_ge(ln_ready, 2)
                bias(0)
                for e in range(NE + 2):
                    if e < NE:
                        pool.wait_ge(mv1_ready, e + 1)
                        moments(mv1, rs1, e, 1e-6, rs1_ready)
                    if e >= 2:
                        pool.wait_ge(mv2_ready, e - 1)
                        moments(mv2, rs2, e - 2, 1e-5, rs2_ready)
                    if e < NE:
                        pool.wait_ge(z_ready, e + 1)
                        nc.gpsimd.tensor_tensor(z[:, e % 2, :], z[:, e % 2, :], scale_b[:, :], ALU.mult).then_inc(z_scaled, 1)
                    if e + 1 < NE:
                        bias(e + 1)

            @block.scalar
            def _(act):
                def split(e):
                    act.wait_ge(a_in[e % RA], 16 * (e // RA + 1))
                    if e >= RA:
                        act.wait_ge(out_ready, e - RA + 1)
                    nc.scalar.activation(ah[:, e % RA], aland[:, e % RA], ACT.Copy).then_inc(a_hi, 1)

                for kt in range(KI):
                    act.wait_ge(w_in[2 * kt // KI], 16)
                    nc.scalar.activation(wh[:, kt, :], wland[:, kt, :], ACT.Copy).then_inc(w_hi, 1)
                    if kt == KI // 2 - 1:
                        split(0)
                split(1)
                for e in range(NE + 3):
                    if e < NE:
                        act.wait_ge(rs1_ready, e + 1)
                        if e >= 2:
                            act.wait_ge(x_new, e - 1)
                        nc.scalar.activation(z[:, e % 2, :], psum[0:TT, e % 4, :], ACT.Identity,
                                             bias=rs1[:, e % 2, 1:2], scale=rs1[:, e % 2, 0:1]).then_inc(z_ready, 1)
                    if e + 2 < NE:
                        split(e + 2)
                    if e >= 3:
                        k = e - 3
                        act.wait_ge(tr_ready, k + 1)
                        nc.scalar.activation(y_all[:, :, TT * k:TT * (k + 1)],
                                             psum[:, 4 + k % 2, 0:KD * TT].rearrange("p (k t) -> p k t", k=KD),
                                             ACT.Copy).then_inc(tr_read, 1)
                    if 2 <= e <= NE + 1:
                        k = e - 2
                        act.wait_ge(rs2_ready, k + 1)
                        if k >= 2:
                            act.wait_ge(max_done, k - 1)
                            act.wait_ge(tr_ready, k - 1)
                        nc.scalar.activation(y[:, k % 2, :], xt[:, k % RX, :], ACT.Identity,
                                             bias=rs2[:, k % 2, 1:2], scale=rs2[:, k % 2, 0:1]).then_inc(y_ready, 1)

            @block.vector
            def _(dve):
                v = nc.vector
                own = Chain(dve, dve_own)

                def split(e):
                    dve.wait_ge(a_hi, e + 1)
                    v.tensor_tensor(al[:, e % RA], aland[:, e % RA], f(ah[:, e % RA]), ALU.subtract).then_inc(a_lo, 1)

                own.step(v.memset(ymax[:, :], 0.0))
                own.wait()
                for kt in range(KI):
                    dve.wait_ge(w_hi, kt + 1)
                    v.tensor_tensor(wl[:, kt, :], wland[:, kt, :], f(wh[:, kt, :]), ALU.subtract).then_inc(w_lo, 1)
                    if kt == KI // 2 - 1:
                        split(0)
                split(1)
                dve.wait_ge(const_in, 32)
                for tile in (scale_b, bias_b):
                    v.tensor_scalar(tile[:, :], tile[:, :], tg[0:TT, 1:2], None, ALU.mult).then_inc(ln_ready, 1)
                for e in range(NE + 3):
                    if e < NE:
                        dve.wait_ge(out_ready, e + 1)
                        own.step(v.bn_stats(st1[:, e % 2, :], psum[0:TT, e % 4, :]))
                        own.wait()
                        if e >= 2:
                            dve.wait_ge(rs1_ready, e - 1)
                        v.bn_aggr(mv1[:, e % 2, :], st1[:, e % 2, :]).then_inc(mv1_ready, 1)
                        if e + 2 < NE:
                            split(e + 2)
                    if e >= 3:
                        k = e - 3
                        dve.wait_ge(y_ready, k + 1)
                        v.tensor_reduce(ymax[0:TT, k:k + 1], y[:, k % 2, :], AX.X, ALU.max, apply_absolute_value=True
                                        ).then_inc(max_done, 1)
                    if 1 <= e <= NE:
                        k = e - 1
                        x = xt[:, k % RX, :]
                        dve.wait_ge(z_scaled, k + 1)
                        dve.wait_ge(x_biased, k + 1)
                        v.tensor_tensor(x, x, z[:, k % 2, :], ALU.add).then_inc(x_new, 1)
                        dve.wait_ge(x_new, k + 1)
                        own.step(v.bn_stats(st2[:, k % 2, :], x))
                        own.wait()
                        v.bn_aggr(mv2[:, k % 2, :], st2[:, k % 2, :]).then_inc(mv2_ready, 1)

            @block.tensor
            def _(pe):
                for e in range(NE + 3):
                    if e < NE:
                        pe.wait_ge(a_lo, e + 1)
                        if e >= 4:
                            pe.wait_ge(z_ready, e - 3)
                        for kt in range(KI):
                            if e == 0:
                                pe.wait_ge(w_lo, kt + 1)
                            ins = three(nc, psum[0:TT, e % 4, :], ah[:, e % RA, kt, :], al[:, e % RA, kt, :],
                                        wh[:, kt, :], wl[:, kt, :], kt == 0, kt == KI - 1)
                        ins.then_inc(out_ready, 1)
                    if e >= 3:
                        k = e - 3
                        pe.wait_ge(y_ready, k + 1)
                        if k >= 2:
                            pe.wait_ge(tr_read, k - 1)
                        for kt in range(KD):
                            ins = nc.tensor.transpose(psum[:, 4 + k % 2, TT * kt:TT * (kt + 1)],
                                                      y[:, k % 2, P * kt:P * (kt + 1)], ident[0:TT, 0:TT])
                        ins.then_inc(tr_ready, 1)


def overall_scale(nc, m, name, maxima, scale, inverse, factor=None):
    top, all_top, steps, reduced = m.sb(f"{name}_top", [P, 1]), m.sb(f"{name}_all", [P, 1]), m.sem(f"{name}_steps"), m.sem(f"{name}_red")

    def on_pool(pool):
        pool.wait_ge(steps, 1)
        nc.gpsimd.partition_all_reduce(all_top[:, :], top[:, :], P, RMAX).then_inc(reduced, 1)

    def on_vector(dve):
        v = nc.vector
        v.tensor_reduce(top[:, :], maxima, AX.X, ALU.max).then_inc(steps, 1)
        dve.wait_ge(reduced, 1)
        n = 1
        if factor is not None:
            v.tensor_tensor(all_top[:, :], all_top[:, :], factor, ALU.mult).then_inc(steps, 1)
            n += 1
            dve.wait_ge(steps, n)
        v.tensor_scalar(scale, all_top[:, :], float(np.float32(1.0) / np.float32(QMAX)), 1e-12, ALU.mult, ALU.max
                        ).then_inc(steps, 1)
        dve.wait_ge(steps, n + 1)
        v.reciprocal(inverse, scale).then_inc(steps, 1)
        dve.wait_ge(steps, n + 2)
        if factor is not None:
            v.tensor_tensor(inverse, inverse, factor, ALU.mult).then_inc(steps, 1)
            dve.wait_ge(steps, n + 3)

    return on_pool, on_vector, steps


def phase_project(nc, psum, g_, y_all, d, ymax, umax, g2max):
    with Mem(nc, "p6a") as m:
        land = m.sb("land", [P, 2, KD, P])
        wh, wl = m.sb("wh", [P, 2, KD, P], F32R), m.sb("wl", [P, 2, KD, P], F32R)
        yh, yl = m.sb("yh", [P, KD, T], F32R), m.sb("yl", [P, KD, T], F32R)
        sig = m.sb("sig", [P, T])
        sy, iy, sg, ig = (m.sb(n, [P, 1]) for n in ("sy", "iy", "sg", "ig"))
        gmax = m.sb("gmax", [P, NI1])
        s = m.sem
        w_in, w_hi, w_lo = [s("w_in0"), s("w_in1")], s("w_hi"), s("w_lo")
        y_scaled, y_hi, y_lo = s("y_scaled"), s("y_hi"), s("y_lo")
        o_ready, o_read, g_max, u_max = s("o_ready"), s("o_read"), s("g_max"), s("u_max")
        u_out = [s(f"u_out{i}") for i in range(RU)]
        act_held, dve_held = s("act_held"), s("dve_held")
        g_scaled, g_whole, sig_ready, sig_own, sig_whole, silu_done, g2_max = (
            s("g_scaled"), s("g_whole"), s("sig_ready"), s("sig_own"), s("sig_whole"), s("silu_done"), s("g2_max"))
        y_pool, y_vector, y_steps = overall_scale(nc, m, "y", ymax[:, :], sy[:, :], iy[:, :])
        g_pool, g_vector, g_steps = overall_scale(nc, m, "g", gmax[:, :], sg[:, :], ig[:, :])
        NE = 2 * NI1
        RB = 2 * NC

        def up_tile(r):
            return y_all[:, r % RU, :]

        with nc.Block() as block:
            @block.sync
            def _(sp):
                for e in range(NE):
                    if e >= 2:
                        sp.wait_ge(w_lo, e - 1 + 2)
                    it, k0 = e % NI1, KD * (e // NI1)
                    sp.dma_start(land[:, e % 2],
                                 d["wdq"][k0:k0 + KD, :, P * it:P * (it + 1)].rearrange("k p n -> p k n")
                                 ).then_inc(w_in[e % 2], 16)

            @block.gpsimd
            def _(pool):
                y_pool(pool)
                g_pool(pool)
                own = Chain(pool, sig_own)
                for t in range(NI1):
                    pool.wait_ge(sig_ready, t + 1)
                    own.step(nc.gpsimd.tensor_scalar(sig[:, :], sig[:, :], 65536.0, MAGIC, ALU.mult, ALU.add))
                    own.wait()
                    nc.gpsimd.tensor_scalar(sig[:, :], sig[:, :], -MAGIC, 65535.0, ALU.add, ALU.min).then_inc(sig_whole, 1)

            @block.scalar
            def _(act):
                def hi(e, par, turn):
                    act.wait_ge(w_in[par], turn * 16 + 16)
                    act.wait_ge(o_ready, e * NC + NC)
                    nc.scalar.activation(wh[:, par], land[:, par], ACT.Copy).then_inc(w_hi, 1)

                def read(e, par, out):
                    for c in range(NC):
                        act.wait_ge(o_ready, e * NC + (c + 1 + RB))
                        hold(act, act_held)
                        nc.scalar.activation(out(c), psum[:, NC * par + c, 0:CH], ACT.Identity, scale=sy[:, :]
                                             ).then_inc(o_read, 1)

                act.sem_inc(o_read, RB)
                act.sem_inc(o_ready, RB)
                for i in range(RU):
                    act.sem_inc(u_out[i], 16)
                hi(0, 0, 0)
                act.wait_ge(y_steps, 3)
                for c in range(NC):
                    chunk = slice(CH * c, CH * (c + 1))
                    nc.scalar.activation(y_all[:, :, chunk], y_all[:, :, chunk], ACT.Copy, bias=MAGIC, scale=iy[:, :]
                                         ).then_inc(y_scaled, 1)
                    act.wait_ge(y_scaled, c + 1)
                    nc.scalar.activation(yh[:, :, chunk], y_all[:, :, chunk], ACT.Copy, bias=-MAGIC).then_inc(y_hi, 1)
                with act.Fori(0, NI1 // 2) as i:
                    for par in (0, 1):
                        it = i * 2 + par
                        hi(it + 1, 1 - par, i + par)
                        read(it, par, lambda c: g_[:, bass.ds(it, 1), CH * c:CH * (c + 1)].rearrange("p a t -> p (a t)"))
                act.wait_ge(g_steps, 3)

                def up_turn(g, r, store, more):
                    it, par = g * RU + r, r % 2
                    e = it + NI1
                    gate = g_[:, bass.ds(it, 1), :].rearrange("p a t -> p (a t)")
                    nc.scalar.activation(gate, gate, ACT.Copy, bias=MAGIC, scale=ig[:, :]).then_inc(g_scaled, 1)
                    if more:
                        hi(e + 1, 1 - par, g * (RU // 2) + (NI1 + r + 1) // 2)
                    act.wait_ge(u_out[r], g * 16 + 16)
                    act.wait_ge(u_max, it + 1)
                    read(e, par, lambda c: up_tile(r)[:, CH * c:CH * (c + 1)])
                    act.wait_ge(g_whole, it + 1)
                    act.wait_ge(silu_done, it + 1)
                    hold(act, act_held)
                    nc.scalar.activation(sig[:, :], gate, ACT.Sigmoid).then_inc(sig_ready, 1)
                    if store:
                        act.wait_ge(o_read, e * NC + (NC + RB))
                        act.dma_start(d["upT"][bass.ds(it * P, P), :], up_tile(r)).then_inc(u_out[r], 16)

                act.wait_ge(y_lo, NC)
                with act.Fori(0, NI1 // RU - 1) as g:
                    for r in range(RU):
                        up_turn(g, r, True, True)
                for r in range(RU):
                    up_turn(NI1 // RU - 1, r, False, r < RU - 1)
                for i in range(RU):
                    act.wait_ge(u_out[i], 16 * (NI1 // RU))

            @block.vector
            def _(dve):
                v = nc.vector

                def lo(e, par):
                    dve.wait_ge(w_hi, e + 1)
                    v.tensor_tensor(wl[:, par], land[:, par], f(wh[:, par]), ALU.subtract).then_inc(w_lo, 1)

                def gate_tile(it):
                    return g_[:, bass.ds(it, 1), :].rearrange("p a t -> p (a t)")

                def silu(it):
                    g = gate_tile(it)
                    dve.wait_ge(sig_whole, it + 1)
                    v.scalar_tensor_tensor(out=g, in0=sig[:, :], scalar=2.0 ** -16, in1=g, op0=ALU.mult, op1=ALU.mult
                                           ).then_inc(silu_done, 1)
                    dve.wait_ge(silu_done, it + (1 + 1))
                    hold(dve, dve_held)
                    v.tensor_reduce(g2max[:, bass.ds(it, 1)], g, AX.X, ALU.max, apply_absolute_value=True
                                    ).then_inc(g2_max, 1)

                dve.sem_inc(w_lo, 2)
                dve.sem_inc(u_max, RU)
                dve.sem_inc(silu_done, 1)
                y_vector(dve)
                lo(0, 0)
                for c in range(NC):
                    chunk = slice(CH * c, CH * (c + 1))
                    dve.wait_ge(y_hi, c + 1)
                    v.scalar_tensor_tensor(out=yl[:, :, chunk], in0=y_all[:, :, chunk], scalar=-MAGIC,
                                           in1=f(yh[:, :, chunk]), op0=ALU.add, op1=ALU.subtract).then_inc(y_lo, 1)
                with dve.Fori(0, NI1 // 2) as i:
                    for par in (0, 1):
                        it = i * 2 + par
                        lo(it + 1, 1 - par)
                        dve.wait_ge(o_read, it * NC + (NC + RB))
                        hold(dve, dve_held)
                        v.tensor_reduce(gmax[:, bass.ds(it, 1)], gate_tile(it), AX.X, ALU.max,
                                        apply_absolute_value=True).then_inc(g_max, 1)
                dve.wait_ge(g_max, NI1)
                g_vector(dve)

                def up_turn(g, r, first, more):
                    it, par = g * RU + r, r % 2
                    gate = gate_tile(it)
                    dve.wait_ge(g_scaled, it + 1)
                    v.tensor_scalar(gate, gate, -MAGIC, sg[:, :], ALU.add, ALU.mult).then_inc(g_whole, 1)
                    if more:
                        lo(it + (NI1 + 1), 1 - par)
                    if not first:
                        silu(it - 1)
                    dve.wait_ge(o_read, it * NC + (NI1 * NC + NC + RB))
                    hold(dve, dve_held)
                    v.tensor_reduce(umax[:, bass.ds(it, 1)], up_tile(r), AX.X, ALU.max,
                                    apply_absolute_value=True).then_inc(u_max, 1)

                for r in range(RU):
                    up_turn(0, r, r == 0, True)
                with dve.Fori(1, NI1 // RU - 1) as g:
                    for r in range(RU):
                        up_turn(g, r, False, True)
                for r in range(RU):
                    up_turn(NI1 // RU - 1, r, False, r < RU - 1)
                silu(NI1 - 1)

            @block.tensor
            def _(pe):
                with pe.Fori(0, NE // 2) as i:
                    for par in (0, 1):
                        e = i * 2 + par
                        pe.wait_ge(w_lo, e + 1 + 2)
                        for c in range(NC):
                            pe.wait_ge(y_lo, c + 1)
                            pe.wait_ge(o_read, e * NC + c + 1)
                            for kt in range(KD):
                                chunk = slice(CH * c, CH * (c + 1))
                                ins = three(nc, psum[:, NC * par + c, 0:CH], wh[:, par, kt, :], wl[:, par, kt, :],
                                            yh[:, kt, chunk], yl[:, kt, chunk], kt == 0, kt == KD - 1)
                            ins.then_inc(o_ready, 1)


def phase_mix_down(nc, psum, g_, u, tg, d, umax, g2max):
    with Mem(nc, "p6b") as m:
        land = m.sb("land", [P, FF1])
        wh, wl = m.sb("wh", [P, NI1, D], F32R), m.sb("wl", [P, NI1, D], F32R)
        ow = m.sb("ow", [P, NI1, TT])
        ohi, olo = m.sb("ohi", [P, 2, NI1, TT], F32R), m.sb("olo", [P, 2, NI1, TT], F32R)
        xt = m.sb("xt", [TT, NT, D])
        omax = m.sb("omax", [P, NI1])
        su, iu, s2, i2, so, io, su2, tgo = (m.sb(n, [P, 1]) for n in ("su", "iu", "s2", "i2", "so", "io", "su2", "tgo"))
        s = m.sem
        w_in, w_hi, w_lo, u_in = s("w_in"), s("w_hi"), s("w_lo"), [s(f"u_in{i}") for i in range(RU)]
        scales, g_scaled, u_scaled, u_whole, mixed, o_max, tgo_ready = (
            s("scales"), s("g_scaled"), s("u_scaled"), s("u_whole"), s("mixed"), s("o_max"), s("tgo_ready"))
        x_in, x_out = [s(f"x_in{i}") for i in range(NT)], [s(f"x_out{i}") for i in range(NT)]
        o_scaled, o_hi, o_lo, out_ready, x_new = s("o_scaled"), s("o_hi"), s("o_lo"), s("out_ready"), s("x_new")
        act_held = s("act_held")
        u_pool, u_vector, u_steps = overall_scale(nc, m, "um", umax[:, :], su[:, :], iu[:, :])
        g_pool, g_vector, g_steps = overall_scale(nc, m, "gm", g2max[:, :], s2[:, :], i2[:, :])
        o_pool, o_vector, o_steps = overall_scale(nc, m, "om", omax[:, :], so[:, :], io[:, :], su2[:, :])
        WS = NI1 // 3
        order = list(range(NI1 - RU, NI1)) + list(range(NI1 - RU))

        with nc.Block() as block:
            @block.sync
            def _(sp):
                def rows(name, c, n):
                    return d[name][CH * c + TT * n:CH * c + TT * (n + 1), :]

                sp.dma_start(land[:, :], d["wdq"][2 * KD]).then_inc(w_in, 16)
                for n in range(NT):
                    sp.dma_start(xt[:, n, :], rows("x3", 0, n)).then_inc(x_in[n], 16)
                for j in range(RU, NI1):
                    sp.wait_ge(mixed, j - RU + 1)
                    sp.dma_start(u[:, j % RU, :], d["upT"][P * order[j]:P * (order[j] + 1), :]).then_inc(u_in[j % RU], 16)
                    t = j - RU + 1
                    if t < WS:
                        sp.wait_ge(w_lo, t)
                        sp.dma_start(land[:, :], d["wdq"][2 * KD + t]).then_inc(w_in, 16)
                for c in range(NC):
                    for n in range(NT):
                        sp.wait_ge(x_new, NT * c + n + 1 + NT)
                        sp.dma_start(rows("out", c, n), xt[:, n, :]).then_inc(x_out[n], 16)
                        sp.wait_ge(x_out[n], 16 * (c + 1))
                        if c + 1 < NC:
                            sp.dma_start(xt[:, n, :], rows("x3", c + 1, n)).then_inc(x_in[n], 16)

            @block.gpsimd
            def _(pool):
                g_pool(pool)
                u_pool(pool)
                for j in range(NI1):
                    ut = u[:, j % RU, :]
                    pool.wait_ge(u_scaled, j + 1)
                    nc.gpsimd.tensor_scalar(ut, ut, -MAGIC, 1.0, ALU.add, ALU.mult).then_inc(u_whole, 1)
                o_pool(pool)

            @block.scalar
            def _(act):
                for j, t in enumerate(order):
                    ut = u[:, j % RU, :]
                    if j == 0:
                        act.wait_ge(scales, 1)
                    if j >= RU:
                        act.wait_ge(u_in[j % RU], 16 * (j // RU))
                    nc.scalar.activation(ut, ut, ACT.Copy, bias=MAGIC, scale=iu[:, :]).then_inc(u_scaled, 1)
                    nc.scalar.activation(g_[:, t, :], g_[:, t, :], ACT.Copy, bias=MAGIC, scale=i2[:, :]).then_inc(g_scaled, 1)
                    if 1 <= j <= WS:
                        act.wait_ge(w_in, 16 * j)
                        nc.scalar.activation(wh[:, 3 * j - 3:3 * j, :].rearrange("p k n -> p (k n)"), land[:, :], ACT.Copy
                                             ).then_inc(w_hi, 1)
                act.sem_inc(out_ready, 2)
                act.sem_inc(o_lo, 1)
                act.wait_ge(o_steps, 5)
                with act.Fori(0, NC) as c:
                    for n in range(NT):
                        act.wait_ge(o_lo, c * NT + n + 1)
                        hold(act, act_held)
                        nc.scalar.activation(ow[:, :, :], g_[:, :, bass.ds(c * CH + n * TT, TT)], ACT.Copy,
                                             bias=MAGIC, scale=io[:, :]).then_inc(o_scaled, 1)
                        act.wait_ge(o_scaled, c * NT + n + 1)
                        act.wait_ge(out_ready, c * NT + n + 1)
                        nc.scalar.activation(ohi[:, n % 2], ow[:, :, :], ACT.Copy, bias=-MAGIC).then_inc(o_hi, 1)

            @block.vector
            def _(dve):
                v = nc.vector
                g_vector(dve)
                u_vector(dve)
                v.tensor_tensor(su2[:, :], su[:, :], s2[:, :], ALU.mult).then_inc(scales, 1)
                for j, t in enumerate(order):
                    dve.wait_ge(g_scaled, j + 1)
                    dve.wait_ge(u_whole, j + 1)
                    v.scalar_tensor_tensor(out=g_[:, t, :], in0=g_[:, t, :], scalar=-MAGIC, in1=u[:, j % RU, :],
                                           op0=ALU.add, op1=ALU.mult).then_inc(mixed, 1)
                    dve.wait_ge(mixed, j + 1)
                    v.tensor_reduce(omax[:, t:t + 1], g_[:, t, :], AX.X, ALU.max, apply_absolute_value=True
                                    ).then_inc(o_max, 1)
                    if 1 <= j <= WS:
                        dve.wait_ge(w_hi, j)
                        v.tensor_tensor(wl[:, 3 * j - 3:3 * j, :].rearrange("p k n -> p (k n)"), land[:, :],
                                        f(wh[:, 3 * j - 3:3 * j, :]).rearrange("p k n -> p (k n)"), ALU.subtract
                                        ).then_inc(w_lo, 1)
                dve.wait_ge(o_max, NI1)
                dve.wait_ge(scales, 1)
                o_vector(dve)
                v.tensor_tensor(tgo[:, :], tg[:, 3:4], so[:, :], ALU.mult).then_inc(tgo_ready, 1)
                dve.wait_ge(tgo_ready, 1)
                dve.sem_inc(x_new, NT)

                def lo(e, par):
                    dve.wait_ge(o_hi, e + 1)
                    v.scalar_tensor_tensor(out=olo[:, par], in0=ow[:, :, :], scalar=-MAGIC, in1=f(ohi[:, par]),
                                           op0=ALU.add, op1=ALU.subtract).then_inc(o_lo, 1)

                def close(e, n, turn):
                    dve.wait_ge(out_ready, e + (1 + 2))
                    dve.wait_ge(x_in[n], turn * 16 + 16)
                    v.scalar_tensor_tensor(out=xt[:, n, :], in0=psum[0:TT, n, :], scalar=tgo[0:TT, :], in1=xt[:, n, :],
                                           op0=ALU.mult, op1=ALU.add).then_inc(x_new, 1)

                lo(0, 0)
                with dve.Fori(0, NC - 1) as c:
                    for n in range(NT):
                        lo(c * NT + (n + 1), (n + 1) % 2)
                        close(c * NT + n, n, c)
                for n in range(NT):
                    e = (NC - 1) * NT + n
                    if n < NT - 1:
                        lo(e + 1, (n + 1) % 2)
                    close(e, n, NC - 1)

            @block.tensor
            def _(pe):
                pe.wait_ge(w_lo, WS)
                with pe.Fori(0, NC) as c:
                    for n in range(NT):
                        pe.wait_ge(o_lo, c * NT + (n + 1 + 1))
                        pe.wait_ge(x_new, c * NT + n + 1)
                        for kt in range(NI1):
                            ins = three(nc, psum[0:TT, n, :], ohi[:, n % 2, kt, :], olo[:, n % 2, kt, :],
                                        wh[:, kt, :], wl[:, kt, :], kt == 0, kt == NI1 - 1)
                        ins.then_inc(out_ready, 1)


def phase_quantised_ffn(nc, psum, tg, ymax, y_all, d):
    with Mem(nc, "p6") as m:
        g_ = m.sb("gate", [P, NI1, T])
        umax, g2max = m.sb("umax", [P, NI1]), m.sb("g2max", [P, NI1])
        phase_project(nc, psum, g_, y_all, d, ymax, umax, g2max)
        phase_mix_down(nc, psum, g_, y_all, tg, d, umax, g2max)


def build(nc, d):
    with Mem(nc, "all") as m:
        psum = m.stack.enter_context(nc.psum_tensor("psum", [P, 8, 512], F32))
        ident = m.sb("ident", [P, P])
        tg = m.sb("tg", [P, 4])
        phase_depool(nc, psum, ident, tg, d)
        phase_relu_ffn(nc, psum, ident, tg, d)
        phase_queries(nc, psum, ident, tg, d)
        phase_attention(nc, psum, ident, d)
        ymax, y_all = m.sb("ymax", [P, NC * NT]), m.sb("y_all", [P, KD, T])
        phase_attention_out(nc, psum, ident, tg, ymax, y_all, d)
        phase_quantised_ffn(nc, psum, tg, ymax, y_all, d)


SCRATCH = {"x1": [T, D], "x2": [T, D], "qT": [INNER, T], "wdq": [3 * KD, P, FF1], "aT": [INNER, T],
           "x3": [T, D], "upT": [FF1, T]}


def kernel(**a):
    import numpy as np
    import concourse.bacc as bacc
    from concourse import mybir as mb
    from concourse.bass_utils import run_bass_kernel_spmd as run

    def cols(v, n):
        return v.reshape(n, 128).T

    def blocks(w):
        o, i = w.shape
        return w.reshape(o // QB, QB, i // P, 4, QB).transpose(2, 3, 1, 0, 4).reshape(i // P, P, o)

    down = blocks(a["L1_ffn_w_down"])
    down = down.reshape(KD, 3, P, D).transpose(0, 2, 1, 3).reshape(KD, P, 3 * D)
    arrays = {
        "x": a["x"].reshape(T, D), "ctx": a["ctx_2048"], "ctx_t": a["ctx_2048"].transpose(0, 2, 1),
        "lens": a["mask_BxS2_if0"], "gates": np.concatenate([a["g_xattn"], a["g_ffn"]]),
        "w_in_t": a["L0_xattn_W_in"].T, "b_in": a["L0_xattn_b_in"],
        "g_res_cols": cols(a["L0_xattn_g_res"], KD), "g_init": a["L0_xattn_g_init"],
        "w1": a["L0_ffn_W1"], "b1_cols": cols(a["L0_ffn_b1"], NI0), "w2": a["L0_ffn_W2"], "b2": a["L0_ffn_b2"],
        "w_q": np.concatenate([blocks(a["L1_ffn_w_gate"]), blocks(a["L1_ffn_w_up"]), down]),
        "wq": a["L1_xattn_Wq"], "wkv": a["L1_xattn_Wkv"], "null_kv": a["L1_xattn_null_kv"], "wout": a["L1_xattn_Wout"],
        "ln_scale": a["L1_xattn_ln_scale"], "ln_bias": a["L1_xattn_ln_bias"],
    }
    nc = bacc.Bacc("TRN2", target_bir_lowering=False, num_devices=1)
    arrays = {k: np.ascontiguousarray(v) for k, v in arrays.items()}
    d = {k: nc.dram_tensor(f"in_{k}", v.shape, mb.dt.from_np(v.dtype), kind="ExternalInput").ap() for k, v in arrays.items()}
    for k, shape in SCRATCH.items():
        d[k] = nc.dram_tensor(f"scratch_{k}", shape, mb.dt.float32, kind="Internal").ap()
    d["out"] = nc.dram_tensor("out", [T, D], mb.dt.float32, kind="ExternalOutput").ap()
    build(nc, d)
    r = run(nc, [{f"in_{k}": v for k, v in arrays.items()}], core_ids=[0])
    return r.results[0]["out"].reshape(B, S, D)
```

```python
import numpy as np
import concourse.bass as bass
from concourse import mybir
from contextlib import ExitStack

F32 = mybir.dt.float32
F32R = mybir.dt.float32r
BF16 = mybir.dt.bfloat16
I32 = mybir.dt.int32
ALU = mybir.AluOpType
ACT = mybir.ActivationFunctionType
AX = mybir.AxisListType
RMAX = bass.bass_isa.ReduceOp.max

P = 128
B, S, D = 8, 224, 512
M, DC = 750, 1024
T = B * S
TT = 112
NT = 4
CH = NT * TT
NC = T // CH
KD = D // P
KC = DC // P
FF0 = 2048
NI0 = FF0 // P
FF1 = 1536
NI1 = FF1 // P
H, DH = 16, 64
INNER = H * DH
RU = KD
QB = 32
MAGIC = 1.5 * 2.0 ** 23
LOGP = np.float32(-0.001)
DT = float(np.float32(-np.log(-np.expm1(LOGP))))
BCOEF = float(np.exp(LOGP))
QMAX = 32767.0


class Chain:

    def __init__(self, eng, sem, per=0):
        self.eng, self.sem, self.per, self.base, self.n = eng, sem, per, 0, 0

    def at(self, turn):
        self.base, self.n = turn * self.per, 0

    def step(self, ins):
        self.n += 1
        return ins.then_inc(self.sem, 1)

    def wait(self):
        self.eng.wait_ge(self.sem, self.base + self.n)

    def done(self):
        assert self.n == self.per, (self.n, self.per)


class Mem:

    def __init__(self, nc, name):
        self.nc, self.name, self.stack, self.sems = nc, name, ExitStack(), []

    def __enter__(self):
        self.stack.__enter__()
        return self

    def __exit__(self, *a):
        if self.sems:
            self.nc.clear_and_free_semaphores(self.sems)
            self.nc.all_engine_barrier()
        return self.stack.__exit__(*a)

    def sb(self, name, shape, dtype=F32):
        return self.stack.enter_context(self.nc.sbuf_tensor(f"{self.name}_{name}", shape, dtype))

    def landing(self, name, shape):
        with self.nc.sbuf_tensor(f"{self.name}_{name}_raw", shape, F32) as raw:
            pass
        return raw, self.sb(name, shape, F32R)

    def sem(self, name):
        self.sems.append(self.nc.alloc_semaphore(f"{self.name}_{name}"))
        return self.sems[-1]


def f(ap):
    return ap.bitcast(F32)


def hold(eng, held):
    eng.sem_inc(held, 1)


def three(nc, out, a_hi, a_lo, b_hi, b_lo, first, last):
    nc.tensor.matmul(out, a_hi, b_hi, start=first, stop=False)
    nc.tensor.matmul(out, a_hi, b_lo, start=False, stop=False)
    return nc.tensor.matmul(out, a_lo, b_hi, start=False, stop=last)


def phase_depool(nc, psum, ident, tg, d):
    RX = 3
    with Mem(nc, "p1") as m:
        wland = m.sb("wland", [P, KD, D])
        wh, wl = m.sb("wh", [P, KD, D], F32R), m.sb("wl", [P, KD, D], F32R)
        brow, bh, bl = m.sb("brow", [1, D]), m.sb("bh", [1, D], F32R), m.sb("bl", [1, D], F32R)
        one_row = m.sb("one_row", [1, TT], F32R)
        gin_b = m.sb("gin_b", [TT, D])
        gres = m.sb("gres", [P, KD])
        graw = m.sb("graw", [P, 4])
        lens = m.sb("lens", [B, M], I32)
        lensf, zeros, cum = (m.sb(n, [B, M]) for n in ("lensf", "zeros", "cum"))
        wrap, idx = zeros, lensf
        JP, JC = 125, M // 125
        idxT = m.sb("idxT", [JP, JC, B])
        ti = m.sb("ti", [P, S], I32)
        tf = m.sb("tf", [P, S])
        si = m.sb("si", [P, 2], I32)
        scol = m.sb("scol", [P, 2])
        eq = m.sb("eq", [JP, 2, JC, 2, S], BF16)
        ones = m.sb("ones", [JP, P], BF16)
        mark, plug = m.sb("mark", [P, B, S]), m.sb("plug", [P, B, S])
        zrow = m.sb("zrow", [P, S])
        xt = m.sb("xt", [TT, RX, NT, D])
        ctxn = m.sb("ctxn", [TT, NT, DC])
        junk = m.sb("junk", [TT, DC], BF16)
        ssq, rsc = m.sb("ssq", [TT, NT]), m.sb("rsc", [TT, 2, NT])
        uh, ul = m.sb("uh", [TT, 2, NT, D], F32R), m.sb("ul", [TT, 2, NT, D], F32R)
        u32 = wland
        dist, far = m.sb("dist", [TT, 2, CH]), m.sb("far", [TT, 2, CH])
        mh, ml = m.sb("mh", [TT, 2, 2, CH], F32R), m.sb("ml", [TT, 2, 2, CH], F32R)
        stats, mv = m.sb("stats", [TT, NT, 6]), m.sb("mv", [TT, NT, 2])
        ve, rs, rr = m.sb("ve", [TT, NT]), m.sb("rs", [TT, NT]), m.sb("rr", [TT, NT])
        nhalf, c_eps, c_dc, c_in = (m.sb(n, [TT, NT]) for n in ("nhalf", "c_eps", "c_dc", "c_in"))
        y = m.sb("y", [TT, NT, D])
        yh, yl = m.sb("yh", [P, 2, KD, CH], F32R), m.sb("yl", [P, 2, KD, CH], F32R)

        s = m.sem
        const_in, w_in, lens_in = s("const_in"), s("w_in"), s("lens_in")
        ctx_in, x_in, x_out = s("ctx_in"), [s(f"x_in{i}") for i in range(RX)], s("x_out")
        pool_c, pool_own, dve_own = s("pool_c"), s("pool_own"), s("dve_own")
        idx_ready, idx_t, eq_ready, count_ready = s("idx_ready"), s("idx_t"), s("eq_ready"), s("count_ready")
        tanh_ready, w_scaled, w_hi, w_lo, b_hi, b_lo = (
            s("tanh_ready"), s("w_scaled"), s("w_hi"), s("w_lo"), s("b_hi"), s("b_lo"))
        mark_ready = s("mark_ready")
        var_ready, rstd_ready, y_ready, tr_ready, tr_hi, y_split = (
            s("var_ready"), s("rstd_ready"), s("y_ready"), s("tr_ready"), s("tr_hi"), s("y_split"))
        ssq_ready, rsc_ready, u_scaled, u_hi, u_split = s("ssq_ready"), s("rsc_ready"), s("u_scaled"), s("u_hi"), s("u_split")
        dist_ready, exp_ready, m_hi, m_split = s("dist_ready"), s("exp_ready"), s("m_hi"), s("m_split")
        out_ready, x_new = s("out_ready"), s("x_new")

        with nc.Block() as block:
            @block.sync
            def _(sp):
                def load_x(c):
                    sp.dma_start(xt[:, c % RX], d["x"][CH * c:CH * (c + 1), :].rearrange("(n p) d -> p n d", p=TT)
                                 ).then_inc(x_in[c % RX], 16)

                def load_ctx(c):
                    for b in range(2):
                        src = d["ctx"][2 * c + b, 0:S, :].rearrange("(n p) d -> p n d", p=TT)
                        sp.dma_start(ctxn[:, 2 * b:2 * b + 2, :], src).then_inc(ctx_in, 16)

                sp.dma_start(lens[:, :], d["lens"]).then_inc(lens_in, 16)
                load_x(0)
                sp.dma_start(wland[:, :, :], d["w_in_t"].rearrange("(k p) n -> p k n", p=P)).then_inc(w_in, 16)
                sp.dma_start(gres[:, :], d["g_res_cols"]).then_inc(w_in, 16)
                sp.dma_start(graw[:, :], d["gates"].partition_broadcast(P)).then_inc(const_in, 16)
                sp.dma_start(brow[:, :], d["b_in"].partition_broadcast(1)).then_inc(const_in, 16)
                sp.dma_start(gin_b[:, :], d["g_init"][0:D].partition_broadcast(TT)).then_inc(const_in, 16)
                load_ctx(0)
                load_x(1)
                load_x(2)
                for c in range(NC):
                    if c + 1 < NC:
                        sp.wait_ge(u_scaled, NT * (c + 1))
                        load_ctx(c + 1)
                    if c >= 1:
                        sp.wait_ge(x_new, NT * c)
                        sp.dma_start(d["x1"][CH * (c - 1):CH * c, :].rearrange("(n p) d -> p n d", p=TT),
                                     xt[:, (c - 1) % RX]).then_inc(x_out, 16)
                        if c - 1 + RX < NC:
                            sp.wait_ge(x_out, 16 * c)
                            load_x(c - 1 + RX)
                sp.wait_ge(x_new, NT * NC)
                sp.dma_start(d["x1"][CH * (NC - 1):T, :].rearrange("(n p) d -> p n d", p=TT), xt[:, (NC - 1) % RX]
                             ).then_inc(x_out, 16)
                sp.wait_ge(x_out, 16 * NC)

            @block.gpsimd
            def _(pool):
                g = nc.gpsimd
                own = Chain(pool, pool_own)
                g.memset(ident[:, :], 0.0).then_inc(pool_c, 1)
                pool.wait_ge(pool_c, 1)
                g.affine_select(out=ident[:, :], in_=ident[:, :], compare_op=ALU.not_equal, fill=1.0,
                                base=0, pattern=[[-1, P]], channel_multiplier=1).then_inc(pool_c, 1)
                g.iota(ti[:, :], [[1, S]], 0, 0).then_inc(pool_c, 1)
                g.iota(si[:, :], [[TT, 2]], 0, 1).then_inc(pool_c, 1)
                for tile, value in ((nhalf, -0.5), (c_eps, 1e-5), (c_dc, 1.0 / DC), (c_in, BCOEF)):
                    g.memset(tile[:, :], value).then_inc(pool_c, 1)
                pool.wait_ge(pool_c, 8)

                def step(out, a, b, op):
                    own.step(g.tensor_tensor(out[:, :], a, b[:, :], op))
                    own.wait()

                def rstd(c):
                    pool.wait_ge(var_ready, c + 1)
                    step(rs, ve[:, :], nhalf, ALU.pow)
                    step(rr, rs[:, :], rs, ALU.mult)
                    own.step(g.tensor_tensor(rr[:, :], rr[:, :], mv[:, :, 1], ALU.mult))
                    own.wait()
                    step(rr, rr[:, :], c_eps, ALU.add)
                    step(rr, rr[:, :], nhalf, ALU.pow)
                    g.tensor_tensor(rs[:, :], rs[:, :], rr[:, :], ALU.mult).then_inc(rstd_ready, 1)

                def rows(c):
                    for n in range(NT):
                        pool.wait_ge(ssq_ready, NT * c + n + 1)
                        if c:
                            pool.wait_ge(u_split, NT * (c - 1) + n + 1)
                        g.tensor_tensor(u32[0:TT, n, :], ctxn[:, n, 0:D], gin_b[:, :], ALU.mult).then_inc(u_scaled, 1)
                    i = c % 2
                    own.step(g.tensor_tensor(rsc[:, i, :], ssq[:, :], c_dc[:, :], ALU.mult))
                    own.wait()
                    own.step(g.tensor_tensor(rsc[:, i, :], rsc[:, i, :], c_eps[:, :], ALU.add))
                    own.wait()
                    own.step(g.tensor_tensor(rsc[:, i, :], rsc[:, i, :], nhalf[:, :], ALU.pow))
                    own.wait()
                    g.tensor_tensor(rsc[:, i, :], rsc[:, i, :], c_in[:, :], ALU.mult).then_inc(rsc_ready, 1)

                rstd(0)
                pool.wait_ge(const_in, 48)
                pool.wait_ge(w_lo, 1)
                for c in range(NC):
                    rows(c)
                    if c + 1 < NC:
                        rstd(c + 1)

            @block.scalar
            def _(act):
                a = nc.scalar.activation
                act.wait_ge(w_scaled, KD)
                a(wh[:, :, :], wland[:, :, :], ACT.Copy).then_inc(w_hi, 1)
                act.wait_ge(const_in, 48)
                a(bh[:, :], brow[:, :], ACT.Copy).then_inc(b_hi, 1)
                a(tg[:, :], graw[:, :], ACT.Tanh).then_inc(tanh_ready, 1)

                def squares(c):
                    act.wait_ge(ctx_in, c * 32 + 32)
                    if c:
                        act.wait_ge(rsc_ready, c)
                    for n in range(NT):
                        a(junk[:, :], ctxn[:, n, :], ACT.Square, accum_out=ssq[:, n:n + 1]).then_inc(ssq_ready, 1)
                        act.wait_ge(ssq_ready, c * NT + n + 1)

                def y_high(c, n):
                    act.wait_ge(tr_ready, c * NT + n + 1)
                    if c >= 2 and n == 0:
                        act.wait_ge(out_ready, NT * (c - 1))
                    a(yh[:, c % 2, :, TT * n:TT * (n + 1)], psum[:, n % 2, 0:KD * TT].rearrange("p (k t) -> p k t", k=KD),
                      ACT.Copy).then_inc(tr_hi, 1)

                def u_high(c, n):
                    if n == 0:
                        act.wait_ge(rsc_ready, c + 1)
                    a(uh[:, c % 2, n, :], u32[0:TT, n, :], ACT.Copy, scale=rsc[:, c % 2, n:n + 1]).then_inc(u_hi, 1)

                def matrix(c):
                    act.wait_ge(dist_ready, c + 1)
                    a(far[:, :, :], dist[:, :, :], ACT.Exp, scale=-DT).then_inc(exp_ready, 1)
                    act.wait_ge(exp_ready, c + 1)
                    if c >= 2:
                        act.wait_ge(out_ready, NT * (c - 1))
                    a(mh[:, c % 2], far[:, :, :], ACT.Copy).then_inc(m_hi, 1)

                for c in range(NC):
                    squares(c)
                    matrix(c)
                    for n in range(NT):
                        y_high(c, n)
                        u_high(c, n)

            @block.vector
            def _(dve):
                v = nc.vector
                own = Chain(dve, dve_own)
                own.step(v.memset(zeros[:, :], 0.0))
                own.step(v.memset(ones[:, :], 1.0))
                own.step(v.memset(zrow[:, :], 0.0))
                dve.wait_ge(lens_in, 16)
                own.step(v.tensor_copy(lensf[:, :], lens[:, :]))
                own.wait()
                own.step(v.tensor_tensor_scan(cum[:, :], lensf[:, :], zeros[:, :], 0.0, ALU.add, ALU.add))
                own.wait()
                own.step(v.tensor_scalar(wrap[:, :], cum[:, :], 0.0, float(S), ALU.is_le, ALU.mult))
                own.wait()
                v.scalar_tensor_tensor(out=idx[:, :], in0=cum[:, :], scalar=-1.0, in1=wrap[:, :],
                                       op0=ALU.add, op1=ALU.add).then_inc(idx_ready, 1)
                dve.wait_ge(pool_c, 8)
                own.step(v.tensor_copy(tf[:, :], ti[:, :]))
                own.step(v.tensor_copy(scol[:, :], si[:, :]))
                own.step(v.tensor_copy(one_row[:, :], ones[0:1, 0:TT]))

                def norm(c):
                    x = xt[:, c % RX]
                    dve.wait_ge(x_in[c % RX], 16 * (c // RX + 1))
                    for n in range(NT):
                        own.step(v.bn_stats(stats[:, n, :], x[:, n, :]))
                    own.wait()
                    if c:
                        dve.wait_ge(rstd_ready, c)
                    for n in range(NT):
                        own.step(v.bn_aggr(mv[:, n, :], stats[:, n, :]))
                    own.wait()
                    v.tensor_scalar(ve[:, :], mv[:, :, 1], 1e-5, None, ALU.add).then_inc(var_ready, 1)
                    yield
                    dve.wait_ge(rstd_ready, c + 1)
                    for n in range(NT):
                        if c:
                            dve.wait_ge(tr_ready, NT * (c - 1) + n + 1)
                        v.tensor_scalar(y[:, n, :], x[:, n, :], mv[:, n, 0:1], rs[:, n:n + 1],
                                        ALU.subtract, ALU.mult).then_inc(y_ready, 1)
                    yield

                def distance(c):
                    if c:
                        dve.wait_ge(exp_ready, c)
                    for h in range(2):
                        own.step(v.tensor_scalar(dist[:, h, :].rearrange("p (b t) -> p b t", b=2),
                                                 plug[0:TT, 2 * c:2 * c + 2, :], scol[0:TT, h:h + 1], None,
                                                 ALU.subtract))
                    own.wait()
                    v.scalar_tensor_tensor(out=dist[:, :, :], in0=dist[:, :, :], scalar=-32.0, in1=dist[:, :, :],
                                           op0=ALU.mult, op1=ALU.max).then_inc(dist_ready, 1)

                def y_low(c, n):
                    dve.wait_ge(tr_hi, c * NT + n + 1)
                    v.tensor_tensor(yl[:, c % 2, :, TT * n:TT * (n + 1)],
                                    psum[:, n % 2, 0:KD * TT].rearrange("p (k t) -> p k t", k=KD),
                                    f(yh[:, c % 2, :, TT * n:TT * (n + 1)]), ALU.subtract).then_inc(y_split, 1)

                def u_low(c, n):
                    dve.wait_ge(u_hi, c * NT + n + 1)
                    v.scalar_tensor_tensor(out=ul[:, c % 2, n, :], in0=u32[0:TT, n, :], scalar=rsc[:, c % 2, n:n + 1],
                                           in1=f(uh[:, c % 2, n, :]), op0=ALU.mult, op1=ALU.subtract).then_inc(u_split, 1)

                def m_low(c):
                    dve.wait_ge(m_hi, c + 1)
                    v.tensor_tensor(ml[:, c % 2], far[:, :, :], f(mh[:, c % 2]), ALU.subtract).then_inc(m_split, 1)

                def close(c, n):
                    x = xt[:, c % RX, n, :]
                    dve.wait_ge(out_ready, c * NT + n + 1)
                    v.scalar_tensor_tensor(out=x, in0=psum[0:TT, 2 + n, :], scalar=tg[0:TT, 0:1], in1=x,
                                           op0=ALU.mult, op1=ALU.add).then_inc(x_new, 1)

                def equal(q):
                    for k in range(JC):
                        v.tensor_tensor(eq[:, q % 2, k, :, :], tf[0:JP, :].unsqueeze(1).broadcast_to([JP, 2, S]),
                                        idxT[:, k, 2 * q:2 * q + 2].unsqueeze(2).broadcast_to([JP, 2, S]), ALU.is_equal
                                        ).then_inc(eq_ready, 1)

                def patch(q):
                    dve.wait_ge(count_ready, q + 1)
                    v.tensor_scalar(mark[:, 2 * q:2 * q + 2, :], psum[:, 6, 0:CH].rearrange("p (b t) -> p b t", b=2),
                                    1.0, None, ALU.min).then_inc(mark_ready, 1)
                    dve.wait_ge(mark_ready, q + 1)
                    for b in (2 * q, 2 * q + 1):
                        own.step(v.tensor_tensor_scan(plug[:, b, :], mark[:, b, :], zrow[:, :], 0.0, ALU.add, ALU.add))
                    own.wait()
                    own.step(v.tensor_scalar(plug[:, 2 * q:2 * q + 2, :], plug[:, 2 * q:2 * q + 2, :], -1.0, 0.0,
                                             ALU.add, ALU.max))
                    own.wait()

                following = norm(0)
                next(following)
                dve.wait_ge(idx_t, 1)
                own.step(v.tensor_copy(idxT[:, :, :], psum[0:JP, 7, 0:JC * B].rearrange("p (c b) -> p c b", c=JC)))
                own.wait()
                equal(0)
                next(following)
                dve.wait_ge(w_in, 32)
                for k in range(KD):
                    v.tensor_scalar(wland[:, k, :], wland[:, k, :], gres[:, k:k + 1], None, ALU.mult).then_inc(w_scaled, 1)
                patch(0)
                distance(0)
                dve.wait_ge(w_hi, 1)
                v.tensor_tensor(wl[:, :, :], wland[:, :, :], f(wh[:, :, :]), ALU.subtract).then_inc(w_lo, 1)
                dve.wait_ge(b_hi, 1)
                v.tensor_tensor(bl[:, :], brow[:, :], f(bh[:, :]), ALU.subtract).then_inc(b_lo, 1)
                for n in range(NT):
                    y_low(0, n)
                equal(1)
                m_low(0)
                following = norm(1)
                next(following)
                for n in range(NT):
                    u_low(0, n)
                dve.wait_ge(tanh_ready, 1)
                for c in range(NC):
                    close(c, 0)
                    if c + 1 < NC:
                        next(following)
                        patch(c + 1)
                        distance(c + 1)
                    for n in range(NT):
                        if n:
                            close(c, n)
                        if c + 1 < NC:
                            if n == 0:
                                m_low(c + 1)
                            y_low(c + 1, n)
                            u_low(c + 1, n)
                        if c + 2 < NC:
                            if n == 1:
                                equal(c + 2)
                            if n == 2:
                                following = norm(c + 2)
                                next(following)

            @block.tensor
            def _(pe):
                pe.wait_ge(pool_c, 2)
                pe.wait_ge(idx_ready, 1)
                for c in range(JC):
                    ins = nc.tensor.transpose(psum[0:JP, 7, B * c:B * (c + 1)], idx[:, JP * c:JP * (c + 1)],
                                              ident[0:B, 0:B])
                ins.then_inc(idx_t, 1)

                def transpose(c, n):
                    pe.wait_ge(y_ready, c * NT + n + 1)
                    if c * NT + n >= 2:
                        pe.wait_ge(y_split, c * NT + n - 1)
                    for kt in range(KD):
                        ins = nc.tensor.transpose(psum[:, n % 2, TT * kt:TT * (kt + 1)],
                                                  y[:, n, P * kt:P * (kt + 1)], ident[0:TT, 0:TT])
                    ins.then_inc(tr_ready, 1)

                def count(q):
                    pe.wait_ge(eq_ready, JC * (q + 1))
                    if q:
                        pe.wait_ge(mark_ready, q)
                    for k in range(JC):
                        ins = nc.tensor.matmul(psum[:, 6, 0:CH], ones[:, :],
                                               eq[:, q % 2, k, :, :].rearrange("p b t -> p (b t)"),
                                               start=(k == 0), stop=(k == JC - 1))
                    ins.then_inc(count_ready, 1)

                count(0)
                for n in range(NT):
                    transpose(0, n)
                pe.wait_ge(w_lo, 1)
                pe.wait_ge(b_lo, 1)
                for c in range(NC):
                    par = c % 2
                    for n in range(NT):
                        if c:
                            pe.wait_ge(x_new, (c - 1) * NT + n + 1)
                        out = psum[0:TT, 2 + n, :]
                        cols = slice(TT * n, TT * (n + 1))
                        pe.wait_ge(y_split, c * NT + n + 1)
                        for kt in range(KD):
                            three(nc, out, yh[:, par, kt, cols], yl[:, par, kt, cols], wh[:, kt, :], wl[:, kt, :],
                                  kt == 0, False)
                        nc.tensor.matmul(out, one_row[:, :], bh[:, :], start=False, stop=False)
                        nc.tensor.matmul(out, one_row[:, :], bl[:, :], start=False, stop=False)
                        pe.wait_ge(m_split, c + 1)
                        pe.wait_ge(u_split, c * NT + 2 * (n // 2) + n % 2 + 1)
                        for g in range(n % 2 + 1):
                            ins = three(nc, out, mh[:, par, g, cols], ml[:, par, g, cols],
                                        uh[:, par, 2 * (n // 2) + g, :], ul[:, par, 2 * (n // 2) + g, :],
                                        False, g == n % 2)
                        ins.then_inc(out_ready, 1)
                        if c + 1 < NC:
                            if n == 0:
                                count(c + 1)
                            transpose(c + 1, n)


class Normed:

    def __init__(self, nc, m, psum, ident, x_dram):
        self.nc, self.psum, self.ident, self.x_dram = nc, psum, ident, x_dram
        self.xt = m.sb("xt", [TT, 2, NT, D])
        self.stats, self.mv = m.sb("stats", [TT, NT, 6]), m.sb("mv", [TT, NT, 2])
        self.ve, self.rs, self.nhalf = m.sb("ve", [TT, NT]), m.sb("rs", [TT, NT]), m.sb("nhalf", [TT, NT])
        self.hold = m.sb("hold", [TT, 1])
        self.y = m.sb("y", [TT, NT, D])
        self.yh, self.yl = m.sb("yh", [P, 2, KD, CH], F32R), m.sb("yl", [P, 2, KD, CH], F32R)
        self.x_in = [m.sem("x_in0"), m.sem("x_in1")]
        self.stats_done, self.var_ready, self.rstd_ready = m.sem("stats_done"), m.sem("var_ready"), m.sem("rstd_ready")
        self.aggr_done, self.nhalf_ready = m.sem("aggr_done"), m.sem("nhalf_ready")
        self.y_ready, self.tr_ready, self.tr_hi, self.tr_free = (
            m.sem("y_ready"), m.sem("tr_ready"), m.sem("tr_hi"), m.sem("tr_free"))

    def load(self, sp, k):
        c = k % NC
        sp.dma_start(self.xt[:, k % 2], self.x_dram[CH * c:CH * (c + 1), :].rearrange("(n p) d -> p n d", p=TT)
                     ).then_inc(self.x_in[k % 2], 16)

    def start_pool(self, pool):
        self.nc.gpsimd.memset(self.nhalf[:, :], -0.5).then_inc(self.nhalf_ready, 1)
        pool.wait_ge(self.nhalf_ready, 1)

    def rstd(self, pool, k):
        pool.wait_ge(self.var_ready, k + 1)
        self.nc.gpsimd.tensor_tensor(self.rs[:, :], self.ve[:, :], self.nhalf[:, :], ALU.pow).then_inc(self.rstd_ready, 1)

    def start_dve(self, dve):
        dve.sem_inc(self.tr_free, 2)

    def row_stats(self, dve, par, turn, n):
        v = self.nc.vector
        if n == 0:
            dve.wait_ge(self.x_in[par], turn * 16 + 16)
        v.bn_stats(self.stats[:, n, :], self.xt[:, par, n, :]).then_inc(self.stats_done, 1)

    def aggregate(self, dve, k):
        v = self.nc.vector
        dve.wait_ge(self.stats_done, k * NT + NT)
        v.memset(self.hold[:, :], 0.0)
        for n in range(NT):
            v.bn_aggr(self.mv[:, n, :], self.stats[:, n, :]).then_inc(self.aggr_done, 1)
        dve.wait_ge(self.aggr_done, k * NT + NT)
        v.tensor_scalar(self.ve[:, :], self.mv[:, :, 1], 1e-5, None, ALU.add).then_inc(self.var_ready, 1)

    def normalise(self, dve, k, par, n):
        if n == 0:
            dve.wait_ge(self.rstd_ready, k + 1)
        self.nc.vector.tensor_scalar(self.y[:, n, :], self.xt[:, par, n, :], self.mv[:, n, 0:1], self.rs[:, n:n + 1],
                                     ALU.subtract, ALU.mult).then_inc(self.y_ready, 1)

    def transpose(self, pe, k, n):
        nc = self.nc
        pe.wait_ge(self.y_ready, k * NT + n + 1)
        pe.wait_ge(self.tr_free, k * NT + n + 1)
        for kt in range(KD):
            ins = nc.tensor.transpose(self.psum[:, n % 2, TT * kt:TT * (kt + 1)], self.y[:, n, P * kt:P * (kt + 1)],
                                      self.ident[0:TT, 0:TT])
        ins.then_inc(self.tr_ready, 1)

    def hi(self, act, k, par, n):
        act.wait_ge(self.tr_ready, k * NT + n + 1)
        self.nc.scalar.activation(self.yh[:, par, :, TT * n:TT * (n + 1)],
                                  self.psum[:, n % 2, 0:KD * TT].rearrange("p (k t) -> p k t", k=KD), ACT.Copy
                                  ).then_inc(self.tr_hi, 1)

    def lo(self, dve, k, par, n):
        dve.wait_ge(self.tr_hi, k * NT + n + 1)
        self.nc.vector.tensor_tensor(self.yl[:, par, :, TT * n:TT * (n + 1)],
                                     self.psum[:, n % 2, 0:KD * TT].rearrange("p (k t) -> p k t", k=KD),
                                     f(self.yh[:, par, :, TT * n:TT * (n + 1)]), ALU.subtract
                                     ).then_inc(self.tr_free, 1)

    def split(self, pe, k):
        pe.wait_ge(self.tr_free, k * NT + NT + 2)


def phase_relu_ffn(nc, psum, ident, tg, d):
    with Mem(nc, "p2") as m:
        nm = Normed(nc, m, psum, ident, d["x1"])
        NW, IW = 8, 4
        w1h, (w1raw, w1l) = m.sb("w1h", [P, KD, FF0], F32R), m.landing("w1l", [P, KD, FF0])
        w2h, (w2raw, w2l) = m.sb("w2h", [P, NI0, D], F32R), m.landing("w2l", [P, NI0, D])
        b1, b2b = m.sb("b1", [P, NI0]), m.sb("b2b", [TT, D])
        hf = m.sb("hf", [P, 2, CH])
        hh, hl = m.sb("hh", [P, 2, CH], F32R), m.sb("hl", [P, 2, CH], F32R)
        fin = m.sb("fin", [TT, NT, D])
        NB = 24
        wq = m.sb("wq", [P, NB, QB])
        wt = m.sb("wt", [P, NB, QB])
        bs, br = m.sb("bs", [P, NB]), m.sb("br", [P, NB])
        QS = 3 * KD * FF1 // (NB * QB) // NC
        s = m.sem
        w_in, w_hi, w_lo, b_in, x_out = [s(f"w_in{j}") for j in range(NW)], s("w_hi"), s("w_lo"), s("b_in"), s("x_out")
        h_ready, h_relu, h_hi, h_split, h_used = s("h_ready"), s("h_relu"), s("h_hi"), s("h_split"), s("h_used")
        b2_ready, x_biased = s("b2_ready"), s("x_biased")
        out_ready, fin_ready, x_new = s("out_ready"), s("fin_ready"), s("x_new")
        q_in, q_own, q_out, q_stored = s("q_in"), s("q_own"), s("q_out"), s("q_stored")

        def slab(name, j):
            return d[name][j // 2, :, NB * QB * (j % 2):NB * QB * (j % 2 + 1)]

        def part(w, j):
            if j < NW // 2:
                return w[0][:, :, P * IW * j:P * IW * (j + 1)]
            i = IW * (j - NW // 2)
            return w[1][:, i:i + IW, :]

        high, low, raw = (w1h, w2h), (w1l, w2l), (w1raw, w2raw)

        with nc.Block() as block:
            @block.sync
            def _(sp):
                nm.load(sp, 0)
                sp.dma_start(b1[:, :], d["b1_cols"]).then_inc(b_in, 16)
                sp.dma_start(b2b[:, :], d["b2"].partition_broadcast(TT)).then_inc(b_in, 16)
                for j in range(NW):
                    if j < NW // 2:
                        src = d["w1"][:, P * IW * j:P * IW * (j + 1)]
                    else:
                        i = P * IW * (j - NW // 2)
                        src = d["w2"][i:i + P * IW, :]
                    if j >= 2:
                        sp.wait_ge(w_in[j - 2], 16)
                    sp.dma_start(part(raw, j), src.rearrange("(k p) n -> p k n", p=P)).then_inc(w_in[j], 16)
                nm.load(sp, 1)
                for j in range(NC * QS):
                    if j:
                        sp.wait_ge(q_out, j)
                        sp.dma_start(slab("wdq", j - 1), wt[:, :, :].rearrange("p a b -> p (a b)")).then_inc(q_stored, 16)
                    sp.dma_start(wq[:, :, :].rearrange("p a b -> p (a b)"), slab("w_q", j)).then_inc(q_in, 16)
                    k = j // QS
                    if j % QS == 0 and k:
                        sp.wait_ge(x_new, NT * k + NT)
                        sp.dma_start(d["x2"][CH * (k - 1):CH * k, :].rearrange("(n p) d -> p n d", p=TT),
                                     nm.xt[:, (k - 1) % 2]).then_inc(x_out, 16)
                    if j % QS == 1 and k:
                        sp.wait_ge(x_out, 16 * k)
                        nm.load(sp, k + 1)
                sp.wait_ge(q_out, NC * QS)
                sp.dma_start(slab("wdq", NC * QS - 1), wt[:, :, :].rearrange("p a b -> p (a b)")).then_inc(q_stored, 16)
                sp.wait_ge(x_new, NT * NC + NT)
                sp.dma_start(d["x2"][CH * (NC - 1):T, :].rearrange("(n p) d -> p n d", p=TT), nm.xt[:, (NC - 1) % 2]
                             ).then_inc(x_out, 16)
                sp.wait_ge(x_out, 16 * NC)
                sp.wait_ge(q_stored, 16 * NC * QS + 16)

            @block.gpsimd
            def _(pool):
                nm.start_pool(pool)
                nm.rstd(pool, 0)
                pool.sem_inc(x_new, NT)
                pool.wait_ge(b2_ready, 1)
                with pool.Fori(0, NC // 2) as i:
                    for par in (0, 1):
                        c = i * 2 + par
                        for n in range(NT):
                            pool.wait_ge(nm.y_ready, c * NT + n + 1)
                            nc.gpsimd.tensor_tensor(nm.xt[:, par, n, :], nm.xt[:, par, n, :], b2b[:, :], ALU.add
                                                    ).then_inc(x_biased, 1)
                        nm.rstd(pool, c + 1)
                        for n in range(NT):
                            pool.wait_ge(x_biased, c * NT + n + 1)
                            pool.wait_ge(fin_ready, c * NT + n + 1 + NT)
                            nc.gpsimd.tensor_tensor(nm.xt[:, par, n, :], nm.xt[:, par, n, :], fin[:, n, :], ALU.add
                                                    ).then_inc(x_new, 1)

            @block.scalar
            def _(act):
                act.sem_inc(h_relu, 2)
                act.sem_inc(fin_ready, NT)
                for j in range(NW):
                    act.wait_ge(w_in[j], 16)
                    nc.scalar.activation(part(high, j), part(raw, j), ACT.Copy).then_inc(w_hi, 1)
                    if j == 0:
                        for n in range(NT):
                            nm.hi(act, 0, 0, n)
                act.wait_ge(b_in, 32)
                with act.Fori(0, NC // 2) as i:
                    for par in (0, 1):
                        c = i * 2 + par
                        for it in range(NI0):
                            act.wait_ge(h_ready, c * NI0 + it + 1)
                            act.wait_ge(h_split, c * NI0 + it + 1)
                            nc.scalar.activation(hf[:, it % 2, :], psum[:, 2 + it % 2, 0:CH], ACT.Relu,
                                                 bias=b1[:, it:it + 1]).then_inc(h_relu, 1)
                            if 11 <= it < 15:
                                nm.hi(act, c + 1, 1 - par, it - 11)
                        for n in range(NT):
                            act.wait_ge(out_ready, c * NT + n + 1 + NT)
                            act.wait_ge(x_new, c * NT + n + 1)
                            nc.scalar.activation(fin[:, n, :], psum[0:TT, 4 + n, :], ACT.Identity, scale=tg[0:TT, 2:3]
                                                 ).then_inc(fin_ready, 1)

            @block.vector
            def _(dve):
                v = nc.vector
                own = Chain(dve, q_own, 6 * QS)

                def dequantise(j):
                    dve.wait_ge(q_in, j * 16 + 16)
                    own.step(v.tensor_reduce(bs[:, :], wq[:, :, :], AX.X, ALU.max, apply_absolute_value=True))
                    own.wait()
                    own.step(v.tensor_scalar(bs[:, :], bs[:, :], float(np.float32(1.0) / np.float32(7.0)), 1e-12, ALU.mult, ALU.max))
                    own.wait()
                    own.step(v.reciprocal(br[:, :], bs[:, :]))
                    own.wait()
                    own.step(v.tensor_tensor(wq[:, :, :], wq[:, :, :], br[:, :].unsqueeze(2).broadcast_to([P, NB, QB]),
                                             ALU.mult))
                    yield
                    own.wait()
                    own.step(v.tensor_scalar(wq[:, :, :], wq[:, :, :], MAGIC, -MAGIC, ALU.add, ALU.add))
                    own.wait()
                    own.step(v.tensor_tensor(wq[:, :, :], wq[:, :, :], bs[:, :].unsqueeze(2).broadcast_to([P, NB, QB]),
                                             ALU.mult))
                    dve.wait_ge(q_stored, j * 16 + 16)
                    own.wait()
                    v.transpose(wt[:, :, :].rearrange("p a b -> p (a b)"), wq[:, :, :].rearrange("p a b -> p (a b)")
                                ).then_inc(q_out, 1)
                    yield

                nm.start_dve(dve)
                dve.sem_inc(h_split, 2)
                dve.sem_inc(out_ready, NT)
                dve.sem_inc(h_used, 1)
                dve.sem_inc(q_stored, 16)
                for n in range(NT):
                    nm.row_stats(dve, 0, 0, n)
                nm.aggregate(dve, 0)
                for n in range(NT):
                    nm.normalise(dve, 0, 0, n)
                dve.wait_ge(b_in, 32)
                v.tensor_scalar(b2b[:, :], b2b[:, :], tg[0:TT, 2:3], None, ALU.mult).then_inc(b2_ready, 1)
                for j in range(NW):
                    dve.wait_ge(w_hi, j + 1)
                    v.tensor_tensor(part(low, j), part(raw, j), f(part(high, j)), ALU.subtract).then_inc(w_lo, 1)
                    if j == 0:
                        for n in range(NT):
                            nm.lo(dve, 0, 0, n)
                with dve.Fori(0, NC // 2) as i:
                    for par in (0, 1):
                        c = i * 2 + par
                        own.at(c)
                        slabs = [dequantise(c * QS + r) for r in range(QS)]
                        for it in range(NI0):
                            dve.wait_ge(h_relu, c * NI0 + it + 1 + 2)
                            if it == 1:
                                dve.wait_ge(out_ready, c * NT + NT)
                            else:
                                dve.wait_ge(h_used, c * (NI0 - 1) + max(it - 1, 0) + 1)
                            v.tensor_copy(hh[:, it % 2, :], hf[:, it % 2, :]).then_inc(h_hi, 1)
                            dve.wait_ge(h_hi, c * NI0 + it + 1)
                            v.tensor_tensor(hl[:, it % 2, :], hf[:, it % 2, :],
                                            f(hh[:, it % 2, :]), ALU.subtract).then_inc(h_split, 1)
                            if it < 2 * QS:
                                next(slabs[it // 2])
                            if 5 <= it < 7:
                                for n in (2 * it - 10, 2 * it - 9):
                                    nm.row_stats(dve, 1 - par, i + par, n)
                            elif it == 7:
                                nm.aggregate(dve, c + 1)
                            elif 8 <= it < 12:
                                nm.normalise(dve, c + 1, 1 - par, it - 8)
                            elif it >= 12:
                                nm.lo(dve, c + 1, 1 - par, it - 12)
                        own.done()

            @block.tensor
            def _(pe):
                for n in range(NT):
                    nm.transpose(pe, 0, n)

                def up(c, par, it):
                    pe.wait_ge(w_lo, it // IW + 1)
                    pe.wait_ge(h_relu, c * NI0 + it + 1)
                    for kt in range(KD):
                        cols = slice(P * it, P * (it + 1))
                        ins = three(nc, psum[:, 2 + it % 2, 0:CH], w1h[:, kt, cols], w1l[:, kt, cols],
                                    nm.yh[:, par, kt, :], nm.yl[:, par, kt, :], kt == 0, kt == KD - 1)
                    ins.then_inc(h_ready, 1)

                def down(c, par, it):
                    pe.wait_ge(h_split, c * NI0 + it + 1 + 2)
                    for n in range(NT):
                        if it == 0:
                            pe.wait_ge(fin_ready, c * NT + n + 1)
                        cols = slice(TT * n, TT * (n + 1))
                        ins = three(nc, psum[0:TT, 4 + n, :], hh[:, it % 2, cols], hl[:, it % 2, cols],
                                    w2h[:, it, :], w2l[:, it, :], it == 0, it == NI0 - 1)
                        if it == NI0 - 1:
                            ins.then_inc(out_ready, 1)
                        elif n == NT - 1:
                            ins.then_inc(h_used, 1)

                with pe.Fori(0, NC // 2) as i:
                    for par in (0, 1):
                        c = i * 2 + par
                        nm.split(pe, c)
                        up(c, par, 0)
                        for it in range(NI0):
                            if it + 1 < NI0:
                                up(c, par, it + 1)
                            pe.wait_ge(w_lo, NW // 2 + it // IW + 1)
                            down(c, par, it)
                            if 9 <= it < 13:
                                nm.transpose(pe, c + 1, it - 9)


class KvLanding:

    GW = 4 * DH
    HW = 376
    LO = M - HW

    def __init__(self, m, d):
        self.d = d
        self.weights = m.sb("wland", [P, 2, KC, self.GW])
        self.context = m.sb("land", [P, 4, 2, self.HW])
        self.w_in, self.c_in = [m.sem("wk_in"), m.sem("wv_in")], [m.sem(f"c_in{i}") for i in range(4)]

    def load_weights(self, sp, g, i):
        src = self.d["wkv"][:, bass.ds(g * self.GW + i * INNER, self.GW)].rearrange("(k p) n -> p k n", p=P)
        sp.dma_start(self.weights[:, i], src).then_inc(self.w_in[i], 16)

    def load_context(self, sp, b, j):
        half, jj = divmod(j, 4)
        src = self.d["ctx_t"][bass.ds(b, 1), 2 * P * jj:2 * P * (jj + 1), half * self.LO:half * self.LO + self.HW]
        sp.dma_start(self.context[:, jj], src.rearrange("o (k p) t -> p (o k) t", p=P)).then_inc(self.c_in[jj], 16)

    def first(self, sp):
        self.load_weights(sp, 0, 0)
        for j in range(4):
            self.load_context(sp, 0, j)
        self.load_weights(sp, 0, 1)


def phase_queries(nc, psum, ident, tg, kv, d):
    with Mem(nc, "p3") as m:
        nm = Normed(nc, m, psum, ident, d["x2"])
        NG = INNER // P
        RG = 4
        NW = 2
        wh, (wraw, wl) = m.sb("wh", [P, KD, INNER], F32R), m.landing("wl", [P, KD, INNER])
        stage = m.sb("stage", [P, RG, CH])
        s = m.sem
        w_in, w_hi, w_lo = [s(f"w_in{j}") for j in range(NW)], s("w_hi"), s("w_lo")
        q_ready, q_done = s("q_ready"), s("q_done")
        q_out = [s(f"q_out{i}") for i in range(RG)]

        def part(w, j):
            return w[:, :, INNER // NW * j:INNER // NW * (j + 1)]

        with nc.Block() as block:
            @block.sync
            def _(sp):
                nm.load(sp, 0)
                for j in range(NW):
                    sp.dma_start(part(wraw, j), part(d["wq"].rearrange("(k p) n -> p k n", p=P), j)).then_inc(w_in[j], 16)
                nm.load(sp, 1)
                for k in range(NC):
                    for g in range(NG):
                        e = k * NG + g
                        sp.wait_ge(q_done, e + 1 + RG)
                        sp.dma_start(d["qT"][P * g:P * (g + 1), CH * k:CH * (k + 1)], stage[:, g % RG, :]
                                     ).then_inc(q_out[g % RG], 16)
                        if g == 0 and k + 2 <= NC:
                            sp.wait_ge(nm.y_ready, NT * (k + 1))
                            nm.load(sp, k + 2)
                        if g == 0 and k == NC - 1:
                            kv.first(sp)
                for i in range(RG):
                    sp.wait_ge(q_out[i], 16 + 16 * NC * NG // RG)

            @block.gpsimd
            def _(pool):
                nm.start_pool(pool)
                nm.rstd(pool, 0)
                with pool.Fori(0, NC // 2) as i:
                    for par in (0, 1):
                        nm.rstd(pool, i * 2 + par + 1)

            @block.scalar
            def _(act):
                act.sem_inc(q_done, RG)
                for i in range(RG):
                    act.sem_inc(q_out[i], 16)
                for j in range(NW):
                    act.wait_ge(w_in[j], 16)
                    nc.scalar.activation(part(wh, j), part(wraw, j), ACT.Copy).then_inc(w_hi, 1)
                    if j == 0:
                        for n in range(NT):
                            nm.hi(act, 0, 0, n)
                with act.Fori(0, NC // 2) as i:
                    for par in (0, 1):
                        c = i * 2 + par
                        for g in range(NG):
                            act.wait_ge(q_ready, c * NG + g + 1)
                            act.wait_ge(q_out[g % RG], (c * (NG // RG) + g // RG) * 16 + 16)
                            nc.scalar.activation(stage[:, g % RG, :], psum[:, 2 + g % RG, 0:CH], ACT.Copy,
                                                 scale=DH ** -0.5).then_inc(q_done, 1)
                            if g >= NG - NT:
                                nm.hi(act, c + 1, 1 - par, g - (NG - NT))

            @block.vector
            def _(dve):
                v = nc.vector
                nm.start_dve(dve)
                for n in range(NT):
                    nm.row_stats(dve, 0, 0, n)
                nm.aggregate(dve, 0)
                for n in range(NT):
                    nm.normalise(dve, 0, 0, n)
                for j in range(NW):
                    dve.wait_ge(w_hi, j + 1)
                    v.tensor_tensor(part(wl, j), part(wraw, j), f(part(wh, j)), ALU.subtract).then_inc(w_lo, 1)
                    if j == 0:
                        for n in range(NT):
                            nm.lo(dve, 0, 0, n)
                with dve.Fori(0, NC // 2) as i:
                    for par in (0, 1):
                        for n in range(NT):
                            nm.row_stats(dve, 1 - par, i + par, n)
                        nm.aggregate(dve, i * 2 + par + 1)
                        for n in range(NT):
                            nm.normalise(dve, i * 2 + par + 1, 1 - par, n)
                        for n in range(NT):
                            nm.lo(dve, i * 2 + par + 1, 1 - par, n)

            @block.tensor
            def _(pe):
                for n in range(NT):
                    nm.transpose(pe, 0, n)
                with pe.Fori(0, NC // 2) as i:
                    for par in (0, 1):
                        c = i * 2 + par
                        nm.split(pe, c)
                        for g in range(NG):
                            pe.wait_ge(w_lo, NW * g // NG + 1)
                            pe.wait_ge(q_done, c * NG + g + 1)
                            for kt in range(KD):
                                cols = slice(P * g, P * (g + 1))
                                ins = three(nc, psum[:, 2 + g % RG, 0:CH], wh[:, kt, cols], wl[:, kt, cols],
                                            nm.yh[:, par, kt, :], nm.yl[:, par, kt, :], kt == 0, kt == KD - 1)
                            ins.then_inc(q_ready, 1)
                            if NG - NT - 1 <= g < NG - 1:
                                nm.transpose(pe, c + 1, g - (NG - NT - 1))


TURN = ("S0 R0 G0 C4 G1 T00 T01 S1 R1 G2 T02 C5 C6 G3 C7 A0 T10 S2 R2 G4 T11 T12 Q G5 c0 A1 T20 "
        "S3 R3 G6 T21 T22 c1 G7 c2 A2 T30 G8 T31 T32 c3 G9 A3").split()


def turn_steps(project=True, read_on=True, keys=False, values=False):
    steps = [x for x in TURN if (project or x[0] not in "GCQ") and (read_on or x[0] != "c")]
    if keys:
        steps.insert(steps.index("G8"), "K")
    if values:
        steps.insert(steps.index("G1"), "V")
    return steps


def phase_attention(nc, psum, ident, kv, d):
    HG = 4
    GW = HG * DH
    NG = H // HG
    ROWS = M // 6
    MK = M + 1
    MP = M + 2
    HW, LO = kv.HW, kv.LO
    BK = 512
    NP = 10
    NU = NG * B
    with Mem(nc, "p4") as m:
        wland, land, w_in, c_in = kv.weights, kv.context, kv.w_in, kv.c_in
        wh, wl = m.sb("wh", [P, 2, KC, GW], F32R), m.sb("wl", [P, 2, KC, GW], F32R)
        ch, cl = m.sb("ch", [P, 2, KC, HW], F32R), m.sb("cl", [P, 2, KC, HW], F32R)
        kt_ = m.sb("kt", [P, 2, HG, MP], F32R)
        v_ = m.sb("v", [P, 2, 6, HG, 2 * DH], F32R)
        q32 = m.sb("q32", [P, HG, S])
        qh, ql = m.sb("qh", [P, 2, HG, S], F32R), m.sb("ql", [P, 2, HG, S], F32R)
        p = m.sb("p", [TT, 4, MP])
        ph, pl = m.sb("ph", [P, 4, 2 * S], F32R), m.sb("pl", [P, 4, 2 * S], F32R)
        tmp = m.sb("tmp", [DH, 2, S])
        ao = m.sb("ao", [P, 2, 2, S])
        negm, rsum, rinv = m.sb("negm", [TT, 4]), m.sb("rsum", [TT, 4]), m.sb("rinv", [TT, 4])
        hold = m.sb("hold", [TT, 4])
        nk, nkh = m.sb("nk", [P, 2]), m.sb("nkh", [P, 2], F32R)
        nv, nvr = m.sb("nv", [1, DH]), m.sb("nvr", [1, HG, 2 * DH], F32R)

        s = m.sem
        w_hi, w_lo = s("w_hi"), s("w_lo")
        c_hi, c_lo = s("c_hi"), s("c_lo")
        q_in, q_hi, q_lo = s("q_in"), s("q_hi"), s("q_lo")
        null_in, null_own, null_row = s("null_in"), s("null_own"), s("null_row")
        sc_ready, mx_done, exp_done = s("sc_ready"), s("mx_done"), s("exp_done")
        rinv_done, norm_done = s("rinv_done"), s("norm_done")
        at_ready, at_hi, at_done = s("at_ready"), s("at_hi"), s("at_done")
        pj_ready, pj_hi, pj_lo = s("pj_ready"), s("pj_hi"), s("pj_lo")
        ao_out = [s(f"ao_out{i}") for i in range(4)]

        def wait(e, sem, value):
            if not isinstance(value, int) or value > 0:
                e.wait_ge(sem, value)

        def group(i):
            half, j = divmod(i, 5)
            return ("k", half, j) if j < 2 else ("v", half, 3 * half + j - 2)

        def run(e, unit, group_start=None):
            def pair(g, k, u0, turn, change=False, last=False):
                if change:
                    later = [(g, B - 1), (g + 1, 0), (g + 1, 1)]
                else:
                    later = [(g, k * 2 + 1), (g, k * 2 + 2), (g, k * 2 + 3)]
                here = [(g, k * 2), (g, k * 2 + 1)]
                for par in (0, 1):
                    unit(u0 + par, par, turn, here[par], later[par], later[par + 1],
                         dict(project=not (last and par), read_on=not last,
                              keys=change and par == 0, values=change and par == 1))

            with e.Fori(0, NG - 1) as g:
                if group_start:
                    group_start(g)
                with e.Fori(0, B // 2 - 1) as k:
                    pair(g, k, g * B + k * 2, g * (B // 2) + k)
                pair(g, B // 2 - 1, g * B + (B - 2), g * (B // 2) + (B // 2 - 1), change=True)
            g = NG - 1
            with e.Fori(0, B // 2 - 1) as k:
                pair(g, k, k * 2 + g * B, k + g * (B // 2))
            pair(g, B // 2 - 1, NU - 2, NU // 2 - 1, last=True)

        with nc.Block() as block:
            @block.sync
            def _(sp):
                def piece(w, b, j):
                    sp.wait_ge(c_lo, w * 8 + j + 1)
                    kv.load_context(sp, b, j)

                def queries(u, g, b):
                    wait(sp, q_lo, u)
                    src = d["qT"][bass.ds(g * GW, GW), bass.ds(b * S, S)].rearrange("(h e) t -> e h t", e=DH)
                    for half in range(2):
                        sp.dma_start(q32[DH * half:DH * (half + 1)], src).then_inc(q_in, 16)

                def store(u, par, g, b, pr):
                    sp.wait_ge(at_done, u * 16 + (8 * pr + 8 + 2))
                    dst = d["aT"][bass.ds(g * GW + pr * P, P), bass.ds(b * S, S)]
                    sp.dma_start(dst, ao[:, par, pr, :]).then_inc(ao_out[2 * par + pr], 16)

                def unit(u, par, turn, here, next1, next2, kind):
                    if kind["project"]:
                        queries(u + 1, *next1)
                    for j in range(8):
                        if j == 4:
                            store(u, par, *here, 0)
                        if kind["read_on"]:
                            piece(u + 2, next2[1], j)
                    store(u, par, *here, 1)

                sp.wait_ge(null_own, 1)
                for half in range(2):
                    sp.dma_start(nk[DH * half:DH * (half + 1), 0:1], d["null_kv"][0].unsqueeze(1)).then_inc(null_in, 16)
                sp.dma_start(nv[:, :], d["null_kv"][1:2, :]).then_inc(null_in, 16)
                for j in range(4, 8):
                    piece(0, 0, j)
                queries(0, 0, 0)
                sp.wait_ge(null_own, 8)
                for par in range(2):
                    sp.dma_start(f(v_[ROWS:ROWS + 1, par, 5, :, :]), f(nvr[:, :, :])).then_inc(null_row, 16)
                for j in range(8):
                    piece(1, 1, j)
                def group_start(g):
                    sp.wait_ge(w_lo, g * 2 + 2)
                    kv.load_weights(sp, g + 1, 0)
                    kv.load_weights(sp, g + 1, 1)
                run(sp, unit, group_start)
                for i in range(4):
                    sp.wait_ge(ao_out[i], 16 * (NU // 2) + 16)

            @block.gpsimd
            def _(pool):
                nc.gpsimd.memset(nk[:, :], 0.0).then_inc(null_own, 1)

                def unit(u, par, turn, here, next1, next2, kind):
                    for n in range(2 * HG):
                        pool.wait_ge(rinv_done, u * 8 + n + 1)
                        nc.gpsimd.tensor_tensor(hold[:, n % 4:n % 4 + 1], rinv[:, n % 4:n % 4 + 1], rinv[:, n % 4:n % 4 + 1], ALU.mult)
                        nc.gpsimd.tensor_scalar(p[:, n % 4, 0:MK], p[:, n % 4, 0:MK], rinv[:, n % 4:n % 4 + 1], 1.0,
                                                ALU.mult, ALU.mult).then_inc(norm_done, 1)
                run(pool, unit)

            def weights_free(e, step, u):
                wait(e, pj_ready, u * NP + (NP + 7 if step == "K" else NP))

            def rows_free(e, u, j):
                wait(e, pj_ready, u * NP + (NP + 5 if j < 4 else NP))

            @block.scalar
            def _(act):
                def split(step, u, par, wgroup):
                    if step in "KV":
                        i = "KV".index(step)
                        act.wait_ge(w_in[i], wgroup * 16 + 16)
                        weights_free(act, step, u)
                        nc.scalar.activation(wh[:, i], wland[:, i], ACT.Copy).then_inc(w_hi, 1)
                    elif step == "Q":
                        act.wait_ge(q_in, u * 32 + 64)
                        nc.scalar.activation(qh[:, 1 - par], q32[:, :, :], ACT.Copy).then_inc(q_hi, 1)
                    else:
                        w, j = u + (1 if step[0] == "C" else 2), int(step[1])
                        act.wait_ge(c_in[j % 4], w * 32 + (j // 4) * 16 + 16)
                        rows_free(act, u, j)
                        nc.scalar.activation(ch[:, j // 4, 2 * (j % 4):2 * (j % 4) + 2, :], land[:, j % 4], ACT.Copy
                                             ).then_inc(c_hi, 1)

                def project(u, par, i):
                    kind, half, j = group(i)
                    act.wait_ge(pj_ready, u * NP + (NP + i + 1))
                    bank = psum[:, 6 + i % 2, :]
                    if kind == "k":
                        t0, t1 = (0, HW) if half == 0 else (HW, M)
                        for e in range(2):
                            ins = nc.scalar.activation(kt_[0:DH, 1 - par, 2 * j + e, t0:t1],
                                                       bank[DH * e:DH * (e + 1), 0:t1 - t0], ACT.Copy)
                    else:
                        ins = nc.scalar.activation(v_[0:ROWS, 1 - par, j, :, 0:DH],
                                                   bank[0:ROWS, 0:GW].rearrange("p (h e) -> p h e", h=HG), ACT.Copy)
                    ins.then_inc(pj_hi, 1)

                def unit(u, par, turn, here, next1, next2, kind):
                    for step in turn_steps(**kind):
                        if step[0] in "CcQKV":
                            split(step, u, par, next1[0] if step == "V" else next2[0])
                        elif step[0] == "G":
                            project(u, par, int(step[1]))
                        elif step[0] == "S":
                            for i in range(2):
                                n = 2 * int(step[1]) + i
                                act.wait_ge(mx_done, u * 8 + n + 1)
                                nc.scalar.activation(p[:, n % 4, 0:MK],
                                                     psum[0:TT, 2 * i:2 * i + 2, :].rearrange("p a n -> p (a n)")[:, 0:MK],
                                                     ACT.Exp, bias=negm[:, n % 4:n % 4 + 1],
                                                     accum_out=rsum[:, n % 4:n % 4 + 1]).then_inc(exp_done, 1)
                        elif step[0] == "T":
                            h, c = int(step[1]), int(step[2])
                            rows = ROWS + (c == 2)
                            act.wait_ge(at_ready, u * 16 + (4 * h + c + 1))
                            nc.scalar.activation(ph[0:rows, (3 * h + c) % 4, :], psum[0:rows, 4 + c % 2, 0:2 * S],
                                                 ACT.Copy).then_inc(at_hi, 1)
                        elif step[0] == "A":
                            h = int(step[1])
                            act.wait_ge(at_ready, u * 16 + (4 * h + 4))
                            nc.scalar.activation(tmp[:, h % 2, :], psum[DH:P, 5, 0:S], ACT.Copy).then_inc(at_hi, 1)

                act.sem_inc(exp_done, 2)
                for step in ("K", "c0", "c1", "c2", "c3"):
                    split(step, -2, 1, 0)
                for step in ("V", "C4", "C5", "C6", "C7"):
                    split(step, -1, 1, 0)
                for i in range(NP):
                    project(-1, 1, i)
                    if i == 5:
                        for step in ("Q", "c0", "c1", "c2", "c3"):
                            split(step, -1, 1, 0)
                run(act, unit)

            @block.vector
            def _(dve):
                v = nc.vector

                def split(step, u, par, wgroup):
                    if step in "KV":
                        i = "KV".index(step)
                        dve.wait_ge(w_hi, wgroup * 2 + i + 1)
                        v.tensor_tensor(wl[:, i], wland[:, i], f(wh[:, i]), ALU.subtract).then_inc(w_lo, 1)
                    elif step == "Q":
                        dve.wait_ge(q_hi, u + 2)
                        v.tensor_tensor(ql[:, 1 - par], q32[:, :, :], f(qh[:, 1 - par]), ALU.subtract).then_inc(q_lo, 1)
                    else:
                        w, j = u + (1 if step[0] == "C" else 2), int(step[1])
                        dve.wait_ge(c_hi, w * 8 + j + 1)
                        at = (slice(None), j // 4, slice(2 * (j % 4), 2 * (j % 4) + 2))
                        v.tensor_tensor(cl[at], land[:, j % 4], f(ch[at]), ALU.subtract).then_inc(c_lo, 1)

                def project(u, par, i):
                    kind, half, j = group(i)
                    dve.wait_ge(pj_hi, u * NP + (NP + i + 1))
                    bank = psum[:, 6 + i % 2, :]
                    if kind == "k":
                        t0, t1 = (0, HW) if half == 0 else (HW, M)
                        for e in range(2):
                            ins = v.tensor_tensor(kt_[DH:P, 1 - par, 2 * j + e, t0:t1],
                                                  bank[DH * e:DH * (e + 1), 0:t1 - t0],
                                                  f(kt_[0:DH, 1 - par, 2 * j + e, t0:t1]), ALU.subtract)
                    else:
                        ins = v.tensor_tensor(v_[0:ROWS, 1 - par, j, :, DH:2 * DH],
                                              bank[0:ROWS, 0:GW].rearrange("p (h e) -> p h e", h=HG),
                                              f(v_[0:ROWS, 1 - par, j, :, 0:DH]), ALU.subtract)
                    ins.then_inc(pj_lo, 1)

                def unit(u, par, turn, here, next1, next2, kind):
                    for step in turn_steps(**kind):
                        if step[0] in "CcQKV":
                            split(step, u, par, next1[0] if step == "V" else next2[0])
                        elif step[0] == "G":
                            project(u, par, int(step[1]))
                        elif step[0] == "S":
                            for i in range(2):
                                n = 2 * int(step[1]) + i
                                dve.wait_ge(sc_ready, u * 8 + n + 1)
                                v.tensor_reduce(negm[:, n % 4:n % 4 + 1],
                                                psum[0:TT, 2 * i:2 * i + 2, :].rearrange("p a n -> p (a n)")[:, 0:MK],
                                                AX.X, ALU.max, negate=True).then_inc(mx_done, 1)
                        elif step[0] == "R":
                            for i in range(2):
                                n = 2 * int(step[1]) + i
                                dve.wait_ge(exp_done, u * 8 + (n + 1 + 2))
                                v.reciprocal(rinv[:, n % 4:n % 4 + 1], rsum[:, n % 4:n % 4 + 1]).then_inc(rinv_done, 1)
                        elif step[0] == "T":
                            h, c = int(step[1]), int(step[2])
                            rows = ROWS + (c == 2)
                            dve.wait_ge(at_hi, u * 16 + (4 * h + c + 1))
                            v.tensor_tensor(pl[0:rows, (3 * h + c) % 4, :], psum[0:rows, 4 + c % 2, 0:2 * S],
                                            f(ph[0:rows, (3 * h + c) % 4, :]), ALU.subtract).then_inc(at_done, 1)
                        elif step[0] == "A":
                            h = int(step[1])
                            dve.wait_ge(at_hi, u * 16 + (4 * h + 4))
                            if h % 2 == 0:
                                dve.wait_ge(ao_out[2 * par + h // 2], turn * 16 + 16)
                            v.tensor_tensor(ao[DH * (h % 2):DH * (h % 2 + 1), par, h // 2, :], psum[0:DH, 5, 0:S],
                                            tmp[:, h % 2, :], ALU.add).then_inc(at_done, 1)

                dve.sem_inc(c_lo, 4)
                dve.sem_inc(at_done, 2)
                dve.sem_inc(pj_lo, 2)
                for i in range(4):
                    dve.sem_inc(ao_out[i], 16)
                for step in ("K", "c0", "c1", "c2", "c3"):
                    split(step, -2, 1, 0)
                null = Chain(dve, null_own)
                null.n = 1
                dve.wait_ge(null_in, 48)
                null.wait()
                null.step(v.tensor_copy(nkh[:, :], nk[:, :]))
                for par in range(2):
                    null.step(v.tensor_copy(kt_[0:DH, par, :, M:MP], nk[0:DH, :].unsqueeze(1).broadcast_to([DH, HG, 2])))
                null.step(v.tensor_copy(nvr[:, :, 0:DH], nv[:, :].unsqueeze(1).broadcast_to([1, HG, DH])))
                null.wait()
                for par in range(2):
                    null.step(v.tensor_tensor(kt_[DH:P, par, :, M:MP],
                                              nk[DH:P, :].unsqueeze(1).broadcast_to([DH, HG, 2]),
                                              f(nkh[DH:P, :]).unsqueeze(1).broadcast_to([DH, HG, 2]), ALU.subtract))
                null.step(v.tensor_tensor(nvr[:, :, DH:2 * DH], nv[:, :].unsqueeze(1).broadcast_to([1, HG, DH]),
                                          f(nvr[:, :, 0:DH]), ALU.subtract))
                assert null.n == 8
                for step in ("V", "C4", "C5", "C6", "C7"):
                    split(step, -1, 1, 0)
                for i in range(NP):
                    project(-1, 1, i)
                    if i == 5:
                        for step in ("Q", "c0", "c1", "c2", "c3"):
                            split(step, -1, 1, 0)
                run(dve, unit)

            @block.tensor
            def _(pe):
                def project(u, i, wgroup):
                    kind, half, j = group(i)
                    pe.wait_ge(pj_lo, u * NP + (NP + i + 1))
                    if i % 5 == 0:
                        pe.wait_ge(c_lo, u * 8 + (8 + 4 * half + 4 + 4))
                    if i == 0 or i == 2:
                        pe.wait_ge(w_lo, wgroup * 2 + (1 if i == 0 else 2))
                    for kt in range(KC):
                        first, last = kt == 0, kt == KC - 1
                        if kind == "k":
                            c0, c1 = (0, HW) if half == 0 else (HW - LO, HW)
                            cols = slice(P * j, P * (j + 1))
                            ins = three(nc, psum[:, 6 + i % 2, 0:c1 - c0], wh[:, 0, kt, cols], wl[:, 0, kt, cols],
                                        ch[:, half, kt, c0:c1], cl[:, half, kt, c0:c1], first, last)
                        else:
                            c0 = ROWS * j - half * LO
                            ins = three(nc, psum[0:ROWS, 6 + i % 2, 0:GW],
                                        ch[:, half, kt, c0:c0 + ROWS], cl[:, half, kt, c0:c0 + ROWS],
                                        wh[:, 1, kt, :], wl[:, 1, kt, :], first, last)
                    ins.then_inc(pj_ready, 1)

                def unit(u, par, turn, here, next1, next2, kind):
                    for step in turn_steps(**kind):
                        if step[0] == "G":
                            project(u, int(step[1]), next1[0])
                        elif step[0] == "S":
                            h = int(step[1])
                            if h == 0:
                                pe.wait_ge(q_lo, u + 1)
                                pe.wait_ge(pj_lo, u * NP + (7 + 2))
                            for i in range(2):
                                pe.wait_ge(exp_done, u * 8 + (2 * h + i + 1))
                                cols = slice(TT * i, TT * (i + 1))
                                for b, c1 in ((0, BK), (1, MP)):
                                    out = psum[0:TT, 2 * i + b, 0:c1 - BK * b]
                                    nc.tensor.matmul(out, qh[:, par, h, cols], kt_[:, par, h, BK * b:c1],
                                                     start=True, stop=False)
                                    ins = nc.tensor.matmul(out, ql[:, par, h, cols], kt_[:, par, h, BK * b:c1],
                                                           start=False, stop=True)
                                ins.then_inc(sc_ready, 1)
                        elif step[0] == "T":
                            h, c = int(step[1]), int(step[2])
                            rows = ROWS + (c == 2)
                            if c == 0:
                                pe.wait_ge(norm_done, u * 8 + (2 * h + 2))
                            pe.wait_ge(at_done, u * 16 + (4 * h + c + 1))
                            for t in (0, 1):
                                for i in range(2):
                                    at = S * t + TT * i
                                    r0 = ROWS * (2 * c + t)
                                    ins = nc.tensor.transpose(psum[0:rows, 4 + c % 2, at:at + TT],
                                                              p[:, (2 * h + i) % 4, r0:r0 + rows], ident[0:TT, 0:TT])
                            ins.then_inc(at_ready, 1)
                        elif step[0] == "A":
                            h = int(step[1])
                            if h == 0:
                                pe.wait_ge(pj_lo, u * NP + (NP + 2))
                            pe.wait_ge(at_done, u * 16 + (4 * h + 3 + 2))
                            for t in range(6):
                                rows = ROWS + (t == 5)
                                slot = (3 * h + t // 2) % 4
                                cols = slice(S * (t % 2), S * (t % 2 + 1))
                                nc.tensor.matmul(psum[:, 5, 0:S], v_[0:rows, par, t, h, :], ph[0:rows, slot, cols],
                                                 start=t == 0, stop=False)
                                ins = nc.tensor.matmul(psum[:, 5, 0:S], v_[0:rows, par, t, h, :], pl[0:rows, slot, cols],
                                                       start=False, stop=t == 5)
                            ins.then_inc(at_ready, 1)

                for i in range(NP):
                    project(-1, i, 0)
                pe.wait_ge(null_own, 8)
                pe.wait_ge(null_row, 32)
                run(pe, unit)


def phase_attention_out(nc, psum, ident, tg, ymax, y_all, d):
    KI = INNER // P
    NE = NC * NT
    RA, RX = 3, 6
    with Mem(nc, "p5") as m:
        wland = m.sb("wland", [P, KI, D])
        wh, wl = m.sb("wh", [P, KI, D], F32R), m.sb("wl", [P, KI, D], F32R)
        aland = m.sb("aland", [P, RA, KI, TT])
        ah, al = m.sb("ah", [P, RA, KI, TT], F32R), m.sb("al", [P, RA, KI, TT], F32R)
        scale_b, bias_b = m.sb("scale_b", [TT, D]), m.sb("bias_b", [TT, D])
        xt = m.sb("xt", [TT, RX, D])
        z, y = m.sb("z", [TT, 2, D]), m.sb("y", [TT, 2, D])
        st1, st2 = m.sb("st1", [TT, 2, 6]), m.sb("st2", [TT, 2, 6])
        mv1, mv2 = m.sb("mv1", [TT, 2, 2]), m.sb("mv2", [TT, 2, 2])
        rs1, rs2 = m.sb("rs1", [TT, 2, 2]), m.sb("rs2", [TT, 2, 2])
        nhalf = m.sb("nhalf", [TT, 1])
        s = m.sem
        const_in, w_in, w_hi, w_lo, ln_ready = s("const_in"), [s("w_in0"), s("w_in1")], s("w_hi"), s("w_lo"), s("ln_ready")
        a_in, a_hi, a_lo = [s(f"a_in{i}") for i in range(RA)], s("a_hi"), s("a_lo")
        x_in, x_out = [s(f"x_in{i}") for i in range(RX)], [s(f"x_out{i}") for i in range(RX)]
        dve_own, pool_own, nhalf_ready, x_biased = s("dve_own"), s("pool_own"), s("nhalf_ready"), s("x_biased")
        out_ready, mv1_ready, rs1_ready, z_ready, z_scaled = (
            s("out_ready"), s("mv1_ready"), s("rs1_ready"), s("z_ready"), s("z_scaled"))
        x_new, mv2_ready, rs2_ready, y_ready, max_done = (
            s("x_new"), s("mv2_ready"), s("rs2_ready"), s("y_ready"), s("max_done"))
        tr_ready, tr_read = s("tr_ready"), s("tr_read")

        def rows(name, e):
            return d[name][TT * e:TT * (e + 1), :]

        with nc.Block() as block:
            @block.sync
            def _(sp):
                def load_a(e):
                    sp.dma_start(aland[:, e % RA], d["aT"][:, TT * e:TT * (e + 1)].rearrange("(k p) t -> p k t", p=P)
                                 ).then_inc(a_in[e % RA], 16)

                def load_x(e):
                    sp.dma_start(xt[:, e % RX, :], rows("x2", e)).then_inc(x_in[e % RX], 16)

                for h in (0, 1):
                    half = slice(KI // 2 * h, KI // 2 * (h + 1))
                    sp.dma_start(wland[:, half, :], d["wout"].rearrange("(k p) n -> p k n", p=P)[:, half, :]
                                 ).then_inc(w_in[h], 16)
                    load_a(h)
                sp.dma_start(scale_b[:, :], d["ln_scale"].partition_broadcast(TT)).then_inc(const_in, 16)
                sp.dma_start(bias_b[:, :], d["ln_bias"].partition_broadcast(TT)).then_inc(const_in, 16)
                for e in range(RX):
                    load_x(e)
                for e in range(2, NE + RX):
                    if e < NE:
                        if e >= RA:
                            sp.wait_ge(a_lo, e - RA + 1)
                        load_a(e)
                    if e >= RX:
                        k = e - RX
                        sp.wait_ge(x_new, k + 1)
                        sp.dma_start(rows("x3", k), xt[:, k % RX, :]).then_inc(x_out[k % RX], 16)
                        sp.wait_ge(x_out[k % RX], 16 * (k // RX + 1))
                        if e < NE:
                            sp.wait_ge(y_ready, k + 1)
                            load_x(e)

            @block.gpsimd
            def _(pool):
                own = Chain(pool, pool_own)
                nc.gpsimd.memset(nhalf[:, :], -0.5).then_inc(nhalf_ready, 1)
                pool.wait_ge(nhalf_ready, 1)

                def moments(mv, rs, e, eps, done):
                    i = e % 2
                    own.step(nc.gpsimd.tensor_scalar(rs[:, i, 0:1], mv[:, i, 1:2], eps, 1.0, ALU.add, ALU.mult))
                    own.wait()
                    own.step(nc.gpsimd.tensor_tensor(rs[:, i, 0:1], rs[:, i, 0:1], nhalf[:, :], ALU.pow))
                    own.wait()
                    nc.gpsimd.tensor_scalar(rs[:, i, 1:2], mv[:, i, 0:1], rs[:, i, 0:1], -1.0, ALU.mult, ALU.mult
                                            ).then_inc(done, 1)

                def bias(e):
                    pool.wait_ge(x_in[e % RX], 16 * (e // RX + 1))
                    nc.gpsimd.tensor_tensor(xt[:, e % RX, :], xt[:, e % RX, :], bias_b[:, :], ALU.add).then_inc(x_biased, 1)

                pool.wait_ge(ln_ready, 2)
                bias(0)
                for e in range(NE + 2):
                    if e < NE:
                        pool.wait_ge(mv1_ready, e + 1)
                        moments(mv1, rs1, e, 1e-6, rs1_ready)
                    if e >= 2:
                        pool.wait_ge(mv2_ready, e - 1)
                        moments(mv2, rs2, e - 2, 1e-5, rs2_ready)
                    if e < NE:
                        pool.wait_ge(z_ready, e + 1)
                        nc.gpsimd.tensor_tensor(z[:, e % 2, :], z[:, e % 2, :], scale_b[:, :], ALU.mult).then_inc(z_scaled, 1)
                    if e + 1 < NE:
                        bias(e + 1)

            @block.scalar
            def _(act):
                def split(e):
                    act.wait_ge(a_in[e % RA], 16 * (e // RA + 1))
                    if e >= RA:
                        act.wait_ge(out_ready, e - RA + 1)
                    nc.scalar.activation(ah[:, e % RA], aland[:, e % RA], ACT.Copy).then_inc(a_hi, 1)

                for kt in range(KI):
                    act.wait_ge(w_in[2 * kt // KI], 16)
                    nc.scalar.activation(wh[:, kt, :], wland[:, kt, :], ACT.Copy).then_inc(w_hi, 1)
                    if kt == KI // 2 - 1:
                        split(0)
                split(1)
                for e in range(NE + 3):
                    if e + 2 < NE:
                        split(e + 2)
                    if e < NE:
                        act.wait_ge(rs1_ready, e + 1)
                        if e >= 2:
                            act.wait_ge(x_new, e - 1)
                        nc.scalar.activation(z[:, e % 2, :], psum[0:TT, e % 4, :], ACT.Identity,
                                             bias=rs1[:, e % 2, 1:2], scale=rs1[:, e % 2, 0:1]).then_inc(z_ready, 1)
                    if e >= 3:
                        k = e - 3
                        act.wait_ge(tr_ready, k + 1)
                        nc.scalar.activation(y_all[:, :, TT * k:TT * (k + 1)],
                                             psum[:, 4 + k % 2, 0:KD * TT].rearrange("p (k t) -> p k t", k=KD),
                                             ACT.Copy).then_inc(tr_read, 1)
                    if 2 <= e <= NE + 1:
                        k = e - 2
                        act.wait_ge(rs2_ready, k + 1)
                        if k >= 2:
                            act.wait_ge(max_done, k - 1)
                            act.wait_ge(tr_ready, k - 1)
                        nc.scalar.activation(y[:, k % 2, :], xt[:, k % RX, :], ACT.Identity,
                                             bias=rs2[:, k % 2, 1:2], scale=rs2[:, k % 2, 0:1]).then_inc(y_ready, 1)

            @block.vector
            def _(dve):
                v = nc.vector
                own = Chain(dve, dve_own)

                def split(e):
                    dve.wait_ge(a_hi, e + 1)
                    v.tensor_tensor(al[:, e % RA], aland[:, e % RA], f(ah[:, e % RA]), ALU.subtract).then_inc(a_lo, 1)

                own.step(v.memset(ymax[:, :], 0.0))
                own.wait()
                for kt in range(KI):
                    dve.wait_ge(w_hi, kt + 1)
                    v.tensor_tensor(wl[:, kt, :], wland[:, kt, :], f(wh[:, kt, :]), ALU.subtract).then_inc(w_lo, 1)
                    if kt == KI // 2 - 1:
                        split(0)
                split(1)
                dve.wait_ge(const_in, 32)
                for tile in (scale_b, bias_b):
                    v.tensor_scalar(tile[:, :], tile[:, :], tg[0:TT, 1:2], None, ALU.mult).then_inc(ln_ready, 1)
                for e in range(NE + 3):
                    if e < NE:
                        dve.wait_ge(out_ready, e + 1)
                        own.step(v.bn_stats(st1[:, e % 2, :], psum[0:TT, e % 4, :]))
                        own.wait()
                        if e >= 2:
                            dve.wait_ge(rs1_ready, e - 1)
                        v.bn_aggr(mv1[:, e % 2, :], st1[:, e % 2, :]).then_inc(mv1_ready, 1)
                        if e + 2 < NE:
                            split(e + 2)
                    if e >= 3:
                        k = e - 3
                        dve.wait_ge(y_ready, k + 1)
                        v.tensor_reduce(ymax[0:TT, k:k + 1], y[:, k % 2, :], AX.X, ALU.max, apply_absolute_value=True
                                        ).then_inc(max_done, 1)
                    if 1 <= e <= NE:
                        k = e - 1
                        x = xt[:, k % RX, :]
                        dve.wait_ge(z_scaled, k + 1)
                        dve.wait_ge(x_biased, k + 1)
                        v.tensor_tensor(x, x, z[:, k % 2, :], ALU.add).then_inc(x_new, 1)
                        dve.wait_ge(x_new, k + 1)
                        own.step(v.bn_stats(st2[:, k % 2, :], x))
                        own.wait()
                        v.bn_aggr(mv2[:, k % 2, :], st2[:, k % 2, :]).then_inc(mv2_ready, 1)

            @block.tensor
            def _(pe):
                for e in range(NE + 3):
                    if e < NE:
                        pe.wait_ge(a_lo, e + 1)
                        if e >= 4:
                            pe.wait_ge(z_ready, e - 3)
                        for kt in range(KI):
                            if e == 0:
                                pe.wait_ge(w_lo, kt + 1)
                            ins = three(nc, psum[0:TT, e % 4, :], ah[:, e % RA, kt, :], al[:, e % RA, kt, :],
                                        wh[:, kt, :], wl[:, kt, :], kt == 0, kt == KI - 1)
                        ins.then_inc(out_ready, 1)
                    if e >= 3:
                        k = e - 3
                        pe.wait_ge(y_ready, k + 1)
                        if k >= 2:
                            pe.wait_ge(tr_read, k - 1)
                        for kt in range(KD):
                            ins = nc.tensor.transpose(psum[:, 4 + k % 2, TT * kt:TT * (kt + 1)],
                                                      y[:, k % 2, P * kt:P * (kt + 1)], ident[0:TT, 0:TT])
                        ins.then_inc(tr_ready, 1)


def overall_scale(nc, m, name, maxima, scale, inverse, factor=None):
    top, all_top, steps, reduced = m.sb(f"{name}_top", [P, 1]), m.sb(f"{name}_all", [P, 1]), m.sem(f"{name}_steps"), m.sem(f"{name}_red")

    def on_pool(pool):
        pool.wait_ge(steps, 1)
        nc.gpsimd.partition_all_reduce(all_top[:, :], top[:, :], P, RMAX).then_inc(reduced, 1)

    def on_vector(dve):
        v = nc.vector
        v.tensor_reduce(top[:, :], maxima, AX.X, ALU.max).then_inc(steps, 1)
        dve.wait_ge(reduced, 1)
        n = 1
        if factor is not None:
            v.tensor_tensor(all_top[:, :], all_top[:, :], factor, ALU.mult).then_inc(steps, 1)
            n += 1
            dve.wait_ge(steps, n)
        v.tensor_scalar(scale, all_top[:, :], float(np.float32(1.0) / np.float32(QMAX)), 1e-12, ALU.mult, ALU.max
                        ).then_inc(steps, 1)
        dve.wait_ge(steps, n + 1)
        v.reciprocal(inverse, scale).then_inc(steps, 1)
        dve.wait_ge(steps, n + 2)
        if factor is not None:
            v.tensor_tensor(inverse, inverse, factor, ALU.mult).then_inc(steps, 1)
            dve.wait_ge(steps, n + 3)

    return on_pool, on_vector, steps


def phase_project(nc, psum, g_, y_all, d, ymax, umax, g2max):
    with Mem(nc, "p6a") as m:
        land = m.sb("land", [P, 2, KD, P])
        wh, wl = m.sb("wh", [P, 2, KD, P], F32R), m.sb("wl", [P, 2, KD, P], F32R)
        yh, yl = m.sb("yh", [P, KD, T], F32R), m.sb("yl", [P, KD, T], F32R)
        sig = m.sb("sig", [P, 2, T])
        sy, iy, sg, ig = (m.sb(n, [P, 1]) for n in ("sy", "iy", "sg", "ig"))
        gmax = m.sb("gmax", [P, NI1])
        s = m.sem
        w_in, w_hi, w_lo = [s("w_in0"), s("w_in1")], s("w_hi"), s("w_lo")
        y_scaled, y_hi, y_lo = s("y_scaled"), s("y_hi"), s("y_lo")
        o_ready, o_read, g_max, u_max = s("o_ready"), s("o_read"), s("g_max"), s("u_max")
        u_out = [s(f"u_out{i}") for i in range(RU)]
        act_held, dve_held = s("act_held"), s("dve_held")
        g_scaled, g_whole, sig_ready, sig_rounded, sig_whole, silu_done, g2_max = (
            s("g_scaled"), s("g_whole"), s("sig_ready"), s("sig_rounded"), s("sig_whole"), s("silu_done"), s("g2_max"))
        y_pool, y_vector, y_steps = overall_scale(nc, m, "y", ymax[:, :], sy[:, :], iy[:, :])
        g_pool, g_vector, g_steps = overall_scale(nc, m, "g", gmax[:, :], sg[:, :], ig[:, :])
        NE = 2 * NI1
        RB = 2 * NC
        SIG = 1.5 * 2.0 ** 7

        def up_tile(r):
            return y_all[:, r % RU, :]

        with nc.Block() as block:
            @block.sync
            def _(sp):
                for e in range(NE):
                    if e >= 2:
                        sp.wait_ge(w_lo, e - 1 + 2)
                    it, k0 = e % NI1, KD * (e // NI1)
                    sp.dma_start(land[:, e % 2],
                                 d["wdq"][k0:k0 + KD, :, P * it:P * (it + 1)].rearrange("k p n -> p k n")
                                 ).then_inc(w_in[e % 2], 16)

            @block.gpsimd
            def _(pool):
                y_pool(pool)
                g_pool(pool)
                for t in range(NI1):
                    pool.wait_ge(sig_rounded, t + 1)
                    nc.gpsimd.tensor_scalar(sig[:, t % 2, :], sig[:, t % 2, :], -SIG, 1.0, ALU.add, ALU.mult
                                            ).then_inc(sig_whole, 1)

            @block.scalar
            def _(act):
                def hi(e, par, turn):
                    act.wait_ge(w_in[par], turn * 16 + 16)
                    act.wait_ge(o_ready, e * NC + NC)
                    nc.scalar.activation(wh[:, par], land[:, par], ACT.Copy).then_inc(w_hi, 1)

                def read(e, par, out):
                    for c in range(NC):
                        act.wait_ge(o_ready, e * NC + (c + 1 + RB))
                        hold(act, act_held)
                        nc.scalar.activation(out(c), psum[:, NC * par + c, 0:CH], ACT.Identity, scale=sy[:, :]
                                             ).then_inc(o_read, 1)

                act.sem_inc(o_read, RB)
                act.sem_inc(o_ready, RB)
                for i in range(RU):
                    act.sem_inc(u_out[i], 16)
                hi(0, 0, 0)
                act.wait_ge(y_steps, 3)
                for c in range(NC):
                    chunk = slice(CH * c, CH * (c + 1))
                    nc.scalar.activation(y_all[:, :, chunk], y_all[:, :, chunk], ACT.Copy, bias=MAGIC, scale=iy[:, :]
                                         ).then_inc(y_scaled, 1)
                    act.wait_ge(y_scaled, c + 1)
                    nc.scalar.activation(yh[:, :, chunk], y_all[:, :, chunk], ACT.Copy, bias=-MAGIC).then_inc(y_hi, 1)
                with act.Fori(0, NI1 // 2) as i:
                    for par in (0, 1):
                        it = i * 2 + par
                        hi(it + 1, 1 - par, i + par)
                        read(it, par, lambda c: g_[:, bass.ds(it, 1), CH * c:CH * (c + 1)].rearrange("p a t -> p (a t)"))
                act.wait_ge(g_steps, 3)

                def scale_gate(it):
                    gate = g_[:, bass.ds(it, 1), :].rearrange("p a t -> p (a t)")
                    nc.scalar.activation(gate, gate, ACT.Copy, bias=MAGIC, scale=ig[:, :]).then_inc(g_scaled, 1)

                def up_turn(g, r, store, more):
                    it, par = g * RU + r, r % 2
                    e = it + NI1
                    if more:
                        hi(e + 1, 1 - par, g * (RU // 2) + (NI1 + r + 1) // 2)
                    act.wait_ge(g_whole, it + 1)
                    act.wait_ge(silu_done, it + 1)
                    hold(act, act_held)
                    nc.scalar.activation(sig[:, par, :], g_[:, bass.ds(it, 1), :].rearrange("p a t -> p (a t)"),
                                         ACT.Sigmoid).then_inc(sig_ready, 1)
                    act.wait_ge(sig_ready, it + 1)
                    nc.scalar.activation(sig[:, par, :], sig[:, par, :], ACT.Copy, bias=SIG).then_inc(sig_rounded, 1)
                    if more:
                        scale_gate(it + 1)
                    act.wait_ge(u_out[r], g * 16 + 16)
                    act.wait_ge(u_max, it + 1)
                    read(e, par, lambda c: up_tile(r)[:, CH * c:CH * (c + 1)])
                    if store:
                        act.wait_ge(o_read, e * NC + (NC + RB))
                        act.dma_start(d["upT"][bass.ds(it * P, P), :], up_tile(r)).then_inc(u_out[r], 16)

                scale_gate(0)
                act.wait_ge(y_lo, NC)
                with act.Fori(0, NI1 // RU - 1) as g:
                    for r in range(RU):
                        up_turn(g, r, True, True)
                for r in range(RU):
                    up_turn(NI1 // RU - 1, r, False, r < RU - 1)
                for i in range(RU):
                    act.wait_ge(u_out[i], 16 * (NI1 // RU))

            @block.vector
            def _(dve):
                v = nc.vector

                def lo(e, par):
                    dve.wait_ge(w_hi, e + 1)
                    v.tensor_tensor(wl[:, par], land[:, par], f(wh[:, par]), ALU.subtract).then_inc(w_lo, 1)

                def gate_tile(it):
                    return g_[:, bass.ds(it, 1), :].rearrange("p a t -> p (a t)")

                def silu(it, par):
                    g = gate_tile(it)
                    dve.wait_ge(sig_whole, it + 1)
                    v.scalar_tensor_tensor(out=g, in0=sig[:, par, :], scalar=1.0 - 2.0 ** -16, in1=g,
                                           op0=ALU.min, op1=ALU.mult).then_inc(silu_done, 1)
                    dve.wait_ge(silu_done, it + (1 + 2))
                    hold(dve, dve_held)
                    v.tensor_reduce(g2max[:, bass.ds(it, 1)], g, AX.X, ALU.max, apply_absolute_value=True
                                    ).then_inc(g2_max, 1)

                def quantise_gate(it):
                    dve.wait_ge(g_scaled, it + 1)
                    v.tensor_scalar(gate_tile(it), gate_tile(it), -MAGIC, sg[:, :], ALU.add, ALU.mult).then_inc(g_whole, 1)

                dve.sem_inc(w_lo, 2)
                dve.sem_inc(u_max, RU)
                dve.sem_inc(silu_done, 2)
                y_vector(dve)
                lo(0, 0)
                for c in range(NC):
                    chunk = slice(CH * c, CH * (c + 1))
                    dve.wait_ge(y_hi, c + 1)
                    v.scalar_tensor_tensor(out=yl[:, :, chunk], in0=y_all[:, :, chunk], scalar=-MAGIC,
                                           in1=f(yh[:, :, chunk]), op0=ALU.add, op1=ALU.subtract).then_inc(y_lo, 1)
                with dve.Fori(0, NI1 // 2) as i:
                    for par in (0, 1):
                        it = i * 2 + par
                        lo(it + 1, 1 - par)
                        dve.wait_ge(o_read, it * NC + (NC + RB))
                        hold(dve, dve_held)
                        v.tensor_reduce(gmax[:, bass.ds(it, 1)], gate_tile(it), AX.X, ALU.max,
                                        apply_absolute_value=True).then_inc(g_max, 1)
                dve.wait_ge(g_max, NI1)
                g_vector(dve)

                def up_turn(g, r, more=True):
                    it, par = g * RU + r, r % 2
                    if more:
                        lo(it + (NI1 + 1), 1 - par)
                        quantise_gate(it + 1)
                    silu(it, par)
                    dve.wait_ge(o_read, it * NC + (NI1 * NC + NC + RB))
                    hold(dve, dve_held)
                    v.tensor_reduce(umax[:, bass.ds(it, 1)], up_tile(r), AX.X, ALU.max,
                                    apply_absolute_value=True).then_inc(u_max, 1)

                quantise_gate(0)
                with dve.Fori(0, NI1 // RU - 1) as g:
                    for r in range(RU):
                        up_turn(g, r)
                for r in range(RU):
                    up_turn(NI1 // RU - 1, r, r < RU - 1)

            @block.tensor
            def _(pe):
                with pe.Fori(0, NE // 2) as i:
                    for par in (0, 1):
                        e = i * 2 + par
                        pe.wait_ge(w_lo, e + 1 + 2)
                        for c in range(NC):
                            pe.wait_ge(y_lo, c + 1)
                            pe.wait_ge(o_read, e * NC + c + 1)
                            for kt in range(KD):
                                chunk = slice(CH * c, CH * (c + 1))
                                ins = three(nc, psum[:, NC * par + c, 0:CH], wh[:, par, kt, :], wl[:, par, kt, :],
                                            yh[:, kt, chunk], yl[:, kt, chunk], kt == 0, kt == KD - 1)
                            ins.then_inc(o_ready, 1)


def phase_mix_down(nc, psum, g_, u, tg, d, umax, g2max):
    with Mem(nc, "p6b") as m:
        wh, (wraw, wl) = m.sb("wh", [P, NI1, D], F32R), m.landing("wl", [P, NI1, D])
        ow = m.sb("ow", [P, NI1, TT])
        ohi, olo = m.sb("ohi", [P, 2, NI1, TT], F32R), m.sb("olo", [P, 2, NI1, TT], F32R)
        xt = m.sb("xt", [TT, NT, D])
        omax = m.sb("omax", [P, NI1])
        su, iu, s2, i2, so, io, su2, tgo = (m.sb(n, [P, 1]) for n in ("su", "iu", "s2", "i2", "so", "io", "su2", "tgo"))
        s = m.sem
        u_in = [s(f"u_in{i}") for i in range(RU)]
        scales, g_scaled, u_scaled, u_whole, mixed, o_max, tgo_ready = (
            s("scales"), s("g_scaled"), s("u_scaled"), s("u_whole"), s("mixed"), s("o_max"), s("tgo_ready"))
        x_in, x_out = [s(f"x_in{i}") for i in range(NT)], [s(f"x_out{i}") for i in range(NT)]
        o_scaled, o_hi, o_lo, out_ready, x_new = s("o_scaled"), s("o_hi"), s("o_lo"), s("out_ready"), s("x_new")
        act_held = s("act_held")
        u_pool, u_vector, _ = overall_scale(nc, m, "um", umax[:, :], su[:, :], iu[:, :])
        g_pool, g_vector, _ = overall_scale(nc, m, "gm", g2max[:, :], s2[:, :], i2[:, :])
        o_pool, o_vector, o_steps = overall_scale(nc, m, "om", omax[:, :], so[:, :], io[:, :], su2[:, :])
        WS = NI1 // 3
        w_in, w_hi, w_lo = [s(f"w_in{j}") for j in range(WS)], s("w_hi"), s("w_lo")

        def part(w, j):
            return w[:, 3 * j:3 * j + 3, :].rearrange("p k n -> p (k n)")

        order = list(range(NI1 - RU, NI1)) + list(range(NI1 - RU))

        with nc.Block() as block:
            @block.sync
            def _(sp):
                def rows(name, c, n):
                    return d[name][CH * c + TT * n:CH * c + TT * (n + 1), :]

                for j in range(WS):
                    sp.dma_start(part(wraw, j), d["wdq"][2 * KD + j]).then_inc(w_in[j], 16)
                for n in range(NT):
                    sp.dma_start(xt[:, n, :], rows("x3", 0, n)).then_inc(x_in[n], 16)
                for j in range(RU, NI1):
                    sp.wait_ge(mixed, j - RU + 1)
                    sp.dma_start(u[:, j % RU, :], d["upT"][P * order[j]:P * (order[j] + 1), :]).then_inc(u_in[j % RU], 16)
                for c in range(NC):
                    for n in range(NT):
                        sp.wait_ge(x_new, NT * c + n + 1 + NT)
                        sp.dma_start(rows("out", c, n), xt[:, n, :]).then_inc(x_out[n], 16)
                        sp.wait_ge(x_out[n], 16 * (c + 1))
                        if c + 1 < NC:
                            sp.dma_start(xt[:, n, :], rows("x3", c + 1, n)).then_inc(x_in[n], 16)

            @block.gpsimd
            def _(pool):
                g_pool(pool)
                u_pool(pool)
                for j in range(NI1):
                    ut = u[:, j % RU, :]
                    pool.wait_ge(u_scaled, j + 1)
                    nc.gpsimd.tensor_scalar(ut, ut, -MAGIC, 1.0, ALU.add, ALU.mult).then_inc(u_whole, 1)
                    if 4 <= j < 4 + WS:
                        pool.wait_ge(w_hi, j - 3)
                        nc.gpsimd.tensor_tensor(part(wl, j - 4), part(wraw, j - 4), f(part(wh, j - 4)), ALU.subtract
                                                ).then_inc(w_lo, 1)
                o_pool(pool)

            @block.scalar
            def _(act):
                for j, t in enumerate(order):
                    ut = u[:, j % RU, :]
                    if j == 0:
                        act.wait_ge(scales, 1)
                    if j >= RU:
                        act.wait_ge(u_in[j % RU], 16 * (j // RU))
                    nc.scalar.activation(ut, ut, ACT.Copy, bias=MAGIC, scale=iu[:, :]).then_inc(u_scaled, 1)
                    nc.scalar.activation(g_[:, t, :], g_[:, t, :], ACT.Copy, bias=MAGIC, scale=i2[:, :]).then_inc(g_scaled, 1)
                    if 3 <= j < 3 + WS:
                        act.wait_ge(w_in[j - 3], 16)
                        nc.scalar.activation(part(wh, j - 3), part(wraw, j - 3), ACT.Copy).then_inc(w_hi, 1)
                act.sem_inc(out_ready, 2)
                act.sem_inc(o_lo, 1)
                act.wait_ge(o_steps, 5)
                with act.Fori(0, NC) as c:
                    for n in range(NT):
                        act.wait_ge(o_lo, c * NT + n + 1)
                        hold(act, act_held)
                        nc.scalar.activation(ow[:, :, :], g_[:, :, bass.ds(c * CH + n * TT, TT)], ACT.Copy,
                                             bias=MAGIC, scale=io[:, :]).then_inc(o_scaled, 1)
                        act.wait_ge(o_scaled, c * NT + n + 1)
                        act.wait_ge(out_ready, c * NT + n + 1)
                        nc.scalar.activation(ohi[:, n % 2], ow[:, :, :], ACT.Copy, bias=-MAGIC).then_inc(o_hi, 1)

            @block.vector
            def _(dve):
                v = nc.vector
                g_vector(dve)
                u_vector(dve)
                v.tensor_tensor(su2[:, :], su[:, :], s2[:, :], ALU.mult).then_inc(scales, 1)
                for j, t in enumerate(order):
                    dve.wait_ge(g_scaled, j + 1)
                    dve.wait_ge(u_whole, j + 1)
                    v.scalar_tensor_tensor(out=g_[:, t, :], in0=g_[:, t, :], scalar=-MAGIC, in1=u[:, j % RU, :],
                                           op0=ALU.add, op1=ALU.mult).then_inc(mixed, 1)
                    dve.wait_ge(mixed, j + 1)
                    v.tensor_reduce(omax[:, t:t + 1], g_[:, t, :], AX.X, ALU.max, apply_absolute_value=True
                                    ).then_inc(o_max, 1)
                dve.wait_ge(o_max, NI1)
                dve.wait_ge(scales, 1)
                o_vector(dve)
                v.tensor_tensor(tgo[:, :], tg[:, 3:4], so[:, :], ALU.mult).then_inc(tgo_ready, 1)
                dve.wait_ge(tgo_ready, 1)
                dve.sem_inc(x_new, NT)

                def lo(e, par):
                    dve.wait_ge(o_hi, e + 1)
                    v.scalar_tensor_tensor(out=olo[:, par], in0=ow[:, :, :], scalar=-MAGIC, in1=f(ohi[:, par]),
                                           op0=ALU.add, op1=ALU.subtract).then_inc(o_lo, 1)

                def close(e, n, turn):
                    dve.wait_ge(out_ready, e + (1 + 2))
                    dve.wait_ge(x_in[n], turn * 16 + 16)
                    v.scalar_tensor_tensor(out=xt[:, n, :], in0=psum[0:TT, n, :], scalar=tgo[0:TT, :], in1=xt[:, n, :],
                                           op0=ALU.mult, op1=ALU.add).then_inc(x_new, 1)

                lo(0, 0)
                with dve.Fori(0, NC - 1) as c:
                    for n in range(NT):
                        lo(c * NT + (n + 1), (n + 1) % 2)
                        close(c * NT + n, n, c)
                for n in range(NT):
                    e = (NC - 1) * NT + n
                    if n < NT - 1:
                        lo(e + 1, (n + 1) % 2)
                    close(e, n, NC - 1)

            @block.tensor
            def _(pe):
                pe.wait_ge(w_lo, WS)
                with pe.Fori(0, NC) as c:
                    for n in range(NT):
                        pe.wait_ge(o_lo, c * NT + (n + 1 + 1))
                        pe.wait_ge(x_new, c * NT + n + 1)
                        for kt in range(NI1):
                            ins = three(nc, psum[0:TT, n, :], ohi[:, n % 2, kt, :], olo[:, n % 2, kt, :],
                                        wh[:, kt, :], wl[:, kt, :], kt == 0, kt == NI1 - 1)
                        ins.then_inc(out_ready, 1)


def phase_quantised_ffn(nc, psum, tg, ymax, y_all, d):
    with Mem(nc, "p6") as m:
        g_ = m.sb("gate", [P, NI1, T])
        umax, g2max = m.sb("umax", [P, NI1]), m.sb("g2max", [P, NI1])
        phase_project(nc, psum, g_, y_all, d, ymax, umax, g2max)
        phase_mix_down(nc, psum, g_, y_all, tg, d, umax, g2max)


def build(nc, d):
    with Mem(nc, "all") as m:
        psum = m.stack.enter_context(nc.psum_tensor("psum", [P, 8, 512], F32))
        ident = m.sb("ident", [P, P])
        tg = m.sb("tg", [P, 4])
        phase_depool(nc, psum, ident, tg, d)
        phase_relu_ffn(nc, psum, ident, tg, d)
        with Mem(nc, "kv") as m_kv:
            kv = KvLanding(m_kv, d)
            phase_queries(nc, psum, ident, tg, kv, d)
            phase_attention(nc, psum, ident, kv, d)
        ymax, y_all = m.sb("ymax", [P, NC * NT]), m.sb("y_all", [P, KD, T])
        phase_attention_out(nc, psum, ident, tg, ymax, y_all, d)
        phase_quantised_ffn(nc, psum, tg, ymax, y_all, d)


SCRATCH = {"x1": [T, D], "x2": [T, D], "qT": [INNER, T], "wdq": [3 * KD, P, FF1], "aT": [INNER, T],
           "x3": [T, D], "upT": [FF1, T]}


def kernel(**a):
    import numpy as np
    import concourse.bacc as bacc
    from concourse import mybir as mb
    from concourse.bass_utils import run_bass_kernel_spmd as run

    def cols(v, n):
        return v.reshape(n, 128).T

    def blocks(w):
        o, i = w.shape
        return w.reshape(o // QB, QB, i // P, 4, QB).transpose(2, 3, 1, 0, 4).reshape(i // P, P, o)

    down = blocks(a["L1_ffn_w_down"])
    down = down.reshape(KD, 3, P, D).transpose(0, 2, 1, 3).reshape(KD, P, 3 * D)
    arrays = {
        "x": a["x"].reshape(T, D), "ctx": a["ctx_2048"], "ctx_t": a["ctx_2048"].transpose(0, 2, 1),
        "lens": a["mask_BxS2_if0"], "gates": np.concatenate([a["g_xattn"], a["g_ffn"]]),
        "w_in_t": a["L0_xattn_W_in"].T, "b_in": a["L0_xattn_b_in"],
        "g_res_cols": cols(a["L0_xattn_g_res"], KD), "g_init": a["L0_xattn_g_init"],
        "w1": a["L0_ffn_W1"], "b1_cols": cols(a["L0_ffn_b1"], NI0), "w2": a["L0_ffn_W2"], "b2": a["L0_ffn_b2"],
        "w_q": np.concatenate([blocks(a["L1_ffn_w_gate"]), blocks(a["L1_ffn_w_up"]), down]),
        "wq": a["L1_xattn_Wq"], "wkv": a["L1_xattn_Wkv"], "null_kv": a["L1_xattn_null_kv"], "wout": a["L1_xattn_Wout"],
        "ln_scale": a["L1_xattn_ln_scale"], "ln_bias": a["L1_xattn_ln_bias"],
    }
    nc = bacc.Bacc("TRN2", target_bir_lowering=False, num_devices=1)
    arrays = {k: np.ascontiguousarray(v) for k, v in arrays.items()}
    d = {k: nc.dram_tensor(f"in_{k}", v.shape, mb.dt.from_np(v.dtype), kind="ExternalInput").ap() for k, v in arrays.items()}
    for k, shape in SCRATCH.items():
        d[k] = nc.dram_tensor(f"scratch_{k}", shape, mb.dt.float32, kind="Internal").ap()
    d["out"] = nc.dram_tensor("out", [T, D], mb.dt.float32, kind="ExternalOutput").ap()
    build(nc, d)
    r = run(nc, [{f"in_{k}": v for k, v in arrays.items()}], core_ids=[0])
    return r.results[0]["out"].reshape(B, S, D)
```
